# Optimizing a Trainium2 kernel written in Bass

```python
import numpy as np
import jax
import jax.numpy as jnp

def _softmax(x, axis=-1):
    return jax.nn.softmax(x, axis=axis)

def _gelu(x):
    return jax.nn.gelu(x, approximate=True)

def _silu(x):
    return jax.nn.silu(x)

def _sigmoid(x):
    return jax.nn.sigmoid(x)

def _layernorm(x, axis=-1, eps=1e-05):
    m = jnp.mean(x, axis=axis, keepdims=True)
    v = jnp.var(x, axis=axis, keepdims=True)
    return (x - m) / jnp.sqrt(v + eps)

def _scatter_add(tgt, idx, src, axis=0):
    return tgt.at[idx].add(src)

def _segment_sum(src, seg, n):
    return jax.ops.segment_sum(src, seg, n)
kernel_name = 'mk_gnn_preln_d2_gnn_r32_7d8713'

def setup_inputs(seed: int=0):
    np.random.seed(seed)
    _w = jnp.asarray

    def _rec_inputs():
        import jax
        import jax.numpy as jnp
        _gk = jax.random.key(seed)
        x = -0.0009044 + 1 * jax.random.normal(jax.random.fold_in(_gk, 1), (3125, 32), jnp.float32)
        _s = jax.random.randint(jax.random.fold_in(_gk, 2), (25000,), 0, 3125, jnp.int32)
        _d = jax.random.randint(jax.random.fold_in(_gk, 3), (25000,), 0, 3125, jnp.int32)
        _loop = jnp.arange(3125, dtype=jnp.int32)
        src = jnp.concatenate([_s, _d, _loop])
        dst = jnp.concatenate([_d, _s, _loop])
        _o = jnp.argsort(dst, stable=True)
        src = src[_o]
        dst = dst[_o]
        edge_attr_10 = jax.random.uniform(jax.random.fold_in(_gk, 12), (53125, 10), jnp.float32, 0.0, 1)
        edge_attr_3 = 0.00109039 + 0.999626 * jax.random.normal(jax.random.fold_in(_gk, 13), (53125, 3), jnp.float32)
        edge_weight = jax.random.uniform(jax.random.fold_in(_gk, 15), (53125,), jnp.float32, 0.0, 0.999997)
        return (x, src, dst, edge_attr_10, edge_attr_3, edge_weight)
    x, src, dst, edge_attr_10, edge_attr_3, edge_weight = _rec_inputs()

    def _L0_gnn_setup():
        import jax, jax.numpy as jnp
        import numpy as np
        MUL = 16
        MOUT = 8
        TANH_GAIN = 1.593
        INV_SQRT3 = 0.5773502691896258
        PW_S = 0.17677669529663687
        PW_V = 0.25

        def _w3j_121():
            s2, s6 = (2 ** 0.5, 6 ** 0.5)
            M = np.zeros((5, 3, 3))
            M[0, 0, 1] = M[0, 1, 0] = 1 / s2
            M[1, 1, 2] = M[1, 2, 1] = 1 / s2
            M[2] = np.diag([-1.0, -1.0, 2.0]) / s6
            M[3, 0, 2] = M[3, 2, 0] = 1 / s2
            M[4] = np.diag([1.0, -1.0, 0.0]) / s2
            return jnp.asarray(np.transpose(M, (1, 0, 2)) / 5 ** 0.5, jnp.float32)
        W3J121 = _w3j_121()

        def _sph(edge_vec):
            n = edge_vec / jnp.linalg.norm(edge_vec, axis=1, keepdims=True)
            x, y, z = (n[:, 0], n[:, 1], n[:, 2])
            y1 = 3.0 ** 0.5 * n
            s15 = 15.0 ** 0.5
            y2 = jnp.stack([s15 * x * y, s15 * y * z, 5.0 ** 0.5 / 2 * (3 * z * z - 1), s15 * x * z, s15 / 2 * (x * x - y * y)], axis=1)
            return (y1, y2)

        def _forward(x, edge_src, edge_dst, edge_vec, emb, norm, W1, W2):
            N, E = (x.shape[0], edge_src.shape[0])
            xs = jnp.concatenate([x[edge_src, :8], x[edge_dst, :8]], axis=1)
            xv = jnp.concatenate([x[edge_src, 8:].reshape(E, 8, 3), x[edge_dst, 8:].reshape(E, 8, 3)], axis=1)
            y1, y2 = _sph(edge_vec)
            h = 2.0 ** 0.5 * jax.nn.relu(emb @ W1 / 10.0 ** 0.5)
            w = (h @ W2 / 16.0 ** 0.5).reshape(E, 7, MUL, MOUT)
            wa_s, wb_s, wa_g, wb_g, wc, wd, we = [w[:, i] for i in range(7)]
            s_out = PW_S * (jnp.einsum('eu,euw->ew', xs, wa_s) + INV_SQRT3 * jnp.einsum('eui,ei,euw->ew', xv, y1, wb_s))
            g_out = PW_S * (jnp.einsum('eu,euw->ew', xs, wa_g) + INV_SQRT3 * jnp.einsum('eui,ei,euw->ew', xv, y1, wb_g))
            v_out = PW_V * (INV_SQRT3 * jnp.einsum('eu,ek,euw->ewk', xs, y1, wc) + INV_SQRT3 * jnp.einsum('eui,euw->ewi', xv, wd) + jnp.einsum('eui,ea,iak,euw->ewk', xv, y2, W3J121, we))
            s_act = TANH_GAIN * jnp.tanh(s_out)
            gates = TANH_GAIN * jnp.tanh(g_out)
            edge_ftr = jnp.concatenate([s_act, (gates[:, :, None] * v_out).reshape(E, 24)], axis=1) * norm[:, None]
            return jax.ops.segment_sum(edge_ftr, edge_dst, num_segments=N)
        key = jax.random.key(seed)
        ks = jax.random.split(key, 8)
        N, E = (50000, 9375)
        return {'x': jax.random.normal(ks[0], (N, 32), jnp.float32), 'edge_src': jax.random.randint(ks[1], (E,), 0, N), 'edge_dst': jax.random.randint(ks[2], (E,), 0, N), 'edge_vec': jax.random.normal(ks[3], (E, 3), jnp.float32), 'emb': jax.random.uniform(ks[4], (E, 10), jnp.float32), 'norm': jax.random.uniform(ks[5], (E,), jnp.float32), 'W1': jax.random.normal(ks[6], (10, 16), jnp.float32), 'W2': jax.random.normal(ks[7], (16, 896), jnp.float32)}
    _L0_gnn_all = _L0_gnn_setup()
    _L0_gnn_in = {k: v for k, v in _L0_gnn_all.items() if k in ('W1', 'W2')}
    del _L0_gnn_all

    def _L1_gnn_setup():
        import jax, jax.numpy as jnp
        import numpy as np
        H, C = (8, 32)
        N, E = (3125, 50000)
        NEG_SLOPE = 0.2
        LN_EPS = 1e-05

        def layer_norm(x, g, b):
            mu = jnp.mean(x, axis=-1, keepdims=True)
            var = jnp.mean((x - mu) ** 2, axis=-1, keepdims=True)
            return (x - mu) * jax.lax.rsqrt(var + LN_EPS) * g + b

        def gat_conv(x, edge_index, W_gat, att_src, att_dst, bias_gat):
            n = x.shape[0]
            loops = jnp.arange(n, dtype=edge_index.dtype)
            ei = jnp.concatenate([edge_index, jnp.stack([loops, loops])], axis=1)
            src, dst = (ei[0], ei[1])
            xp = (x @ W_gat).reshape(n, H, C)
            a_src = jnp.einsum('nhc,hc->nh', xp, att_src)
            a_dst = jnp.einsum('nhc,hc->nh', xp, att_dst)
            alpha = jax.nn.leaky_relu(a_src[src] + a_dst[dst], NEG_SLOPE)
            m = jax.ops.segment_max(alpha, dst, num_segments=n)
            ea = jnp.exp(alpha - m[dst])
            denom = jax.ops.segment_sum(ea, dst, num_segments=n)
            attn = ea / (denom[dst] + 1e-16)
            msg = xp[src] * attn[..., None]
            out = jax.ops.segment_sum(msg, dst, num_segments=n)
            return out.mean(axis=1) + bias_gat
        key = jax.random.key(seed)
        ks = jax.random.split(key, 8)
        x = jax.random.normal(ks[0], (N, C), dtype=jnp.float32)
        edge_index = jax.random.randint(ks[1], (2, E), 0, N, dtype=jnp.int64)
        s = 1.0 / np.sqrt(C)
        W_gat = jax.random.normal(ks[2], (C, H * C), dtype=jnp.float32) * s
        att_src = jax.random.normal(ks[3], (H, C), dtype=jnp.float32) * s
        att_dst = jax.random.normal(ks[4], (H, C), dtype=jnp.float32) * s
        bias_gat = jnp.zeros((C,), jnp.float32)
        w1 = jax.random.normal(ks[5], (C, 128), dtype=jnp.float32) * s
        b1 = jnp.zeros((128,), jnp.float32)
        w2 = jax.random.normal(ks[6], (128, C), dtype=jnp.float32) / np.sqrt(128)
        b2 = jnp.zeros((C,), jnp.float32)
        g1 = jnp.ones((C,), jnp.float32)
        be1 = jnp.zeros((C,), jnp.float32)
        g2 = jnp.ones((C,), jnp.float32)
        be2 = jnp.zeros((C,), jnp.float32)
        return dict(x=x, edge_index=edge_index, W_gat=W_gat, att_src=att_src, att_dst=att_dst, bias_gat=bias_gat, w1=w1, b1=b1, w2=w2, b2=b2, g1=g1, be1=be1, g2=g2, be2=be2)
    _L1_gnn_all = _L1_gnn_setup()
    _L1_gnn_in = {k: v for k, v in _L1_gnn_all.items() if k in ('W_gat', 'att_src', 'att_dst', 'bias_gat', 'w1', 'b1', 'w2', 'b2', 'g1', 'be1', 'g2', 'be2')}
    del _L1_gnn_all
    return {'x': x, 'src': src, 'dst': dst, 'edge_attr_10': edge_attr_10, 'edge_attr_3': edge_attr_3, 'edge_weight': edge_weight, 'L0_gnn_W1': _L0_gnn_in['W1'], 'L0_gnn_W2': _L0_gnn_in['W2'], 'L1_gnn_W_gat': _L1_gnn_in['W_gat'], 'L1_gnn_att_src': _L1_gnn_in['att_src'], 'L1_gnn_att_dst': _L1_gnn_in['att_dst'], 'L1_gnn_bias_gat': _L1_gnn_in['bias_gat'], 'L1_gnn_w1': _L1_gnn_in['w1'], 'L1_gnn_b1': _L1_gnn_in['b1'], 'L1_gnn_w2': _L1_gnn_in['w2'], 'L1_gnn_b2': _L1_gnn_in['b2'], 'L1_gnn_g1': _L1_gnn_in['g1'], 'L1_gnn_be1': _L1_gnn_in['be1'], 'L1_gnn_g2': _L1_gnn_in['g2'], 'L1_gnn_be2': _L1_gnn_in['be2']}

def reference(x, src, dst, edge_attr_10, edge_attr_3, edge_weight, L0_gnn_W1, L0_gnn_W2, L1_gnn_W_gat, L1_gnn_att_src, L1_gnn_att_dst, L1_gnn_bias_gat, L1_gnn_w1, L1_gnn_b1, L1_gnn_w2, L1_gnn_b2, L1_gnn_g1, L1_gnn_be1, L1_gnn_g2, L1_gnn_be2):
    import jax
    import jax.numpy as jnp

    def _L0_gnn_ref(x, edge_src, edge_dst, edge_vec, emb, norm, W1, W2):
        import jax, jax.numpy as jnp
        import numpy as np
        MUL = 16
        MOUT = 8
        TANH_GAIN = 1.593
        INV_SQRT3 = 0.5773502691896258
        PW_S = 0.17677669529663687
        PW_V = 0.25

        def _w3j_121():
            s2, s6 = (2 ** 0.5, 6 ** 0.5)
            M = np.zeros((5, 3, 3))
            M[0, 0, 1] = M[0, 1, 0] = 1 / s2
            M[1, 1, 2] = M[1, 2, 1] = 1 / s2
            M[2] = np.diag([-1.0, -1.0, 2.0]) / s6
            M[3, 0, 2] = M[3, 2, 0] = 1 / s2
            M[4] = np.diag([1.0, -1.0, 0.0]) / s2
            return jnp.asarray(np.transpose(M, (1, 0, 2)) / 5 ** 0.5, jnp.float32)
        W3J121 = _w3j_121()

        def _sph(edge_vec):
            n = edge_vec / jnp.linalg.norm(edge_vec, axis=1, keepdims=True)
            x, y, z = (n[:, 0], n[:, 1], n[:, 2])
            y1 = 3.0 ** 0.5 * n
            s15 = 15.0 ** 0.5
            y2 = jnp.stack([s15 * x * y, s15 * y * z, 5.0 ** 0.5 / 2 * (3 * z * z - 1), s15 * x * z, s15 / 2 * (x * x - y * y)], axis=1)
            return (y1, y2)

        def _forward(x, edge_src, edge_dst, edge_vec, emb, norm, W1, W2):
            N, E = (x.shape[0], edge_src.shape[0])
            xs = jnp.concatenate([x[edge_src, :8], x[edge_dst, :8]], axis=1)
            xv = jnp.concatenate([x[edge_src, 8:].reshape(E, 8, 3), x[edge_dst, 8:].reshape(E, 8, 3)], axis=1)
            y1, y2 = _sph(edge_vec)
            h = 2.0 ** 0.5 * jax.nn.relu(emb @ W1 / 10.0 ** 0.5)
            w = (h @ W2 / 16.0 ** 0.5).reshape(E, 7, MUL, MOUT)
            wa_s, wb_s, wa_g, wb_g, wc, wd, we = [w[:, i] for i in range(7)]
            s_out = PW_S * (jnp.einsum('eu,euw->ew', xs, wa_s) + INV_SQRT3 * jnp.einsum('eui,ei,euw->ew', xv, y1, wb_s))
            g_out = PW_S * (jnp.einsum('eu,euw->ew', xs, wa_g) + INV_SQRT3 * jnp.einsum('eui,ei,euw->ew', xv, y1, wb_g))
            v_out = PW_V * (INV_SQRT3 * jnp.einsum('eu,ek,euw->ewk', xs, y1, wc) + INV_SQRT3 * jnp.einsum('eui,euw->ewi', xv, wd) + jnp.einsum('eui,ea,iak,euw->ewk', xv, y2, W3J121, we))
            s_act = TANH_GAIN * jnp.tanh(s_out)
            gates = TANH_GAIN * jnp.tanh(g_out)
            edge_ftr = jnp.concatenate([s_act, (gates[:, :, None] * v_out).reshape(E, 24)], axis=1) * norm[:, None]
            return jax.ops.segment_sum(edge_ftr, edge_dst, num_segments=N)
        return _forward(x, edge_src, edge_dst, edge_vec, emb, norm, W1, W2)

    def _L1_gnn_ref(x, edge_index, W_gat, att_src, att_dst, bias_gat, w1, b1, w2, b2, g1, be1, g2, be2):
        import jax, jax.numpy as jnp
        import numpy as np
        H, C = (8, 32)
        N, E = (3125, 50000)
        NEG_SLOPE = 0.2
        LN_EPS = 1e-05

        def layer_norm(x, g, b):
            mu = jnp.mean(x, axis=-1, keepdims=True)
            var = jnp.mean((x - mu) ** 2, axis=-1, keepdims=True)
            return (x - mu) * jax.lax.rsqrt(var + LN_EPS) * g + b

        def gat_conv(x, edge_index, W_gat, att_src, att_dst, bias_gat):
            n = x.shape[0]
            loops = jnp.arange(n, dtype=edge_index.dtype)
            ei = jnp.concatenate([edge_index, jnp.stack([loops, loops])], axis=1)
            src, dst = (ei[0], ei[1])
            xp = (x @ W_gat).reshape(n, H, C)
            a_src = jnp.einsum('nhc,hc->nh', xp, att_src)
            a_dst = jnp.einsum('nhc,hc->nh', xp, att_dst)
            alpha = jax.nn.leaky_relu(a_src[src] + a_dst[dst], NEG_SLOPE)
            m = jax.ops.segment_max(alpha, dst, num_segments=n)
            ea = jnp.exp(alpha - m[dst])
            denom = jax.ops.segment_sum(ea, dst, num_segments=n)
            attn = ea / (denom[dst] + 1e-16)
            msg = xp[src] * attn[..., None]
            out = jax.ops.segment_sum(msg, dst, num_segments=n)
            return out.mean(axis=1) + bias_gat
        h = gat_conv(x, edge_index, W_gat, att_src, att_dst, bias_gat)
        h = layer_norm(h + x, g1, be1)
        ff = jax.nn.relu(h @ w1 + b1) @ w2 + b2
        return layer_norm(ff + h, g2, be2)
    edge_index = jnp.stack([src, dst])
    h = jnp.maximum(_layernorm(x, axis=-1), 0.0)
    x = x + _L0_gnn_ref(h, src, dst, edge_attr_3, edge_attr_10, edge_weight, L0_gnn_W1, L0_gnn_W2)
    h = jnp.maximum(_layernorm(x, axis=-1), 0.0)
    x = x + _L1_gnn_ref(h, edge_index, L1_gnn_W_gat, L1_gnn_att_src, L1_gnn_att_dst, L1_gnn_bias_gat, L1_gnn_w1, L1_gnn_b1, L1_gnn_w2, L1_gnn_b2, L1_gnn_g1, L1_gnn_be1, L1_gnn_g2, L1_gnn_be2)
    return x

_drawn_inputs = setup_inputs


def setup_inputs(seed=0):
    import zlib

    import numpy as np

    out = dict(_drawn_inputs(seed))
    spreads = {'L1_gnn_bias_gat': (0.0, 0.1),
     'L1_gnn_b1': (0.0, 0.463),
     'L1_gnn_b2': (0.0, 0.1),
     'L1_gnn_g1': (1.0, 0.2),
     'L1_gnn_be1': (0.0, 0.1),
     'L1_gnn_g2': (1.0, 0.2),
     'L1_gnn_be2': (0.0, 0.1)}
    factors = {'L1_gnn_att_src': 3.677, 'L1_gnn_att_dst': 8.0}
    for name, (base, spread) in spreads.items():
        noise = np.random.default_rng([zlib.crc32(name.encode()), seed]).standard_normal(out[name].shape)
        drawn = base * np.exp(spread * noise) if base else spread * noise
        out[name] = jnp.asarray(drawn.astype(out[name].dtype))
    for name, factor in factors.items():
        out[name] = (out[name] * factor).astype(out[name].dtype)
    return out
```

```python
from contextlib import ExitStack

import numpy as np
import concourse.bass as bass
from concourse import mybir

F32 = mybir.dt.float32
I32 = mybir.dt.int32
BF16 = mybir.dt.bfloat16
ALU = mybir.AluOpType
ACT = mybir.ActivationFunctionType
AX = mybir.AxisListType

N, E, C = 3125, 53125, 32
P = 128
A = -(-N // P)
NP = A * P
J = 416
EP = P * J
S3 = 3 * C
HEADS = 8
K = 16
U = 8
TC = 4
CE = TC * P
NCH = J // TC
RING = 4
ROW1 = S3 + 2 * HEADS
LN_EPS = 1e-5
TANH_GAIN = 1.593
PW_S = 0.17677669529663687
PW_V = 0.25
BIG = 1e30
NOWHERE = 1e6


def tensor_network(nc, x, src, dst_ext, dst_ends, emb, vec, weight, w1rep, w2r, rep_sel, ident, identb, tri,
                   iota_b, w_gat, w_stack, att, sel_x, sel_attn, ffn1, ffn2, rows, b1, out):
    dram = lambda name, shape, dt: nc.dram_tensor(name, shape, dt, kind="Internal").ap()
    src_table0 = dram("src_table0", (NP, S3), BF16)
    node_table0 = dram("node_table0", (NP, C), F32)
    at_starts0 = dram("at_starts0", (EP, C), F32)
    dst_parts0 = dram("dst_parts0", (EP, S3), BF16)
    sums0 = dram("sums0", (EP, C), F32)
    src_table1 = dram("src_table1", (NP, ROW1 // 2), F32)
    node_table1 = dram("node_table1", (NP, 2 * HEADS), F32)
    at_starts1 = dram("at_starts1", (EP, 2 * HEADS), F32)
    attn_parts = dram("attn_parts", (EP, 3 * HEADS), BF16)
    sums1 = dram("sums1", (EP, C + HEADS), F32)

    nodes_of = lambda t: t.rearrange("(a b) c -> b a c", b=P)
    edges_of = lambda t: t.rearrange("(p j) c -> p j c", p=P)

    with ExitStack() as ctx:
        sb = lambda name, shape, dt=F32: ctx.enter_context(nc.sbuf_tensor(name, shape, dt))
        psum = lambda name, shape, dt=F32: ctx.enter_context(nc.psum_tensor(name, shape, dt))
        sem = lambda name: ctx.enter_context(nc.semaphore(name))

        area_a = sb("area_a", [P, J * C])
        area_b = sb("area_b", [P, J * ROW1 // 2])
        area_e = sb("area_e", [P, 2 * J * HEADS])
        a3 = area_a[:].rearrange("p (j c) -> p j c", c=C)
        b_parts = area_b[:, 0:J * S3 // 2].bitcast(BF16).rearrange("p (j c) -> p j c", c=S3)

        def views(area, sizes, start=0):
            got, at = [], start
            for s in sizes:
                got.append(area[:, at:at + s])
                at += s
            return got

        pr_, xt_, hid_, emb_, g_, tmp_, acc_, v_, sg_, sgn_ = views(
            area_b, [2 * 8 * CE, 2 * CE, 2 * CE, RING * CE, 16 * 120, 16 * 72, 16 * 24, 16 * 24, 256, 256])
        prod = pr_.rearrange("p (s u d e) -> p s u d e", s=2, u=4, d=2)
        x_t = xt_.bitcast(BF16).rearrange("p (s d e) -> p s d e", s=2, d=2)
        hid = hid_.rearrange("p (s e) -> p s e", s=2)
        emb_ring = emb_.rearrange("p (s e) -> p s e", s=RING)
        tp_out = g_.rearrange("p (t c) -> p t c", c=120)
        tmp = tmp_.rearrange("p (t i w) -> p t i w", t=16, i=3)
        acc = acc_.rearrange("p (t w) -> p t w", t=16)
        vbuf = v_.rearrange("p (t k w) -> p t k w", t=16, k=3)
        sg = sg_.rearrange("p (t w) -> p t w", t=16)
        sgn = sgn_.rearrange("p (t w) -> p t w", t=16)
        oh_hi_, oh_lo_, iota_x_ = views(area_b, [A * J // 2, 2 * P * 8, P * 8])
        oh_hi = oh_hi_.bitcast(BF16).rearrange("p (a j) -> p a j", a=A)
        oh_lo = oh_lo_.bitcast(BF16).rearrange("p (s b t) -> p s b t", s=2, b=P)
        iota_x = iota_x_.bitcast(BF16).rearrange("p (b t) -> p b t", b=P)
        hid1_, xself_ = views(area_b, [NP, A * 256])
        node_t = area_b[0:C, 9600:9600 + NP]
        xself = xself_.rearrange("p (a h c) -> p a h c", a=A, h=HEADS)
        vec_, wt_, r_, dlo_, dhi_, dbf_ = views(area_e, [3 * J, J, J, J, J, J])
        nvec = vec_.rearrange("p (i j) -> p i j", i=3)
        lo_i, hi_i = dlo_.bitcast(I32), dhi_.bitcast(I32)
        lo_bf, hi_bf = views(dbf_.bitcast(BF16), [J, J])
        gath1 = area_b[:].rearrange("p (j c) -> p j c", c=ROW1 // 2)
        h8 = lambda v: v.rearrange("p (j h) -> p j h", h=HEADS)
        alpha, self1 = map(h8, views(area_e, [J * HEADS] * 2))
        d16_, seg_, tmp8_ = views(area_a, [2 * J * HEADS, J * HEADS, J * HEADS])
        d16 = d16_.rearrange("p (j c) -> p j c", c=2 * HEADS)
        seg, tmp8 = h8(seg_), h8(tmp8_)
        apart = d16_[:, 0:J * 12].bitcast(BF16).rearrange("p (j c) -> p j c", c=3 * HEADS)
        pr1_, xrep_, xt1_ = views(area_e, [2 * 2 * CE, 2 * CE, CE + P])
        xt1_s = xt1_[0:S3, :].bitcast(BF16).rearrange("p (s e) -> p s e", s=2)
        prod1 = pr1_.rearrange("p (s g e) -> p s g e", s=2, g=2)
        xrep = xrep_.rearrange("p (s e) -> p s e", s=2)

        asrc_e = area_b[:].rearrange("p (j c) -> p j c", c=ROW1 // 2)[:, :, S3 // 2:ROW1 // 2]
        split_, att_, dnode_, tri_s, iota_, sel_, ends_ = views(
            area_b, [A * ROW1 // 2, 4 * P, A * 2 * HEADS, P, P // 2, 2 * P, 4 * P], J * S3 // 2)
        hsplit = split_.bitcast(BF16).rearrange("p (a c) -> p a c", a=A)
        att_s = att_[0:C, :].rearrange("p (k n) -> p k n", k=2)
        dnode = dnode_.rearrange("p (a c) -> p a c", a=A)
        iota_s = iota_.bitcast(BF16)
        sel_s = sel_[0:S3, :].bitcast(BF16).rearrange("p (u n) -> p u n", u=4)
        ends_s = ends_[0:HEADS, :].bitcast(I32).rearrange("p (k n) -> p k n", k=4)
        ident_s, identb_s = sb("ident_s", [P, P]), sb("identb_s", [P, P], BF16)
        ones_s = sb("ones_s", [P, P])
        w1_s, w2_s = sb("w1_s", [10, P]), sb("w2_s", [P, 2, 56])
        wgat_s = sb("wgat_s", [C, 2 * P])
        wst_s = sb("wst_s", [P, 2, C])
        selx_s, sela_s = sb("selx_s", [S3, P], BF16), sb("sela_s", [S3, TC, 2, P], BF16)
        f1_s, f2_s, b1_s, rows_s = sb("f1_s", [C, P]), sb("f2_s", [P, C]), sb("b1_s", [P, 1]), sb("rows_s", [P, 6, C])
        bias_g, b2_r, g1_r, be1_r, g2_r, be2_r = (rows_s[:, i, :] for i in range(6))
        src_s, dst_s = sb("src_s", [P, J], I32), sb("dst_s", [P, J + 2], I32)
        eps_s = sb("eps_s", [P, 1])
        same_prev, same_next = sb("same_prev", [P, J]), sb("same_next", [P, J])
        pen = sb("pen", [P, J])
        idx_ring = sb("idx_ring", [P, 2, 16], I32)
        xs_words = sb("xs_words", [P, RING, TC, ROW1 // 2])
        xs_ring = xs_words[:].bitcast(BF16)
        xd_area = sb("xd_area", [P, RING * TC * S3 // 2])
        xd_ring = xd_area[:].bitcast(BF16).rearrange("p (q t c) -> p q t c", q=RING, t=TC)
        flags_, car_t_, car_l = views(xd_area[:], [4 * P, P, HEADS])
        flags = flags_[0:HEADS, :].rearrange("p (k n) -> p k n", k=4)
        car_t = car_t_[0:HEADS, :]
        node = lambda name: sb(name, [P, A, C])
        xn, hn, nt, agg = node("xn"), node("hn"), node("nt"), sb("agg", [P, A, C + HEADS])
        hsp = hsplit[:, :, 0:S3]
        asrc_n = hsplit[:, :, S3:ROW1].bitcast(F32)
        st = sb("st", [P, 4, A])
        hist, start_i, end_i = sb("hist", [P, A]), sb("start_i", [P, A], I32), sb("end_i", [P, A], I32)
        e_lo, e_hi = sb("e_lo", [P, P]), sb("e_hi", [P, A])
        carry_in, last = sb("carry_in", [P, C]), sb("last", [P, C])
        endf = sb("endf", [P, 4])
        zerob = sb("zerob", [P, P], BF16)
        vatt = sb("vatt", [C, 16])

        rep = psum("rep", [P, 2, 2, CE])
        tp = psum("tp", [P, 2, CE])
        hp = psum("hp", [P, CE])
        po = psum("po", [P, CE])
        tpb = tp[:].bitcast(BF16).rearrange("p s (d e) -> p s d e", d=2)
        flat = rep[:].rearrange("p s g e -> p (s g e)")

        consts, x_in, dst_in = sem("consts"), sem("x_in"), sem("dst_in")
        zero_set, zeroed = sem("zero_set"), sem("zeroed")
        dve_step, act_step, pool_step = sem("dve_step"), sem("act_step"), sem("pool_step")
        var_ready, root_ready = sem("var_ready"), sem("root_ready")
        table0_ready, tables0 = sem("table0_ready"), sem("tables0")
        onehot_ready, onehot_used, hist_done = sem("onehot_ready"), sem("onehot_used"), sem("hist_done")
        hist_copied, cum_done, bounds_ready = sem("hist_copied"), sem("cum_done"), sem("bounds_ready")
        carry0, scattered0, starts0 = sem("carry0"), sem("scattered0"), sem("starts0")
        spread_ready, hi_cast, r1_done, mid_cast = sem("spread_ready"), sem("hi_cast"), sem("r1_done"), sem("mid_cast")
        parts_ready, parts_out = sem("parts_ready"), sem("parts_out")
        idx_copied = [sem(f"idx_copied{i}") for i in range(2)]
        idx_used = [sem(f"idx_used{i}") for i in range(2)]
        src_landed = [sem(f"src_landed{q}") for q in range(RING)]
        dst_landed = [sem(f"dst_landed{q}") for q in range(RING)]
        emb_landed = [sem(f"emb_landed{q}") for q in range(RING)]
        turned, hidden_done = sem("turned"), sem("hidden_done")
        turned_out, hidden_ready = sem("turned_out"), sem("hidden_ready")
        rep_ready, prod_done, tiles_done, tiles_out, post_read = (
            sem("rep_ready"), sem("prod_done"), sem("tiles_done"), sem("tiles_out"), sem("post_read"))
        gates_in, gates_out = sem("gates_in"), sem("gates_out")
        sums0_ready, sums0_out, ended0, last0 = sem("sums0_ready"), sem("sums0_out"), sem("ended0"), sem("last0")
        carried, flags_ready = sem("carried"), sem("flags_ready")
        nodes_in, nodes_turned, nodes_out = sem("nodes_in"), sem("nodes_turned"), sem("nodes_out")
        vatt_ready, att_done, table1_ready, tables1 = (
            sem("vatt_ready"), sem("att_done"), sem("table1_ready"), sem("tables1"))
        carry1, scattered1, starts1 = sem("carry1"), sem("scattered1"), sem("starts1")
        src1_landed = [sem(f"src1_landed{q}") for q in range(RING)]
        src1_kept = [sem(f"src1_kept{q}") for q in range(RING)]
        ends_in, ends_turned, ends_back, ends_done = (
            sem("ends_in"), sem("ends_turned"), sem("ends_back"), sem("ends_done"))
        exp_in, exp_out = sem("exp_in"), sem("exp_out")
        attn_ready, attn_out = sem("attn_ready"), sem("attn_out")
        x1_landed = [sem(f"x1_landed{q}") for q in range(RING)]
        at_landed = [sem(f"at_landed{q}") for q in range(RING)]
        turned1, turned1_out, xrep1, xrep1_out = sem("turned1"), sem("turned1_out"), sem("xrep1"), sem("xrep1_out")
        arep1, prod1_done, tiles1_done, tiles1_out = (
            sem("arep1"), sem("prod1_done"), sem("tiles1_done"), sem("tiles1_out"))
        sums1_ready, sums1_out, ended1, last1, agg_set = (
            sem("sums1_ready"), sem("sums1_out"), sem("ended1"), sem("last1"), sem("agg_set"))
        own_done, own_used, ffn_done, ffn_out, ffn2_done = (
            sem("own_done"), sem("own_used"), sem("ffn_done"), sem("ffn_out"), sem("ffn2_done"))
        result, written = sem("result"), sem("written")

        constants = [(ident_s, ident), (identb_s, identb), (tri_s, tri), (iota_s, iota_b), (sel_s, rep_sel),
                     (w1_s, w1rep), (w2_s, w2r), (wgat_s, w_gat), (wst_s, w_stack), (selx_s, sel_x),
                     (sela_s, sel_attn), (f1_s, ffn1), (f2_s, ffn2), (b1_s, b1),
                     (rows_s, rows.partition_broadcast(P)), (att_s, att.partition_broadcast(C)),
                     (ends_s, dst_ends.partition_broadcast(HEADS)), (src_s, src), (nvec, vec), (wt_, weight)]
        CONSTS = 16 * len(constants)
        QUARTERS = 4
        JQ = J // QUARTERS
        GROUPS = -(-NP // CE)
        LOOPS = J // 16

        def hold(eng, semaphore, value):
            eng.wait_ge(semaphore, value)
            eng.wait_ge(consts, CONSTS)

        def hold_pool(pool, semaphore, value):
            pool.wait_ge(semaphore, value)
            pool.sem_inc(pool_step, 1)

        class Steps:

            def __init__(self, eng, semaphore):
                self.eng, self.sem, self.count, self.offset = eng, semaphore, 0, 0

            def __call__(self, instruction):
                instruction.then_inc(self.sem, 1)
                self.count += 1
                self.eng.wait_ge(self.sem, self.offset + self.count)

        block = ctx.enter_context(nc.Block())

        @block.sync
        def _(sp):
            for q in range(RING):
                sp.sem_inc(src1_kept[q], 16)
            sp.dma_start(dst_s[:], dst_ext).then_inc(dst_in, 16)
            sp.dma_start(xn[:], nodes_of(x)).then_inc(x_in, 16)
            for to, of in constants:
                sp.dma_start(to[:] if not isinstance(to, bass.AP) else to, of).then_inc(consts, 16)
            sp.wait_ge(zero_set, 1)
            sp.dma_start(edges_of(at_starts0), a3).then_inc(zeroed, 16)
            sp.dma_start(edges_of(at_starts1), area_a[:, 0:J * 16].rearrange("p (j c) -> p j c", c=16)).then_inc(zeroed, 16)
            sp.wait_ge(table0_ready, 1)
            sp.dma_start(nodes_of(node_table0), hn[:]).then_inc(tables0, 16)
            sp.dma_start(nodes_of(src_table0), hsp).then_inc(tables0, 16)
            sp.wait_ge(scattered0, 16 * A)
            sp.dma_start(a3, edges_of(at_starts0)).then_inc(starts0, 16)
            for q in range(QUARTERS):
                sp.wait_ge(parts_ready, q + 1)
                sp.dma_start(edges_of(dst_parts0)[:, q * JQ:(q + 1) * JQ, :],
                             b_parts[:, q * JQ:(q + 1) * JQ, :]).then_inc(parts_out, 16)
            sp.wait_ge(parts_out, 16 * QUARTERS)
            with sp.Fori(0, LOOPS) as i:
                for q in range(RING):
                    hold(sp, turned, RING * i + q + 1)
                    sp.dma_start(xd_ring[:, q, :, :], edges_of(dst_parts0)[:, bass.ds(16 * i + TC * q, TC), :]).then_inc(dst_landed[q], 16)
                    hold(sp, hidden_done, RING * i + q + 1)
                    sp.dma_start(emb_ring[0:10, q, :], emb[:, bass.ds((RING * i + q) * CE, CE)]).then_inc(emb_landed[q], 16)
            sp.wait_ge(sums0_ready, 1)
            sp.dma_start(edges_of(sums0), a3).then_inc(sums0_out, 16)
            sp.wait_ge(table1_ready, 1)
            sp.dma_start(nodes_of(node_table1), dnode).then_inc(tables1, 16)
            sp.dma_start(nodes_of(src_table1), split_.rearrange("p (a c) -> p a c", a=A)).then_inc(tables1, 16)
            sp.wait_ge(scattered1, 16 * A)
            sp.wait_ge(sums0_out, 16)
            sp.dma_start(d16, edges_of(at_starts1)).then_inc(starts1, 16)
            sp.wait_ge(flags_ready, 1)
            with sp.Fori(0, LOOPS) as i:
                for q in range(RING):
                    hold(sp, src1_landed[q], 16 * TC * (i + 1))
                    sp.dma_start(gath1[:, bass.ds(16 * i + TC * q, TC), :], xs_words[:, q, :, :]).then_inc(src1_kept[q], 16)
            sp.wait_ge(attn_ready, 1)
            sp.dma_start(edges_of(attn_parts), apart).then_inc(attn_out, 16)
            sp.dma_start(edges_of(sums1)[:, :, C:C + HEADS], self1).then_inc(attn_out, 16)
            sp.wait_ge(attn_out, 32)
            with sp.Fori(0, LOOPS) as i:
                for q in range(RING):
                    hold(sp, turned1, RING * i + q + 1)
                    sp.dma_start(xs_words[:, q, :, 0:S3 // 2], gath1[:, bass.ds(16 * i + TC * q, TC), 0:S3 // 2]).then_inc(x1_landed[q], 16)
                    sp.dma_start(xd_ring[:, q, 0, :], edges_of(attn_parts)[:, bass.ds(16 * i + TC * q, TC), :].rearrange("p t c -> p (t c)")).then_inc(at_landed[q], 16)
            sp.wait_ge(sums1_ready, 1)
            sp.dma_start(edges_of(sums1)[:, :, 0:C], a3).then_inc(sums1_out, 16)
            sp.wait_ge(result, 1)
            full = N // P
            sp.dma_start(out[0:full * P, :].rearrange("(a b) c -> b a c", b=P), hn[:, 0:full, :]).then_inc(written, 16)
            sp.dma_start(out[full * P:N, :], hn[0:N - full * P, full, :]).then_inc(written, 16)
            sp.wait_ge(written, 32)

        @block.gpsimd
        def _(pool):
            pool.memset(area_a[:], 0.0).then_inc(zero_set, 1)

            def gather_row(to, table, index, last_row, semaphore):
                pool.indirect_dma_start(to, None, table, bass.IndirectOffsetOnAxis(ap=index, axis=0),
                                        bounds_check=last_row, oob_is_err=False).then_inc(semaphore, 16)

            def gather_sources(table, ring, landed, first):
                with pool.Fori(0, LOOPS // 2) as i:
                    for half in range(2):
                        if first:
                            hold_pool(pool, turned, 2 * RING * i + RING * half + 1)
                        else:
                            hold_pool(pool, src1_kept[0], 16 * (2 * i + half) + 16)
                        pool.tensor_copy(idx_ring[:, half, :], src_s[:, bass.ds(32 * i + 16 * half, 16)]).then_inc(idx_copied[half], 1)
                        hold_pool(pool, idx_copied[half], i + 1 + (0 if first else LOOPS // 2))
                        for q in range(RING):
                            c = 2 * RING * i + RING * half + q
                            if first:
                                hold_pool(pool, turned, c + 1)
                            else:
                                hold_pool(pool, src1_kept[q], 16 * (2 * i + half) + 16)
                            for t in range(TC):
                                gather_row(ring[:, q, t, :], table, idx_ring[:, half, TC * q + t:TC * q + t + 1],
                                           NP - 1, landed[q])

            pool.wait_ge(tables0, 32)
            gather_row(carry_in[:], node_table0, dst_s[:, 0:1], NP - 1, carry0)
            pool.wait_ge(bounds_ready, 1)
            pool.wait_ge(zeroed, 32)
            for a in range(A):
                pool.indirect_dma_start(at_starts0, bass.IndirectOffsetOnAxis(ap=start_i[:, a:a + 1], axis=0), hn[:, a, :],
                                        None, bounds_check=EP - 1, oob_is_err=False).then_inc(scattered0, 16)
            pool.wait_ge(consts, CONSTS)
            gather_sources(src_table0, xs_ring[:, :, :, 0:S3], src_landed, True)
            pool.wait_ge(sums0_out, 16)
            pool.wait_ge(agg_set, 1)
            for a in range(A):
                gather_row(agg[:, a, 0:C], sums0, end_i[:, a:a + 1], EP - 1, ended0)
            pool.wait_ge(tables1, 32)
            gather_row(carry_in[:, 0:16], node_table1, dst_s[:, 0:1], NP - 1, carry1)
            for a in range(A):
                pool.indirect_dma_start(at_starts1, bass.IndirectOffsetOnAxis(ap=start_i[:, a:a + 1], axis=0), dnode[:, a, :],
                                        None, bounds_check=EP - 1, oob_is_err=False).then_inc(scattered1, 16)
            gather_sources(src_table1, xs_words, src1_landed, False)
            pool.wait_ge(sums1_out, 16)
            pool.wait_ge(attn_out, 32)
            pool.wait_ge(agg_set, 2)
            for a in range(A):
                gather_row(agg[:, a, :], sums1, end_i[:, a:a + 1], EP - 1, ended1)

        @block.vector
        def _(dve):
            step = Steps(dve, dve_step)
            roots = [0]
            across = lambda v, n=C: v.unsqueeze(2).to_broadcast([P, A, n])
            row = lambda v: v.unsqueeze(1).to_broadcast([P, A, C])

            def root():
                roots[0] += 1
                dve.wait_ge(root_ready, roots[0])

            def layer_norm(to, of, scratch):
                step(dve.reduce_sum(st[:, 0, :], of, AX.X))
                step(dve.tensor_scalar(st[:, 0, :], st[:, 0, :], -1.0 / C, None, ALU.mult))
                step(dve.tensor_tensor(scratch, of, across(st[:, 0, :]), ALU.add))
                step(dve.tensor_tensor(to, scratch, scratch, ALU.mult))
                dve.reduce_sum(st[:, 1, :], to, AX.X).then_inc(var_ready, 1)
                root()
                step(dve.reciprocal(st[:, 3, :], st[:, 2, :]))
                step(dve.tensor_tensor(to, scratch, across(st[:, 3, :]), ALU.mult))

            def split(parts, of, scratch):
                step(dve.tensor_copy(parts[0], of))
                step(dve.tensor_tensor(scratch, of, parts[0], ALU.subtract))
                step(dve.tensor_copy(parts[1], scratch))
                step(dve.tensor_tensor(scratch, scratch, parts[1], ALU.subtract))
                return dve.tensor_copy(parts[2], scratch)

            three = lambda v: [v[:, :, C * k:C * (k + 1)] for k in range(3)]

            step(dve.memset(eps_s[:], LN_EPS))
            step(dve.memset(ones_s[:], 1.0))
            step(dve.memset(zerob[:], 0.0))
            step(dve.memset(carry_in[:], 0.0))
            dve.memset(agg[:], 0.0).then_inc(agg_set, 1)

            dve.wait_ge(x_in, 16)
            layer_norm(hn[:], xn[:], nt[:])
            step(dve.tensor_scalar(hn[:], hn[:], 0.0, None, ALU.max))
            split(three(hsp), hn[:], nt[:]).then_inc(table0_ready, 1)

            dve.wait_ge(dst_in, 16)
            target = dst_s[:, 1:J + 1]
            dve.wait_ge(consts, CONSTS)
            step(dve.tensor_tensor(same_prev[:], target, dst_s[:, 0:J], ALU.is_equal))
            step(dve.tensor_tensor(same_next[:], target, dst_s[:, 2:J + 2], ALU.is_equal))
            step(dve.tensor_scalar(lo_i, target, P - 1, None, ALU.bitwise_and))
            step(dve.tensor_scalar(hi_i, target, P.bit_length() - 1, None, ALU.logical_shift_right))
            step(dve.tensor_copy(lo_bf, lo_i))
            step(dve.tensor_copy(hi_bf, hi_i))
            step(dve.tensor_copy(endf[:, 0:1], lo_i[:, J - 1:J]))
            step(dve.tensor_copy(endf[:, 1:2], hi_i[:, J - 1:J]))
            step(dve.tensor_copy(iota_x, iota_s.unsqueeze(2).to_broadcast([P, P, 16])))
            for a in range(A):
                ins = dve.tensor_scalar(oh_hi[:, a, :], hi_bf, float(a), None, ALU.is_equal)
                if a == A - 1:
                    step(ins)
            with dve.Fori(0, LOOPS // 2) as i:
                for half in range(2):
                    dve.wait_ge(onehot_used, 2 * i + half + 1)
                    dve.tensor_tensor(oh_lo[:, half, :, :], iota_x,
                                      lo_bf[:, bass.ds(32 * i + 16 * half, 16)].unsqueeze(1).to_broadcast([P, P, 16]),
                                      ALU.is_equal).then_inc(onehot_ready, 1)
            step(dve.tensor_scalar(e_lo[:], iota_s, endf[:, 0:1], same_next[:, J - 1:J], ALU.is_equal, ALU.mult))
            step(dve.tensor_scalar(e_hi[:], iota_s[:, 0:A], endf[:, 1:2], None, ALU.is_equal))

            dve.wait_ge(hist_done, 1)
            dve.tensor_copy(hist[:], po[:, 0:A]).then_inc(hist_copied, 1)
            dve.wait_ge(hist_copied, 1)
            dve.wait_ge(cum_done, 1)
            step(dve.tensor_tensor_scan(st[:, 0, :], ones_s[:, 0:A], hp[:, 32:32 + A], 0.0, ALU.mult, ALU.add))
            step(dve.tensor_tensor(st[:, 0, :], st[:, 0, :], hp[:, 32:32 + A], ALU.subtract))
            step(dve.tensor_tensor(st[:, 0, :], st[:, 0, :], hp[:, 0:A], ALU.add))
            step(dve.tensor_scalar(st[:, 1, :], hist[:], 0.0, NOWHERE, ALU.is_equal, ALU.mult))
            step(dve.tensor_tensor(st[:, 2, :], st[:, 0, :], hist[:], ALU.subtract))
            step(dve.tensor_tensor(start_i[:], st[:, 2, :], st[:, 1, :], ALU.add))
            dve.scalar_tensor_tensor(out=end_i[:], in0=st[:, 0, :], scalar=-1.0, in1=st[:, 1, :],
                                     op0=ALU.add, op1=ALU.add).then_inc(bounds_ready, 1)
            dve.wait_ge(bounds_ready, 1)

            step(dve.tensor_tensor(r_, nvec[:, 0, :], nvec[:, 0, :], ALU.mult))
            for k in (1, 2):
                step(dve.tensor_tensor(dlo_, nvec[:, k, :], nvec[:, k, :], ALU.mult))
                ins = dve.tensor_tensor(r_, r_, dlo_, ALU.add)
                if k == 1:
                    step(ins)
            ins.then_inc(var_ready, 1)
            root()
            step(dve.reciprocal(dlo_, r_))
            step(dve.tensor_tensor(nvec, nvec, dlo_.unsqueeze(1).to_broadcast([P, 3, J]), ALU.mult))
            step(dve.tensor_scalar(wt_, wt_, TANH_GAIN, None, ALU.mult))
            step(dve.tensor_scalar(w2_s[:, :, 48:56], w2_s[:, :, 48:56], PW_V / 3 ** 0.5, None, ALU.mult))
            step(dve.scalar_tensor_tensor(out=w2_s[:, :, 48:56], in0=w2_s[:, :, 40:48], scalar=-PW_V / 6 ** 0.5,
                                          in1=w2_s[:, :, 48:56], op0=ALU.mult, op1=ALU.add))
            step(dve.tensor_scalar(w2_s[:, :, 40:48], w2_s[:, :, 40:48], PW_V * 1.5 ** 0.5, None, ALU.mult))
            step(dve.tensor_scalar(w2_s[:, :, 16:24], w2_s[:, :, 16:24], PW_V, None, ALU.mult))
            step(dve.tensor_scalar(wst_s[:], wst_s[:], 1.0 / HEADS, None, ALU.mult))

            dve.wait_ge(starts0, 16)
            dve.wait_ge(carry0, 16)
            for c in range(C):
                ins = dve.tensor_tensor_scan(a3[:, :, c], same_prev[:], a3[:, :, c], carry_in[:, c:c + 1], ALU.mult, ALU.add)
            ins.then_inc(spread_ready, 1)
            dve.wait_ge(spread_ready, 1)
            quarter = lambda v, q: v[:, q * JQ:(q + 1) * JQ, :]
            for q in range(QUARTERS + 1):
                if q < QUARTERS:
                    dve.wait_ge(hi_cast, q + 1)
                    dve.tensor_tensor(quarter(a3, q), quarter(a3, q), quarter(b_parts, q)[:, :, 0:C], ALU.subtract).then_inc(r1_done, 1)
                if q > 0:
                    dve.wait_ge(mid_cast, q)
                    dve.tensor_tensor(quarter(b_parts, q - 1)[:, :, 2 * C:S3], quarter(a3, q - 1),
                                      quarter(b_parts, q - 1)[:, :, C:2 * C], ALU.subtract).then_inc(parts_ready, 1)
            dve.wait_ge(parts_out, 16 * QUARTERS)

            post_steps = 8
            base = step.count
            with dve.Fori(0, LOOPS) as i:
                step.offset, step.count = i * post_steps, base
                for q in range(RING):
                    dve.wait_ge(hidden_ready, RING * i + q + 2)
                    if True:
                        dve.wait_ge(tiles_done, RING * i + q + 1)
                    for u in range(4):
                        dve.wait_ge(rep_ready, 4 * (RING * i + q) + u + 1)
                        dve.tensor_tensor(prod[:, q % 2, u, :, :], rep[:, u % 2, :, :],
                                          hid[:, q % 2, :].unsqueeze(1).to_broadcast([P, 2, CE]), ALU.mult).then_inc(prod_done, 1)
                tiles = bass.ds(16 * i, 16)
                dve.wait_ge(tiles_out, RING * i + RING + 1)
                vect = tp_out[:, :, 24:120].rearrange("p t (i w) -> p t i w", i=3)
                n_t = nvec[:, :, tiles].rearrange("p i t -> p t i").unsqueeze(3)
                step(dve.tensor_tensor(tmp, vect[:, :, :, 0:24], n_t.to_broadcast([P, 16, 3, 24]), ALU.mult))
                step(dve.tensor_tensor(acc, tp_out[:, :, 0:24], tmp[:, :, 0, :], ALU.add))
                step(dve.tensor_tensor(acc, acc, tmp[:, :, 1, :], ALU.add))
                dve.tensor_tensor(acc, acc, tmp[:, :, 2, :], ALU.add).then_inc(gates_in, 1)
                dve.wait_ge(gates_in, i + 1)
                step(dve.tensor_tensor(vbuf, n_t.to_broadcast([P, 16, 3, 8]),
                                       acc[:, :, 16:24].unsqueeze(2).to_broadcast([P, 16, 3, 8]), ALU.mult))
                dve.tensor_tensor(vbuf, vbuf, vect[:, :, :, 24:32], ALU.add).then_inc(post_read, 1)
                dve.wait_ge(gates_out, i + 1)
                w_t = wt_[:, tiles].unsqueeze(2)
                step(dve.tensor_tensor(sgn[:, :, 0:8], sg[:, :, 8:16], w_t.to_broadcast([P, 16, 8]), ALU.mult))
                step(dve.tensor_tensor(a3[:, tiles, 0:8], sg[:, :, 0:8], w_t.to_broadcast([P, 16, 8]), ALU.mult))
                dve.wait_ge(post_read, i + 2)
                step(dve.tensor_tensor(a3[:, tiles, 8:32].rearrange("p t (w k) -> p t k w", k=3), vbuf,
                                       sgn[:, :, 0:8].unsqueeze(2).to_broadcast([P, 16, 3, 8]), ALU.mult))
                assert step.count - base == post_steps - 1
                step(dve.tensor_copy(endf[:, 2:3], endf[:, 1:2]))
            step.offset, step.count = 0, base + post_steps * LOOPS

            def sum_edges(ready, last_ready):
                for c in range(C):
                    ins = dve.tensor_tensor_scan(a3[:, :, c], same_prev[:], a3[:, :, c], 0.0, ALU.mult, ALU.add)
                ins.then_inc(ready, 1)
                dve.wait_ge(ready, 1)
                step(dve.tensor_copy(last[:], a3[:, J - 1, :]))
                dve.tensor_tensor(nt[:], last[:].unsqueeze(1).to_broadcast([P, A, C]), across(e_hi[:]), ALU.mult).then_inc(last_ready, 1)


            def add_carried(to, n):
                dve.wait_ge(carried, n)
                for k in range(2):
                    half = to.rearrange("p a c -> p (a c)")[:, A * C // 2 * k:A * C // 2 * (k + 1)]
                    ins = dve.tensor_tensor(half, half, (po, hp)[k][:, 0:A * C // 2], ALU.add)
                step(ins)

            sum_edges(sums0_ready, last0)
            add_carried(xn[:], 1)
            dve.wait_ge(ended0, 16 * A)
            step(dve.tensor_tensor(xn[:], xn[:], agg[:, :, 0:C], ALU.add))

            layer_norm(hn[:], xn[:], nt[:])
            dve.tensor_scalar(hn[:], hn[:], 0.0, None, ALU.max).then_inc(nodes_in, 1)
            dve.wait_ge(nodes_in, 1)
            for k in range(2):
                step(dve.tensor_tensor(att_s[:, k, :], att_s[:, k, :], wgat_s[:], ALU.mult))
                ins = dve.reduce_sum(vatt[:, 8 * k:8 * k + 8], att_s[:, k, :].rearrange("p (h c) -> p h c", c=C), AX.X)
            ins.then_inc(vatt_ready, 1)
            step(split(three(hsp), hn[:], nt[:]))
            dve.memset(agg[:, :, 0:C], 0.0)
            dve.memset(agg[:, :, C:C + HEADS], 1.0).then_inc(agg_set, 1)
            dve.wait_ge(att_done, 1)
            att_ps = po[:, 0:A * 16].rearrange("p (a h) -> p a h", h=16)
            step(dve.tensor_copy(asrc_n, att_ps[:, :, 0:8]))
            step(dve.tensor_copy(dnode[:, :, 0:8], att_ps[:, :, 8:16]))
            dve.tensor_tensor(dnode[:, :, 8:16], asrc_n, att_ps[:, :, 8:16], ALU.add).then_inc(table1_ready, 1)

            first_t, last_t, prev_t, next_t = (ends_s[:, k, :] for k in range(4))
            step(dve.tensor_tensor(flags[:, 2, :], first_t, last_t, ALU.is_equal))
            for k, (own, other) in enumerate(((first_t, prev_t), (last_t, next_t))):
                step(dve.tensor_tensor(flags[:, k, :], own, other, ALU.is_equal))
                step(dve.tensor_tensor(flags[:, k, :], flags[:, k, :], flags[:, 2, :], ALU.mult))
            for k in range(2):
                ins = dve.tensor_scalar(flags[:, 2 + k, :], flags[:, k, :], -1.0, BIG, ALU.add, ALU.mult)
            ins.then_inc(flags_ready, 1)
            dve.wait_ge(flags_ready, 1)

            carries = [0]

            def carry(values, forward, maximum):
                step(dve.tensor_copy(car_l, values))
                init = -BIG if maximum else 0.0
                flag = flags[:, (2 if maximum else 0) + (0 if forward else 1), :]
                ops = (ALU.add, ALU.max) if maximum else (ALU.mult, ALU.add)
                end = slice(0, 1) if forward else slice(P - 1, P)
                dve.memset(car_t[:, end], init).then_inc(ends_in, 1)
                carries[0] += 1
                dve.wait_ge(ends_turned, carries[0])
                if forward:
                    ins = dve.tensor_tensor_scan(car_t[:, 1:P], flag[:, 0:P - 1], hp[0:HEADS, 0:P - 1], init, *ops)
                else:
                    ins = dve.tensor_tensor_scan(car_t[:, P - 2::-1], flag[:, P - 1:0:-1], hp[0:HEADS, P - 1:0:-1], init, *ops)
                ins.then_inc(ends_back, 1)
                dve.wait_ge(ends_done, carries[0])
                step(dve.tensor_copy(car_l, hp[:, P:P + HEADS]))

            def scan_heads(to, mask, of, forward, maximum, initial):
                ops = (ALU.add, ALU.max) if maximum else (ALU.mult, ALU.add)
                d = slice(None) if forward else slice(None, None, -1)
                for h in range(HEADS):
                    ins = dve.tensor_tensor_scan(to[:, d, h], mask[:, d], of[:, d, h],
                                                 initial if initial is not None else car_l[:, h:h + 1], *ops)
                step(ins)

            dve.wait_ge(starts1, 16)
            dve.wait_ge(carry1, 16)
            for h in range(2 * HEADS):
                ins = dve.tensor_tensor_scan(d16[:, :, h], same_prev[:], d16[:, :, h], carry_in[:, h:h + 1], ALU.mult, ALU.add)
            step(ins)
            leaky = lambda v: dve.scalar_tensor_tensor(out=v, in0=v, scalar=0.2, in1=v, op0=ALU.mult, op1=ALU.max)
            step(dve.tensor_copy(self1, d16[:, :, 8:16]))
            step(leaky(self1))
            for q in range(RING):
                dve.wait_ge(src1_kept[q], 16 * LOOPS + 16)
            step(dve.tensor_tensor(alpha, asrc_e, d16[:, :, 0:8], ALU.add))
            step(leaky(alpha))
            step(dve.tensor_tensor(seg, alpha, self1, ALU.max))
            step(dve.tensor_scalar(pen[:], same_prev[:], -1.0, BIG, ALU.add, ALU.mult))
            scan_heads(tmp8, pen[:], seg, True, True, -BIG)
            carry(tmp8[:, J - 1, :], True, True)
            scan_heads(seg, pen[:], seg, True, True, None)
            step(dve.tensor_scalar(pen[:], same_next[:], -1.0, BIG, ALU.add, ALU.mult))
            scan_heads(tmp8, pen[:], seg, False, True, -BIG)
            carry(tmp8[:, 0, :], False, True)
            scan_heads(seg, pen[:], seg, False, True, None)
            step(dve.tensor_tensor(alpha, alpha, seg, ALU.subtract))
            dve.tensor_tensor(self1, self1, seg, ALU.subtract).then_inc(exp_in, 1)
            dve.wait_ge(exp_out, 1)
            scan_heads(tmp8, same_prev[:], alpha, True, False, 0.0)
            carry(tmp8[:, J - 1, :], True, False)
            scan_heads(seg, same_prev[:], alpha, True, False, None)
            step(dve.tensor_scalar(pen[:], same_next[:], -1.0, 1.0, ALU.mult, ALU.add))
            step(dve.tensor_tensor(seg, seg, pen[:].unsqueeze(2).to_broadcast([P, J, HEADS]), ALU.mult))
            scan_heads(tmp8, same_next[:], seg, False, False, 0.0)
            carry(tmp8[:, 0, :], False, False)
            scan_heads(seg, same_next[:], seg, False, False, None)
            dve.wait_ge(exp_out, 2)
            step(dve.scalar_tensor_tensor(out=seg, in0=seg, scalar=1e-16, in1=self1, op0=ALU.add, op1=ALU.add))
            step(dve.reciprocal(seg, seg))
            step(dve.tensor_tensor(alpha, alpha, seg, ALU.mult))
            step(dve.tensor_tensor(self1, self1, seg, ALU.mult))
            split([apart[:, :, 8 * k:8 * k + 8] for k in range(3)], alpha, alpha).then_inc(attn_ready, 1)
            dve.wait_ge(attn_ready, 1)

            with dve.Fori(0, LOOPS) as i:
                for q in range(RING):
                    c = RING * i + q
                    dve.wait_ge(xrep1_out, c + 2)
                    dve.wait_ge(tiles1_done, c + 1)
                    dve.wait_ge(arep1, c + 1)
                    dve.tensor_tensor(prod1[:, q % 2, :, :], rep[:, q % 2, :, :],
                                      xrep[:, q % 2, :].unsqueeze(1).to_broadcast([P, 2, CE]), ALU.mult).then_inc(prod1_done, 1)
            dve.wait_ge(tiles1_out, NCH + 1)
            sum_edges(sums1_ready, last1)

            for g in range(-(-A // 2)):
                n = min(2, A - 2 * g)
                dve.wait_ge(own_done, g + 1)
                of = rep[:, g % 4 // 2, g % 2, 0:256 * n].rearrange("p (a h c) -> p a h c", h=HEADS, c=C)
                if g == 0:
                    dve.wait_ge(ended1, 16 * A)
                for k in range(n):
                    ins = dve.tensor_tensor(xself[:, 2 * g + k, :, :], of[:, k],
                                            agg[:, 2 * g + k, C:C + HEADS].unsqueeze(2).to_broadcast([P, HEADS, C]), ALU.mult)
                ins.then_inc(own_used, 1)
            dve.wait_ge(own_used, -(-A // 2))
            hist_row = lambda v: v[:].rearrange("p a c -> p (a c)")
            dve.wait_ge(carried, 2)
            step(dve.reduce_sum(nt[:], xself.rearrange("p a h c -> p a c h"), AX.X))
            step(dve.scalar_tensor_tensor(out=hist_row(nt), in0=hist_row(nt), scalar=1.0 / HEADS, in1=hist_row(hn), op0=ALU.mult, op1=ALU.add))
            step(dve.tensor_tensor(nt[:], nt[:], agg[:, :, 0:C], ALU.add))
            step(dve.tensor_tensor(nt[:], nt[:], row(bias_g), ALU.add))
            add_carried(nt[:], 2)
            layer_norm(hn[:], nt[:], agg[:, :, 0:C])
            step(dve.tensor_tensor(hn[:], hn[:], row(g1_r), ALU.mult))
            dve.tensor_tensor(hn[:], hn[:], row(be1_r), ALU.add).then_inc(nodes_in, 1)
            dve.wait_ge(nodes_in, 2)
            dve.wait_ge(nodes_turned, 3 * GROUPS)
            step(dve.tensor_tensor(hn[:], hn[:], row(b2_r), ALU.add))
            dve.wait_ge(ffn2_done, 1)
            step(dve.tensor_tensor(hist_row(nt), hist_row(hn), rep[:, 0, :, :].rearrange("p g e -> p (g e)")[:, 0:A * C], ALU.add))
            layer_norm(hn[:], nt[:], agg[:, :, 0:C])
            step(dve.tensor_tensor(hn[:], hn[:], row(g2_r), ALU.mult))
            step(dve.tensor_tensor(hn[:], hn[:], row(be2_r), ALU.add))
            dve.tensor_tensor(hn[:], hn[:], xn[:], ALU.add).then_inc(result, 1)

        @block.scalar
        def _(act):
            roots = [0]

            def root_of(to, of, scale, bias):
                roots[0] += 1
                act.wait_ge(var_ready, roots[0])
                act.activation(to, of, ACT.Sqrt, scale=scale, bias=bias).then_inc(root_ready, 1)

            variance_root = lambda: root_of(st[:, 2, :], st[:, 1, :], 1.0 / C, eps_s[:])

            def nodes_to_sbuf(first):
                for g in range(GROUPS):
                    n = min(CE, NP - CE * g)
                    act.wait_ge(nodes_turned, first + g + 1)
                    act.activation(node_t[:, CE * g:CE * g + n], tp[0:C, g % 2, 0:n], ACT.Copy).then_inc(nodes_out, 1)

            act.sem_inc(turned_out, 2)
            act.sem_inc(hidden_ready, 1)
            act.sem_inc(tiles_out, 1)
            act.sem_inc(turned1_out, 2)
            act.sem_inc(xrep1_out, 1)
            act.sem_inc(tiles1_out, 1)
            act.sem_inc(post_read, 1)
            act.sem_inc(prod_done, 8)
            act.sem_inc(prod1_done, 2)
            variance_root()
            roots[0] += 1
            act.wait_ge(var_ready, roots[0])
            act.activation(r_, r_, ACT.Sqrt).then_inc(root_ready, 1)
            quarter = lambda v, q: v[:, q * JQ:(q + 1) * JQ, :]
            act.wait_ge(spread_ready, 1)
            for q in range(QUARTERS + 1):
                if q < QUARTERS:
                    act.activation(quarter(b_parts, q)[:, :, 0:C], quarter(a3, q), ACT.Copy).then_inc(hi_cast, 1)
                if q > 0:
                    act.wait_ge(r1_done, q)
                    act.activation(quarter(b_parts, q - 1)[:, :, C:2 * C], quarter(a3, q - 1), ACT.Copy).then_inc(mid_cast, 1)
            act.wait_ge(parts_out, 16 * QUARTERS)

            def open_chunk(c, s):
                hold(act, turned, c + 1 + RING)
                act.activation(x_t[0:S3, s, :, :], tpb[0:S3, s, :, :], ACT.Copy).then_inc(turned_out, 1)
                hold(act, prod_done, 4 * c + 4)
                hold(act, hidden_done, c + 1 + RING)
                act.activation(hid[:, s, :], hp[:], ACT.Relu, scale=(2.0 / 10.0 / K) ** 0.5).then_inc(hidden_ready, 1)

            open_chunk(0, 0)
            def group(i, more):
                for q in range(RING):
                    c = RING * i + q
                    if more or q + 1 < RING:
                        open_chunk(c + 1, (q + 1) % 2)
                    if q == 0:
                        hold(act, post_read, i + 1)
                    hold(act, tiles_done, c + 3)
                    act.activation(tp_out[:, TC * q:TC * q + TC, :], po[:, 0:480].rearrange("p (t c) -> p t c", c=120), ACT.Copy).then_inc(tiles_out, 1)
                hold(act, gates_in, i + 1)
                act.activation(sg, acc[:, :, 0:16], ACT.Tanh, scale=PW_S).then_inc(gates_out, 1)

            with act.Fori(0, LOOPS - 1) as i:
                group(i, True)
            group(LOOPS - 1, False)

            variance_root()
            nodes_to_sbuf(0)
            act.wait_ge(exp_in, 1)
            act.activation(alpha, alpha, ACT.Exp).then_inc(exp_out, 1)
            act.activation(self1, self1, ACT.Exp).then_inc(exp_out, 1)
            act.wait_ge(attn_out, 32)

            def open_chunk1(c, s):
                hold(act, turned1, c + 1 + RING)
                act.activation(xt1_s[:, s, :], tp[:].bitcast(BF16)[0:S3, s, 0:CE + P], ACT.Copy).then_inc(turned1_out, 1)
                hold(act, prod1_done, c + 1)
                hold(act, xrep1, c + 1)
                act.activation(xrep[:, s, :], hp[:], ACT.Copy).then_inc(xrep1_out, 1)

            open_chunk1(0, 0)

            def group1(i, more):
                for q in range(RING):
                    c = RING * i + q
                    if more or q + 1 < RING:
                        open_chunk1(c + 1, (q + 1) % 2)
                    hold(act, tiles1_done, c + 3)
                    act.activation(a3[:, bass.ds(16 * i + TC * q, TC), :], po[:, 0:TC * C].rearrange("p (t c) -> p t c", c=C), ACT.Copy).then_inc(tiles1_out, 1)

            with act.Fori(0, LOOPS - 1) as i:
                group1(i, True)
            group1(LOOPS - 1, False)
            nodes_to_sbuf(GROUPS)
            variance_root()
            nodes_to_sbuf(2 * GROUPS)
            for g in range(GROUPS):
                n = min(CE, NP - CE * g)
                act.wait_ge(ffn_done, g + 1)
                act.activation(hid1_[:, CE * g:CE * g + n], tp[:, g % 2, 0:n], ACT.Relu, bias=b1_s[:]).then_inc(ffn_out, 1)
            variance_root()

        @block.tensor
        def _(pe):
            pe.sem_inc(onehot_used, 2)
            pe.sem_inc(turned, RING)
            pe.sem_inc(hidden_done, RING)
            pe.sem_inc(tiles_done, 2)
            pe.sem_inc(turned1, RING)
            pe.sem_inc(tiles1_done, 2)
            pe.wait_ge(consts, CONSTS)
            pe.wait_ge(agg_set, 1)
            pe.matmul(po[:, 0:A], zerob[:], zerob[:, 0:A], start=True, stop=False, skip_group_check=True)
            with pe.Fori(0, LOOPS // 2) as i:
                for half in range(2):
                    pe.wait_ge(onehot_ready, 2 * i + half + 1)
                    for t in range(16):
                        ins = pe.matmul(po[:, 0:A], oh_lo[:, half, :, t], oh_hi[:, :, bass.ds(32 * i + 16 * half + t, 1)].squeeze(2),
                                        start=False, stop=False, skip_group_check=True)
                    ins.then_inc(onehot_used, 1)
            pe.matmul(po[:, 0:A], zerob[:], zerob[:, 0:A], start=False, stop=True, skip_group_check=True).then_inc(hist_done, 1)
            pe.wait_ge(hist_copied, 1)
            pe.matmul(hp[:, 0:A], tri_s, hist[:], start=True, stop=True)
            pe.matmul(hp[:, 32:32 + A], ones_s[:], hist[:], start=True, stop=True).then_inc(cum_done, 1)
            pe.wait_ge(parts_ready, QUARTERS)

            def turn(c, i, q):
                s = q % 2
                pe.wait_ge(turned_out, c + 1)
                pe.wait_ge(src_landed[q], 16 * TC * (i + 1))
                for t in range(TC):
                    pe.transpose(tpb[0:S3, s, 0, P * t:P * t + P], xs_ring[:, q, t, 0:S3], identb_s[:])
                pe.wait_ge(dst_landed[q], 16 * (i + 1))
                for t in range(TC):
                    ins = pe.transpose(tpb[0:S3, s, 1, P * t:P * t + P], xd_ring[:, q, t, :], identb_s[:])
                ins.then_inc(turned, 1)
                pe.wait_ge(hidden_ready, c + 1)
                pe.wait_ge(emb_landed[q], 16 * (i + 1))
                pe.matmul(hp[:], w1_s[:], emb_ring[0:10, q, :], start=True, stop=True).then_inc(hidden_done, 1)

            def repeat(c, q, u):
                if u == 0:
                    pe.wait_ge(turned_out, c + 3)
                pe.wait_ge(prod_done, 4 * c + u + 7)
                for d in range(2):
                    ins = pe.matmul(rep[:, u % 2, d, :], sel_s[:, u, :], x_t[0:S3, q % 2, d, :], start=True, stop=True)
                ins.then_inc(rep_ready, 1)

            def contract(c, q, u):
                pe.wait_ge(prod_done, 4 * c + u + 9)
                if u == 0:
                    pe.wait_ge(tiles_out, c + 1)
                lo, hi = (0, 24) if u == 0 else (24, 56)
                at = 0 if u == 0 else 24 + 32 * (u - 1)
                for t in range(TC):
                    for d in range(2):
                        ins = pe.matmul(po[:, 120 * t + at:120 * t + at + hi - lo], prod[:, q % 2, u, d, P * t:P * t + P],
                                        w2_s[:, d, lo:hi], start=(d == 0), stop=(d == 1))
                if u == 3:
                    ins.then_inc(tiles_done, 1)

            def chunk0(c, i, q, more):
                contract(c, q, 0)
                repeat(c, q, 2)
                contract(c, q, 1)
                repeat(c, q, 3)
                if more:
                    turn(c + 1, i if q + 1 < RING else i + 1, (q + 1) % RING)
                    repeat(c + 1, q + 1, 0)
                contract(c, q, 2)
                if more:
                    repeat(c + 1, q + 1, 1)
                contract(c, q, 3)

            turn(0, 0, 0)
            repeat(0, 0, 0)
            repeat(0, 0, 1)
            with pe.Fori(0, LOOPS - 1) as i:
                for q in range(RING):
                    chunk0(RING * i + q, i, q, True)
            for q in range(RING):
                chunk0(RING * (LOOPS - 1) + q, LOOPS - 1, q, q + 1 < RING)

            def carry_over(ready):
                pe.wait_ge(ready, 1)
                flat = nt[:].rearrange("p a c -> p (a c)")
                for k in range(2):
                    ins = pe.matmul((po, hp)[k][:, 0:A * C // 2], e_lo[:], flat[:, 400 * k:400 * k + 400], start=True, stop=True)
                ins.then_inc(carried, 1)

            def turn_nodes(first):
                for g in range(GROUPS):
                    pe.wait_ge(nodes_out, first + g - 1) if first + g > 1 else None
                    for a in range(4 * g, min(4 * g + 4, A)):
                        ins = pe.transpose(tp[0:C, g % 2, P * (a - 4 * g):P * (a - 4 * g) + P], hn[:, a, :], ident_s[:])
                    ins.then_inc(nodes_turned, 1)
                pe.wait_ge(nodes_out, first + GROUPS)

            carry_over(last0)
            pe.wait_ge(nodes_in, 1)
            turn_nodes(0)
            pe.wait_ge(vatt_ready, 1)
            for a in range(A):
                ins = pe.matmul(po[:, 16 * a:16 * a + 16], node_t[:, P * a:P * a + P], vatt[:], start=True, stop=True)
            ins.then_inc(att_done, 1)
            for k in range(4):
                pe.wait_ge(ends_in, k + 1)
                pe.transpose(hp[0:HEADS, 0:P], car_l, ident_s[:]).then_inc(ends_turned, 1)
                pe.wait_ge(ends_back, k + 1)
                pe.transpose(hp[:, P:P + HEADS], car_t, ident_s[0:HEADS, 0:HEADS]).then_inc(ends_done, 1)

            pe.wait_ge(attn_out, 32)

            def open1(c, i, q):
                s = q % 2
                pe.wait_ge(turned1_out, c + 1)
                pe.wait_ge(x1_landed[q], 16 * (i + 1))
                for t in range(TC):
                    pe.transpose(tpb[0:S3, s, 0, P * t:P * t + P], xs_ring[:, q, t, 0:S3], identb_s[:])
                pe.wait_ge(at_landed[q], 16 * (i + 1))
                pe.transpose(tpb[0:S3, s, 1, 0:P], xd_ring[:, q, 0, :], identb_s[:]).then_inc(turned1, 1)
                pe.wait_ge(turned1_out, c + 3)
                pe.wait_ge(xrep1_out, c + 1)
                pe.matmul(hp[:], selx_s[:], xt1_s[:, s, 0:CE], start=True, stop=True).then_inc(xrep1, 1)
                pe.wait_ge(prod1_done, c + 1)
                for g in range(2):
                    for t in range(TC):
                        ins = pe.matmul(rep[:, s, g, P * t:P * t + P], sela_s[:, t, g, :], xt1_s[:, s, CE:CE + P], start=True, stop=True)
                ins.then_inc(arep1, 1)

            def close1(c, q):
                pe.wait_ge(prod1_done, c + 3)
                pe.wait_ge(tiles1_out, c + 1)
                for t in range(TC):
                    for g in range(2):
                        ins = pe.matmul(po[:, C * t:C * t + C], prod1[:, q % 2, g, P * t:P * t + P], wst_s[:, g, :],
                                        start=(g == 0), stop=(g == 1))
                ins.then_inc(tiles1_done, 1)

            open1(0, 0, 0)
            with pe.Fori(0, LOOPS - 1) as i:
                for q in range(RING):
                    open1(RING * i + q + 1, i if q + 1 < RING else i + 1, (q + 1) % RING)
                    close1(RING * i + q, q)
            for q in range(RING):
                if q + 1 < RING:
                    open1(RING * (LOOPS - 1) + q + 1, LOOPS - 1, q + 1)
                close1(RING * (LOOPS - 1) + q, q)

            carry_over(last1)
            turn_nodes(GROUPS)
            for g in range(-(-A // 2)):
                if g >= 4:
                    pe.wait_ge(own_used, g - 3)
                for k in range(min(2, A - 2 * g)):
                    a = 2 * g + k
                    ins = pe.matmul(rep[:, g % 4 // 2, g % 2, 256 * k:256 * k + 256], node_t[:, P * a:P * a + P], wgat_s[:],
                                    start=True, stop=True)
                ins.then_inc(own_done, 1)
            pe.wait_ge(own_used, -(-A // 2))
            pe.wait_ge(nodes_in, 2)
            turn_nodes(2 * GROUPS)
            for g in range(GROUPS):
                n = min(CE, NP - CE * g)
                if g >= 2:
                    pe.wait_ge(ffn_out, g - 1)
                pe.matmul(tp[:, g % 2, 0:n], f1_s[:], node_t[:, CE * g:CE * g + n], start=True, stop=True).then_inc(ffn_done, 1)
            pe.wait_ge(ffn_out, GROUPS)
            ff = rep[:, 0, :, :].rearrange("p g e -> p (g e)")
            for a in range(A):
                ins = pe.matmul(ff[:, C * a:C * a + C], hid1_[:, P * a:P * a + P], f2_s[:], start=True, stop=True)
            ins.then_inc(ffn2_done, 1)


def kernel(x, src, dst, edge_attr_10, edge_attr_3, edge_weight, L0_gnn_W1, L0_gnn_W2, L1_gnn_W_gat, L1_gnn_att_src,
           L1_gnn_att_dst, L1_gnn_bias_gat, L1_gnn_w1, L1_gnn_b1, L1_gnn_w2, L1_gnn_b2, L1_gnn_g1, L1_gnn_be1,
           L1_gnn_g2, L1_gnn_be2):
    import ml_dtypes
    import concourse.bacc as bacc
    from concourse.bass_utils import run_bass_kernel_spmd

    arr = np.asarray
    bf = ml_dtypes.bfloat16
    pads = EP - E

    def edge_rows(v, fill, n=pads):
        return np.concatenate([arr(v), np.full((n,) + arr(v).shape[1:], fill, arr(v).dtype)])

    d = np.concatenate([np.array([4000], np.int32), edge_rows(dst, NP - 1), np.array([5000], np.int32)]).astype(np.int32, copy=False)
    dst_ext = np.stack([d[p * J:p * J + J + 2] for p in range(P)])
    emb = edge_rows(edge_attr_10, 0).reshape(P, J, 10)
    w2 = arr(L0_gnn_W2).reshape(K, 7, 2 * U, U)[:, [0, 2, 4, 1, 3, 6, 5]]
    eye = np.eye(P, dtype=np.float32)
    rep_sel = np.zeros((3, C, 4, U, K), bf)
    sel_x = np.zeros((3, C, C, 4), bf)
    sel_attn = np.zeros((TC, 3, HEADS, TC, 2, C, 4), bf)
    for part in range(3):
        for u in range(U):
            rep_sel[part, u, 0, u] = 1
            for k in range(3):
                rep_sel[part, U + 3 * u + k, k + 1, u] = 1
        for c in range(C):
            sel_x[part, c, c] = 1
        for t in range(TC):
            for h in range(HEADS):
                sel_attn[t, part, h, t, h // 4, :, h % 4] = 1
    wg = arr(L1_gnn_W_gat)
    feeds = {
        "x": np.concatenate([arr(x), np.zeros((NP - N, C), np.float32)]),
        "src": edge_rows(src, 0).reshape(P, J),
        "dst_ext": dst_ext,
        "dst_ends": np.ascontiguousarray(dst_ext[:, [1, J, 0, J + 1]].T),
        "emb": np.ascontiguousarray(emb.transpose(2, 1, 0)).reshape(10, EP),
        "vec": np.ascontiguousarray(edge_rows(edge_attr_3, 1).reshape(P, J, 3).transpose(0, 2, 1)),
        "weight": edge_rows(edge_weight, 0).reshape(P, J),
        "w1rep": np.tile(arr(L0_gnn_W1), (1, U)),
        "w2r": np.ascontiguousarray(w2.transpose(2, 0, 1, 3).reshape(2, P, 56).transpose(1, 0, 2)),
        "rep_sel": rep_sel.reshape(S3, 4, P),
        "ident": eye, "identb": eye.astype(bf), "tri": np.triu(np.ones((P, P), np.float32)),
        "iota_b": np.tile(np.arange(P), (P, 1)).astype(bf),
        "w_gat": wg,
        "w_stack": np.ascontiguousarray(wg.reshape(C, 2, 4, C).transpose(0, 2, 1, 3)).reshape(P, 2, C),
        "att": np.stack([arr(L1_gnn_att_src).reshape(-1), arr(L1_gnn_att_dst).reshape(-1)]),
        "sel_x": sel_x.reshape(S3, P), "sel_attn": sel_attn.reshape(S3, TC, 2, P),
        "ffn1": arr(L1_gnn_w1), "ffn2": arr(L1_gnn_w2),
        "rows": np.stack([arr(v) for v in (L1_gnn_bias_gat, L1_gnn_b2, L1_gnn_g1, L1_gnn_be1, L1_gnn_g2, L1_gnn_be2)]),
        "b1": arr(L1_gnn_b1).reshape(P, 1),
    }
    feeds = {k: np.ascontiguousarray(v) for k, v in feeds.items()}
    nc = bacc.Bacc("TRN2", target_bir_lowering=False, num_devices=1)
    args = [nc.dram_tensor(k, v.shape, mybir.dt.from_np(v.dtype), kind="ExternalInput").ap() for k, v in feeds.items()]
    out = nc.dram_tensor("out", (N, C), F32, kind="ExternalOutput").ap()
    tensor_network(nc, *args, out)
    return run_bass_kernel_spmd(nc, [feeds], core_ids=[0]).results[0]["out"]
```

```python
from contextlib import ExitStack

import numpy as np
import concourse.bass as bass
from concourse import mybir

F32 = mybir.dt.float32
I32 = mybir.dt.int32
BF16 = mybir.dt.bfloat16
ALU = mybir.AluOpType
ACT = mybir.ActivationFunctionType
AX = mybir.AxisListType

N, E, C = 3125, 53125, 32
P = 128
A = -(-N // P)
NP = A * P
J = 416
EP = P * J
S3 = 3 * C
HEADS = 8
K = 16
U = 8
TC = 4
CE = TC * P
NCH = J // TC
RING = 4
PT = 2 * TC
ROW1 = S3 + 2 * HEADS
LN_EPS = 1e-5
TANH_GAIN = 1.593
PW_S = 0.17677669529663687
PW_V = 0.25
BIG = 1e30
NOWHERE = 1e6


def tensor_network(nc, x, src, dst_ext, dst_ends, emb, vec, weight, w1rep, w2r, rep_sel, ident, identb, tri,
                   iota_b, w_gat, w_stack, att, sel_x, sel_attn, ffn1, ffn2, rows, b1, out):
    dram = lambda name, shape, dt: nc.dram_tensor(name, shape, dt, kind="Internal").ap()
    src_table0 = dram("src_table0", (NP, S3), BF16)
    node_table0 = dram("node_table0", (NP, C), F32)
    at_starts0 = dram("at_starts0", (EP, C), F32)
    dst_parts0 = dram("dst_parts0", (EP, S3), BF16)
    sums0 = dram("sums0", (EP, C), F32)
    src_table1 = dram("src_table1", (NP, ROW1 // 2), F32)
    node_table1 = dram("node_table1", (NP, 2 * HEADS), F32)
    at_starts1 = dram("at_starts1", (EP, 2 * HEADS), F32)
    attn_parts = dram("attn_parts", (EP, 3 * HEADS), BF16)
    sums1 = dram("sums1", (EP, C + HEADS), F32)

    nodes_of = lambda t: t.rearrange("(a b) c -> b a c", b=P)
    edges_of = lambda t: t.rearrange("(p j) c -> p j c", p=P)

    with ExitStack() as ctx:
        sb = lambda name, shape, dt=F32: ctx.enter_context(nc.sbuf_tensor(name, shape, dt))
        psum = lambda name, shape, dt=F32: ctx.enter_context(nc.psum_tensor(name, shape, dt))
        sem = lambda name: ctx.enter_context(nc.semaphore(name))

        area_a = sb("area_a", [P, J * C])
        area_b = sb("area_b", [P, J * ROW1 // 2])
        area_e = sb("area_e", [P, 2 * J * HEADS])
        a3 = area_a[:].rearrange("p (j c) -> p j c", c=C)
        b_parts = area_b[:, 0:J * S3 // 2].bitcast(BF16).rearrange("p (j c) -> p j c", c=S3)

        def views(area, sizes, start=0):
            got, at = [], start
            for s in sizes:
                got.append(area[:, at:at + s])
                at += s
            return got

        pr_, xt_, hid_, emb_, g_, tmp_, acc_, v_, sg_, sgn_, fm_, w2w_ = views(
            area_b, [2 * 8 * CE, 2 * CE, 2 * CE, RING * CE, 16 * P, PT * 72, PT * 24, PT * 24, PT * 16, PT * 8, 2 * CE, 8 * P])
        prod = pr_.rearrange("p (s u d e) -> p s u d e", s=2, u=4, d=2)
        x_t = xt_.bitcast(BF16).rearrange("p (s d e) -> p s d e", s=2, d=2)
        hid = hid_.rearrange("p (s e) -> p s e", s=2)
        emb_ring = emb_.rearrange("p (s e) -> p s e", s=RING)
        tp_out = g_.rearrange("p (t c) -> p t c", c=P)
        tmp = tmp_.rearrange("p (t i w) -> p t i w", t=PT, i=3)
        acc = acc_.rearrange("p (t w) -> p t w", t=PT)
        vbuf = v_.rearrange("p (t k w) -> p t k w", t=PT, k=3)
        sg = sg_.rearrange("p (t w) -> p t w", t=PT)
        sgn = sgn_.rearrange("p (t w) -> p t w", t=PT)
        by_feature = fm_.rearrange("p (s e) -> p s e", s=2)
        w2_wide = w2w_.rearrange("p (u d n) -> p u d n", u=4, d=2)
        oh_hi_, oh_lo_, iota_x_ = views(area_b, [A * J // 2, 2 * P * 8, P * 8])
        oh_hi = oh_hi_.bitcast(BF16).rearrange("p (a j) -> p a j", a=A)
        oh_lo = oh_lo_.bitcast(BF16).rearrange("p (s b t) -> p s b t", s=2, b=P)
        iota_x = iota_x_.bitcast(BF16).rearrange("p (b t) -> p b t", b=P)
        hid1_, xself_ = views(area_b, [NP, A * 256])
        node_t = area_b[0:C, 9600:9600 + NP]
        xself = xself_.rearrange("p (a h c) -> p a h c", a=A, h=HEADS)
        vec_, wt_, r_, dlo_, dhi_, dbf_ = views(area_e, [3 * J, J, J, J, J, J])
        nvec = vec_.rearrange("p (i j) -> p i j", i=3)
        lo_i, hi_i = dlo_.bitcast(I32), dhi_.bitcast(I32)
        lo_bf, hi_bf = views(dbf_.bitcast(BF16), [J, J])
        gath1 = area_b[:].rearrange("p (j c) -> p j c", c=ROW1 // 2)
        h8 = lambda v: v.rearrange("p (j h) -> p j h", h=HEADS)
        alpha, self1 = map(h8, views(area_e, [J * HEADS] * 2))
        d16_, seg_, tmp8_ = views(area_a, [2 * J * HEADS, J * HEADS, J * HEADS])
        d16 = d16_.rearrange("p (j c) -> p j c", c=2 * HEADS)
        seg, tmp8 = h8(seg_), h8(tmp8_)
        apart = d16_[:, 0:J * 12].bitcast(BF16).rearrange("p (j c) -> p j c", c=3 * HEADS)
        pr1_, xrep_, xt1_, fm1_, ww1_ = views(area_e, [2 * 2 * CE, 2 * CE, CE + P, CE, RING * 2 * P])
        wst_wide = ww1_.rearrange("p (q g n) -> p q g n", q=RING, g=2)
        xt1_s = xt1_[0:S3, :].bitcast(BF16).rearrange("p (s e) -> p s e", s=2)
        prod1 = pr1_.rearrange("p (s g e) -> p s g e", s=2, g=2)
        xrep = xrep_.rearrange("p (s e) -> p s e", s=2)

        asrc_e = area_b[:].rearrange("p (j c) -> p j c", c=ROW1 // 2)[:, :, S3 // 2:ROW1 // 2]
        split_, att_, dnode_, tri_s, iota_, sel_, ends_ = views(
            area_b, [A * ROW1 // 2, 4 * P, A * 2 * HEADS, P, P // 2, 2 * P, 4 * P], J * S3 // 2)
        hsplit = split_.bitcast(BF16).rearrange("p (a c) -> p a c", a=A)
        att_s = att_[0:C, :].rearrange("p (k n) -> p k n", k=2)
        dnode = dnode_.rearrange("p (a c) -> p a c", a=A)
        iota_s = iota_.bitcast(BF16)
        sel_s = sel_[0:S3, :].bitcast(BF16).rearrange("p (u n) -> p u n", u=4)
        ends_s = ends_[0:HEADS, :].bitcast(I32).rearrange("p (k n) -> p k n", k=4)
        ident_s, identb_s = sb("ident_s", [P, P]), sb("identb_s", [P, P], BF16)
        ones_s = sb("ones_s", [P, P])
        w1_s, w2_s = sb("w1_s", [10, P]), sb("w2_s", [P, 2, 56])
        wgat_s = sb("wgat_s", [C, 2 * P])
        wst_s = sb("wst_s", [P, 2, C])
        selx_s, sela_s = sb("selx_s", [S3, P], BF16), sb("sela_s", [S3, TC, 2, P], BF16)
        f1_s, f2_s, b1_s, rows_s = sb("f1_s", [C, P]), sb("f2_s", [P, C]), sb("b1_s", [P, 1]), sb("rows_s", [P, 6, C])
        bias_g, b2_r, g1_r, be1_r, g2_r, be2_r = (rows_s[:, i, :] for i in range(6))
        src_s, dst_s = sb("src_s", [P, J], I32), sb("dst_s", [P, J + 2], I32)
        eps_s = sb("eps_s", [P, 1])
        same_prev, same_next = sb("same_prev", [P, J]), sb("same_next", [P, J])
        pen = sb("pen", [P, J])
        idx_ring = sb("idx_ring", [P, 2, 16], I32)
        xs_words = sb("xs_words", [P, RING, TC, ROW1 // 2])
        xs_ring = xs_words[:].bitcast(BF16)
        xd_area = sb("xd_area", [P, RING * TC * S3 // 2])
        xd_ring = xd_area[:].bitcast(BF16).rearrange("p (q t c) -> p q t c", q=RING, t=TC)
        flags_, car_t_, car_l = views(xd_area[:], [4 * P, P, HEADS])
        flags = flags_[0:HEADS, :].rearrange("p (k n) -> p k n", k=4)
        car_t = car_t_[0:HEADS, :]
        node = lambda name: sb(name, [P, A, C])
        xn, hn, nt, agg = node("xn"), node("hn"), node("nt"), sb("agg", [P, A, C + HEADS])
        hsp = hsplit[:, :, 0:S3]
        asrc_n = hsplit[:, :, S3:ROW1].bitcast(F32)
        st = sb("st", [P, 4, A])
        hist, start_i, end_i = sb("hist", [P, A]), sb("start_i", [P, A], I32), sb("end_i", [P, A], I32)
        e_lo, e_hi = sb("e_lo", [P, P]), sb("e_hi", [P, A])
        carry_in, last = sb("carry_in", [P, C]), sb("last", [P, C])
        endf = sb("endf", [P, 4])
        zerob = sb("zerob", [P, P], BF16)
        vatt = sb("vatt", [C, 16])

        rep = psum("rep", [P, 2, 2, CE])
        tp = psum("tp", [P, 2, CE])
        hp = psum("hp", [P, CE])
        po = psum("po", [P, CE])
        tpb = tp[:].bitcast(BF16).rearrange("p s (d e) -> p s d e", d=2)
        po2 = (po[:], tp[:, 1, :])

        consts, x_in, dst_in = sem("consts"), sem("x_in"), sem("dst_in")
        zero_set, zeroed = sem("zero_set"), sem("zeroed")
        dve_step, act_step, pool_step = sem("dve_step"), sem("act_step"), sem("pool_step")
        var_ready, root_ready = sem("var_ready"), sem("root_ready")
        table0_ready, tables0, wide_ready = sem("table0_ready"), sem("tables0"), sem("wide_ready")
        onehot_ready, onehot_used, hist_done = sem("onehot_ready"), sem("onehot_used"), sem("hist_done")
        hist_copied, cum_done, bounds_ready = sem("hist_copied"), sem("cum_done"), sem("bounds_ready")
        carry0, scattered0, starts0 = sem("carry0"), sem("scattered0"), sem("starts0")
        spread_ready, hi_cast, r1_done, mid_cast = sem("spread_ready"), sem("hi_cast"), sem("r1_done"), sem("mid_cast")
        parts_ready, parts_out = sem("parts_ready"), sem("parts_out")
        idx_copied = [sem(f"idx_copied{i}") for i in range(2)]
        idx_used = [sem(f"idx_used{i}") for i in range(2)]
        src_landed = [sem(f"src_landed{q}") for q in range(RING)]
        dst_landed = [sem(f"dst_landed{q}") for q in range(RING)]
        emb_landed = [sem(f"emb_landed{q}") for q in range(RING)]
        turned, hidden_done = sem("turned"), sem("hidden_done")
        turned_out, hidden_ready = sem("turned_out"), sem("hidden_ready")
        rep_ready, prod_done, tiles_done, tiles_out, post_read = (
            sem("rep_ready"), sem("prod_done"), sem("tiles_done"), sem("tiles_out"), sem("post_read"))
        features_out, tiles_back = sem("features_out"), sem("tiles_back")
        features1_out, tiles1_back = sem("features1_out"), sem("tiles1_back")
        gates_in, gates_out = sem("gates_in"), sem("gates_out")
        sums0_ready, sums0_out, ended0, last0 = sem("sums0_ready"), sem("sums0_out"), sem("ended0"), sem("last0")
        carried, flags_ready = sem("carried"), sem("flags_ready")
        nodes_in, nodes_turned, nodes_out = sem("nodes_in"), sem("nodes_turned"), sem("nodes_out")
        vatt_ready, att_done, table1_ready, tables1 = (
            sem("vatt_ready"), sem("att_done"), sem("table1_ready"), sem("tables1"))
        carry1, scattered1, starts1 = sem("carry1"), sem("scattered1"), sem("starts1")
        src1_landed = [sem(f"src1_landed{q}") for q in range(RING)]
        src1_kept = [sem(f"src1_kept{q}") for q in range(RING)]
        ends_in, ends_turned, ends_back, ends_done = (
            sem("ends_in"), sem("ends_turned"), sem("ends_back"), sem("ends_done"))
        exp_in, exp_out = sem("exp_in"), sem("exp_out")
        attn_ready, attn_out = sem("attn_ready"), sem("attn_out")
        x1_landed = [sem(f"x1_landed{q}") for q in range(RING)]
        at_landed = [sem(f"at_landed{q}") for q in range(RING)]
        turned1, turned1_out, xrep1, xrep1_out = sem("turned1"), sem("turned1_out"), sem("xrep1"), sem("xrep1_out")
        arep1, prod1_done, tiles1_done, tiles1_out = (
            sem("arep1"), sem("prod1_done"), sem("tiles1_done"), sem("tiles1_out"))
        sums1_ready, sums1_out, ended1, last1, agg_set = (
            sem("sums1_ready"), sem("sums1_out"), sem("ended1"), sem("last1"), sem("agg_set"))
        own_done, own_used, ffn_done, ffn_out, ffn2_done = (
            sem("own_done"), sem("own_used"), sem("ffn_done"), sem("ffn_out"), sem("ffn2_done"))
        result, written = sem("result"), sem("written")

        constants = [(ident_s, ident), (identb_s, identb), (tri_s, tri), (iota_s, iota_b), (sel_s, rep_sel),
                     (w1_s, w1rep), (w2_s, w2r), (wgat_s, w_gat), (wst_s, w_stack), (selx_s, sel_x),
                     (sela_s, sel_attn), (f1_s, ffn1), (f2_s, ffn2), (b1_s, b1),
                     (rows_s, rows.partition_broadcast(P)), (att_s, att.partition_broadcast(C)),
                     (ends_s, dst_ends.partition_broadcast(HEADS)), (src_s, src), (nvec, vec), (wt_, weight)]
        CONSTS = 16 * len(constants)
        QUARTERS = 4
        JQ = J // QUARTERS
        GROUPS = -(-NP // CE)
        GROUP_STEPS = 12
        LOOPS = J // 16

        def hold(eng, semaphore, value):
            eng.wait_ge(semaphore, value)
            eng.wait_ge(consts, CONSTS)

        def hold_pool(pool, semaphore, value):
            pool.wait_ge(semaphore, value)
            pool.sem_inc(pool_step, 1)

        class Steps:

            def __init__(self, eng, semaphore):
                self.eng, self.sem, self.count, self.offset = eng, semaphore, 0, 0

            def __call__(self, instruction):
                instruction.then_inc(self.sem, 1)
                self.count += 1
                self.eng.wait_ge(self.sem, self.offset + self.count)

        block = ctx.enter_context(nc.Block())

        @block.sync
        def _(sp):
            for q in range(RING):
                sp.sem_inc(src1_kept[q], 16)
            sp.dma_start(dst_s[:], dst_ext).then_inc(dst_in, 16)
            sp.dma_start(xn[:], nodes_of(x)).then_inc(x_in, 16)
            for to, of in constants:
                sp.dma_start(to[:] if not isinstance(to, bass.AP) else to, of).then_inc(consts, 16)
            sp.wait_ge(zero_set, 1)
            sp.dma_start(edges_of(at_starts0), a3).then_inc(zeroed, 16)
            sp.dma_start(edges_of(at_starts1), area_a[:, 0:J * 16].rearrange("p (j c) -> p j c", c=16)).then_inc(zeroed, 16)
            sp.wait_ge(table0_ready, 1)
            sp.dma_start(nodes_of(node_table0), hn[:]).then_inc(tables0, 16)
            sp.dma_start(nodes_of(src_table0), hsp).then_inc(tables0, 16)
            sp.wait_ge(scattered0, 16 * A)
            sp.dma_start(a3, edges_of(at_starts0)).then_inc(starts0, 16)
            for q in range(QUARTERS):
                sp.wait_ge(parts_ready, q + 1)
                sp.dma_start(edges_of(dst_parts0)[:, q * JQ:(q + 1) * JQ, :],
                             b_parts[:, q * JQ:(q + 1) * JQ, :]).then_inc(parts_out, 16)
            sp.wait_ge(parts_out, 16 * QUARTERS)
            with sp.Fori(0, LOOPS) as i:
                for q in range(RING):
                    hold(sp, turned, RING * i + q + 1)
                    sp.dma_start(xd_ring[:, q, :, :], edges_of(dst_parts0)[:, bass.ds(16 * i + TC * q, TC), :]).then_inc(dst_landed[q], 16)
                    hold(sp, hidden_done, RING * i + q + 1)
                    sp.dma_start(emb_ring[0:10, q, :], emb[:, bass.ds((RING * i + q) * CE, CE)]).then_inc(emb_landed[q], 16)
            sp.wait_ge(sums0_ready, 1)
            sp.dma_start(edges_of(sums0), a3).then_inc(sums0_out, 16)
            sp.wait_ge(table1_ready, 1)
            sp.dma_start(nodes_of(node_table1), dnode).then_inc(tables1, 16)
            sp.dma_start(nodes_of(src_table1), split_.rearrange("p (a c) -> p a c", a=A)).then_inc(tables1, 16)
            sp.wait_ge(scattered1, 16 * A)
            sp.wait_ge(sums0_out, 16)
            sp.dma_start(d16, edges_of(at_starts1)).then_inc(starts1, 16)
            sp.wait_ge(flags_ready, 1)
            with sp.Fori(0, LOOPS) as i:
                for q in range(RING):
                    hold(sp, src1_landed[q], 16 * TC * (i + 1))
                    sp.dma_start(gath1[:, bass.ds(16 * i + TC * q, TC), :], xs_words[:, q, :, :]).then_inc(src1_kept[q], 16)
            sp.wait_ge(attn_ready, 1)
            sp.dma_start(edges_of(attn_parts), apart).then_inc(attn_out, 16)
            sp.dma_start(edges_of(sums1)[:, :, C:C + HEADS], self1).then_inc(attn_out, 16)
            sp.wait_ge(attn_out, 32)
            with sp.Fori(0, LOOPS) as i:
                for q in range(RING):
                    hold(sp, turned1, RING * i + q + 1)
                    sp.dma_start(xs_words[:, q, :, 0:S3 // 2], gath1[:, bass.ds(16 * i + TC * q, TC), 0:S3 // 2]).then_inc(x1_landed[q], 16)
                    sp.dma_start(xd_ring[:, q, 0, :], edges_of(attn_parts)[:, bass.ds(16 * i + TC * q, TC), :].rearrange("p t c -> p (t c)")).then_inc(at_landed[q], 16)
            sp.wait_ge(sums1_ready, 1)
            sp.dma_start(edges_of(sums1)[:, :, 0:C], a3).then_inc(sums1_out, 16)
            sp.wait_ge(result, 1)
            full = N // P
            sp.dma_start(out[0:full * P, :].rearrange("(a b) c -> b a c", b=P), hn[:, 0:full, :]).then_inc(written, 16)
            sp.dma_start(out[full * P:N, :], hn[0:N - full * P, full, :]).then_inc(written, 16)
            sp.wait_ge(written, 32)

        @block.gpsimd
        def _(pool):
            pool.memset(area_a[:], 0.0).then_inc(zero_set, 1)

            def gather_row(to, table, index, last_row, semaphore):
                pool.indirect_dma_start(to, None, table, bass.IndirectOffsetOnAxis(ap=index, axis=0),
                                        bounds_check=last_row, oob_is_err=False).then_inc(semaphore, 16)

            def gather_sources(table, ring, landed, first):
                with pool.Fori(0, LOOPS // 2) as i:
                    for half in range(2):
                        if first:
                            hold_pool(pool, turned, 2 * RING * i + RING * half + 1)
                        else:
                            hold_pool(pool, src1_kept[0], 16 * (2 * i + half) + 16)
                        pool.tensor_copy(idx_ring[:, half, :], src_s[:, bass.ds(32 * i + 16 * half, 16)]).then_inc(idx_copied[half], 1)
                        hold_pool(pool, idx_copied[half], i + 1 + (0 if first else LOOPS // 2))
                        for q in range(RING):
                            c = 2 * RING * i + RING * half + q
                            if first:
                                hold_pool(pool, turned, c + 1)
                            else:
                                hold_pool(pool, src1_kept[q], 16 * (2 * i + half) + 16)
                            for t in range(TC):
                                gather_row(ring[:, q, t, :], table, idx_ring[:, half, TC * q + t:TC * q + t + 1],
                                           NP - 1, landed[q])

            pool.wait_ge(tables0, 32)
            gather_row(carry_in[:], node_table0, dst_s[:, 0:1], NP - 1, carry0)
            pool.wait_ge(bounds_ready, 1)
            pool.wait_ge(zeroed, 32)
            for a in range(A):
                pool.indirect_dma_start(at_starts0, bass.IndirectOffsetOnAxis(ap=start_i[:, a:a + 1], axis=0), hn[:, a, :],
                                        None, bounds_check=EP - 1, oob_is_err=False).then_inc(scattered0, 16)
            pool.wait_ge(consts, CONSTS)
            gather_sources(src_table0, xs_ring[:, :, :, 0:S3], src_landed, True)
            pool.wait_ge(sums0_out, 16)
            pool.wait_ge(agg_set, 1)
            for a in range(A):
                gather_row(agg[:, a, 0:C], sums0, end_i[:, a:a + 1], EP - 1, ended0)
            pool.wait_ge(tables1, 32)
            gather_row(carry_in[:, 0:16], node_table1, dst_s[:, 0:1], NP - 1, carry1)
            for a in range(A):
                pool.indirect_dma_start(at_starts1, bass.IndirectOffsetOnAxis(ap=start_i[:, a:a + 1], axis=0), dnode[:, a, :],
                                        None, bounds_check=EP - 1, oob_is_err=False).then_inc(scattered1, 16)
            gather_sources(src_table1, xs_words, src1_landed, False)
            pool.wait_ge(sums1_out, 16)
            pool.wait_ge(attn_out, 32)
            pool.wait_ge(agg_set, 2)
            for a in range(A):
                gather_row(agg[:, a, :], sums1, end_i[:, a:a + 1], EP - 1, ended1)

        @block.vector
        def _(dve):
            step = Steps(dve, dve_step)
            roots = [0]
            across = lambda v, n=C: v.unsqueeze(2).to_broadcast([P, A, n])
            row = lambda v: v.unsqueeze(1).to_broadcast([P, A, C])

            def root():
                roots[0] += 1
                dve.wait_ge(root_ready, roots[0])

            def layer_norm(to, of, scratch):
                step(dve.reduce_sum(st[:, 0, :], of, AX.X))
                step(dve.tensor_scalar(st[:, 0, :], st[:, 0, :], -1.0 / C, None, ALU.mult))
                step(dve.tensor_tensor(scratch, of, across(st[:, 0, :]), ALU.add))
                step(dve.tensor_tensor(to, scratch, scratch, ALU.mult))
                dve.reduce_sum(st[:, 1, :], to, AX.X).then_inc(var_ready, 1)
                root()
                step(dve.reciprocal(st[:, 3, :], st[:, 2, :]))
                step(dve.tensor_tensor(to, scratch, across(st[:, 3, :]), ALU.mult))

            def split(parts, of, scratch):
                step(dve.tensor_copy(parts[0], of))
                step(dve.tensor_tensor(scratch, of, parts[0], ALU.subtract))
                step(dve.tensor_copy(parts[1], scratch))
                step(dve.tensor_tensor(scratch, scratch, parts[1], ALU.subtract))
                return dve.tensor_copy(parts[2], scratch)

            three = lambda v: [v[:, :, C * k:C * (k + 1)] for k in range(3)]

            step(dve.memset(eps_s[:], LN_EPS))
            step(dve.memset(ones_s[:], 1.0))
            step(dve.memset(zerob[:], 0.0))
            step(dve.memset(carry_in[:], 0.0))
            dve.memset(agg[:], 0.0).then_inc(agg_set, 1)

            dve.wait_ge(x_in, 16)
            layer_norm(hn[:], xn[:], nt[:])
            step(dve.tensor_scalar(hn[:], hn[:], 0.0, None, ALU.max))
            split(three(hsp), hn[:], nt[:]).then_inc(table0_ready, 1)

            dve.wait_ge(dst_in, 16)
            target = dst_s[:, 1:J + 1]
            dve.wait_ge(consts, CONSTS)
            step(dve.tensor_tensor(same_prev[:], target, dst_s[:, 0:J], ALU.is_equal))
            step(dve.tensor_tensor(same_next[:], target, dst_s[:, 2:J + 2], ALU.is_equal))
            step(dve.tensor_scalar(lo_i, target, P - 1, None, ALU.bitwise_and))
            step(dve.tensor_scalar(hi_i, target, P.bit_length() - 1, None, ALU.logical_shift_right))
            step(dve.tensor_copy(lo_bf, lo_i))
            step(dve.tensor_copy(hi_bf, hi_i))
            step(dve.tensor_copy(endf[:, 0:1], lo_i[:, J - 1:J]))
            step(dve.tensor_copy(endf[:, 1:2], hi_i[:, J - 1:J]))
            step(dve.tensor_copy(iota_x, iota_s.unsqueeze(2).to_broadcast([P, P, 16])))
            for a in range(A):
                ins = dve.tensor_scalar(oh_hi[:, a, :], hi_bf, float(a), None, ALU.is_equal)
                if a == A - 1:
                    step(ins)
            with dve.Fori(0, LOOPS // 2) as i:
                for half in range(2):
                    dve.wait_ge(onehot_used, 2 * i + half + 1)
                    dve.tensor_tensor(oh_lo[:, half, :, :], iota_x,
                                      lo_bf[:, bass.ds(32 * i + 16 * half, 16)].unsqueeze(1).to_broadcast([P, P, 16]),
                                      ALU.is_equal).then_inc(onehot_ready, 1)
            step(dve.tensor_scalar(e_lo[:], iota_s, endf[:, 0:1], same_next[:, J - 1:J], ALU.is_equal, ALU.mult))
            step(dve.tensor_scalar(e_hi[:], iota_s[:, 0:A], endf[:, 1:2], None, ALU.is_equal))

            dve.wait_ge(hist_done, 1)
            dve.tensor_copy(hist[:], po[:, 0:A]).then_inc(hist_copied, 1)
            dve.wait_ge(hist_copied, 1)
            dve.wait_ge(cum_done, 1)
            step(dve.tensor_tensor_scan(st[:, 0, :], ones_s[:, 0:A], hp[:, 32:32 + A], 0.0, ALU.mult, ALU.add))
            step(dve.tensor_tensor(st[:, 0, :], st[:, 0, :], hp[:, 32:32 + A], ALU.subtract))
            step(dve.tensor_tensor(st[:, 0, :], st[:, 0, :], hp[:, 0:A], ALU.add))
            step(dve.tensor_scalar(st[:, 1, :], hist[:], 0.0, NOWHERE, ALU.is_equal, ALU.mult))
            step(dve.tensor_tensor(st[:, 2, :], st[:, 0, :], hist[:], ALU.subtract))
            step(dve.tensor_tensor(start_i[:], st[:, 2, :], st[:, 1, :], ALU.add))
            dve.scalar_tensor_tensor(out=end_i[:], in0=st[:, 0, :], scalar=-1.0, in1=st[:, 1, :],
                                     op0=ALU.add, op1=ALU.add).then_inc(bounds_ready, 1)
            dve.wait_ge(bounds_ready, 1)

            step(dve.tensor_tensor(r_, nvec[:, 0, :], nvec[:, 0, :], ALU.mult))
            for k in (1, 2):
                step(dve.tensor_tensor(dlo_, nvec[:, k, :], nvec[:, k, :], ALU.mult))
                ins = dve.tensor_tensor(r_, r_, dlo_, ALU.add)
                if k == 1:
                    step(ins)
            ins.then_inc(var_ready, 1)
            root()
            step(dve.reciprocal(dlo_, r_))
            step(dve.tensor_tensor(nvec, nvec, dlo_.unsqueeze(1).to_broadcast([P, 3, J]), ALU.mult))
            step(dve.tensor_scalar(wt_, wt_, TANH_GAIN, None, ALU.mult))
            step(dve.tensor_scalar(w2_s[:, :, 48:56], w2_s[:, :, 48:56], PW_V / 3 ** 0.5, None, ALU.mult))
            step(dve.scalar_tensor_tensor(out=w2_s[:, :, 48:56], in0=w2_s[:, :, 40:48], scalar=-PW_V / 6 ** 0.5,
                                          in1=w2_s[:, :, 48:56], op0=ALU.mult, op1=ALU.add))
            step(dve.tensor_scalar(w2_s[:, :, 40:48], w2_s[:, :, 40:48], PW_V * 1.5 ** 0.5, None, ALU.mult))
            step(dve.tensor_scalar(w2_s[:, :, 16:24], w2_s[:, :, 16:24], PW_V, None, ALU.mult))
            step(dve.tensor_scalar(wst_s[:], wst_s[:], 1.0 / HEADS, None, ALU.mult))

            dve.wait_ge(starts0, 16)
            dve.wait_ge(carry0, 16)
            for c in range(C):
                ins = dve.tensor_tensor_scan(a3[:, :, c], same_prev[:], a3[:, :, c], carry_in[:, c:c + 1], ALU.mult, ALU.add)
            ins.then_inc(spread_ready, 1)
            dve.wait_ge(spread_ready, 1)
            quarter = lambda v, q: v[:, q * JQ:(q + 1) * JQ, :]
            for q in range(QUARTERS + 1):
                if q < QUARTERS:
                    dve.wait_ge(hi_cast, q + 1)
                    dve.tensor_tensor(quarter(a3, q), quarter(a3, q), quarter(b_parts, q)[:, :, 0:C], ALU.subtract).then_inc(r1_done, 1)
                if q > 0:
                    dve.wait_ge(mid_cast, q)
                    dve.tensor_tensor(quarter(b_parts, q - 1)[:, :, 2 * C:S3], quarter(a3, q - 1),
                                      quarter(b_parts, q - 1)[:, :, C:2 * C], ALU.subtract).then_inc(parts_ready, 1)
            dve.wait_ge(parts_out, 16 * QUARTERS)

            step(dve.memset(w2_wide, 0.0))
            for u in range(4):
                lo, hi = (0, 24) if u == 0 else (24, 56)
                ins = dve.tensor_copy(w2_wide[:, u, :, 32 * u:32 * u + hi - lo], w2_s[:, :, lo:hi])
            ins.then_inc(wide_ready, 1)

            def products(c, q, after):
                dve.wait_ge(hidden_ready, c + 2)
                dve.wait_ge(tiles_done, c + 1)
                for u in range(4):
                    dve.wait_ge(rep_ready, 4 * c + u + 1)
                    dve.tensor_tensor(prod[:, q % 2, u, :, :], rep[:, u % 2, :, :],
                                      hid[:, q % 2, :].unsqueeze(1).to_broadcast([P, 2, CE]), ALU.mult).then_inc(prod_done, 1)
                    if u in after:
                        after[u]()

            def pair(g, half):
                tiles = bass.ds(PT * g, PT)
                of = tp_out[:, PT * half:PT * half + PT, :]
                vect = of[:, :, 32:128].rearrange("p t (i w) -> p t i w", i=3)
                n_t = nvec[:, :, tiles].rearrange("p i t -> p t i").unsqueeze(3)
                w_t = wt_[:, tiles].unsqueeze(2)

                def along():
                    dve.wait_ge(tiles_out, 2 * g + 5)
                    step(dve.tensor_tensor(tmp, vect[:, :, :, 0:24], n_t.to_broadcast([P, PT, 3, 24]), ALU.mult))

                def sums():
                    step(dve.tensor_tensor(acc, of[:, :, 0:24], tmp[:, :, 0, :], ALU.add))
                    step(dve.tensor_tensor(acc, acc, tmp[:, :, 1, :], ALU.add))
                    dve.tensor_tensor(acc, acc, tmp[:, :, 2, :], ALU.add).then_inc(gates_in, 1)

                def vectors():
                    dve.wait_ge(gates_in, g + 1)
                    step(dve.tensor_tensor(vbuf, n_t.to_broadcast([P, PT, 3, 8]),
                                           acc[:, :, 16:24].unsqueeze(2).to_broadcast([P, PT, 3, 8]), ALU.mult))
                    dve.tensor_tensor(vbuf, vbuf, vect[:, :, :, 24:32], ALU.add).then_inc(post_read, 1)

                def messages():
                    dve.wait_ge(gates_out, g + 1)
                    step(dve.tensor_tensor(sgn, sg[:, :, 8:16], w_t.to_broadcast([P, PT, 8]), ALU.mult))
                    dve.wait_ge(post_read, g + 3)
                    dve.tensor_tensor(a3[:, tiles, 0:8], sg[:, :, 0:8], w_t.to_broadcast([P, PT, 8]), ALU.mult)
                    step(dve.tensor_tensor(a3[:, tiles, 8:32].rearrange("p t (w k) -> p t k w", k=3), vbuf,
                                           sgn.unsqueeze(2).to_broadcast([P, PT, 3, 8]), ALU.mult))

                return along, sums, vectors, messages

            def group(i, first):
                if not first:
                    before2, before1 = pair(2 * i - 2, 0), pair(2 * i - 1, 1)
                own = pair(2 * i, 0)
                products(RING * i, 0, {} if first else {1: before2[3]})
                products(RING * i + 1, 1, {} if first else dict(enumerate(before1[:3])))
                products(RING * i + 2, 2, {} if first else {1: before1[3]})
                products(RING * i + 3, 3, dict(enumerate(own[:3])))

            group(0, True)
            base = step.count
            with dve.Fori(1, LOOPS) as i:
                step.offset, step.count = (i - 1) * GROUP_STEPS, base
                group(i, False)
                assert step.count - base == GROUP_STEPS
            step.offset, step.count = 0, base + GROUP_STEPS * (LOOPS - 1)
            pair(2 * LOOPS - 2, 0)[3]()
            for piece in pair(2 * LOOPS - 1, 1):
                piece()

            def sum_edges(ready, last_ready):
                for c in range(C):
                    ins = dve.tensor_tensor_scan(a3[:, :, c], same_prev[:], a3[:, :, c], 0.0, ALU.mult, ALU.add)
                ins.then_inc(ready, 1)
                dve.wait_ge(ready, 1)
                step(dve.tensor_copy(last[:], a3[:, J - 1, :]))
                dve.tensor_tensor(nt[:], last[:].unsqueeze(1).to_broadcast([P, A, C]), across(e_hi[:]), ALU.mult).then_inc(last_ready, 1)


            def add_carried(to, n):
                dve.wait_ge(carried, n)
                for k in range(2):
                    half = to.rearrange("p a c -> p (a c)")[:, A * C // 2 * k:A * C // 2 * (k + 1)]
                    ins = dve.tensor_tensor(half, half, (po, hp)[k][:, 0:A * C // 2], ALU.add)
                step(ins)

            sum_edges(sums0_ready, last0)
            add_carried(xn[:], 1)
            dve.wait_ge(ended0, 16 * A)
            step(dve.tensor_tensor(xn[:], xn[:], agg[:, :, 0:C], ALU.add))

            layer_norm(hn[:], xn[:], nt[:])
            dve.tensor_scalar(hn[:], hn[:], 0.0, None, ALU.max).then_inc(nodes_in, 1)
            dve.wait_ge(nodes_in, 1)
            for k in range(2):
                step(dve.tensor_tensor(att_s[:, k, :], att_s[:, k, :], wgat_s[:], ALU.mult))
                ins = dve.reduce_sum(vatt[:, 8 * k:8 * k + 8], att_s[:, k, :].rearrange("p (h c) -> p h c", c=C), AX.X)
            ins.then_inc(vatt_ready, 1)
            step(split(three(hsp), hn[:], nt[:]))
            dve.memset(agg[:, :, 0:C], 0.0)
            dve.memset(agg[:, :, C:C + HEADS], 1.0).then_inc(agg_set, 1)
            dve.wait_ge(att_done, 1)
            att_ps = po[:, 0:A * 16].rearrange("p (a h) -> p a h", h=16)
            step(dve.tensor_copy(asrc_n, att_ps[:, :, 0:8]))
            step(dve.tensor_copy(dnode[:, :, 0:8], att_ps[:, :, 8:16]))
            dve.tensor_tensor(dnode[:, :, 8:16], asrc_n, att_ps[:, :, 8:16], ALU.add).then_inc(table1_ready, 1)

            first_t, last_t, prev_t, next_t = (ends_s[:, k, :] for k in range(4))
            step(dve.tensor_tensor(flags[:, 2, :], first_t, last_t, ALU.is_equal))
            for k, (own, other) in enumerate(((first_t, prev_t), (last_t, next_t))):
                step(dve.tensor_tensor(flags[:, k, :], own, other, ALU.is_equal))
                step(dve.tensor_tensor(flags[:, k, :], flags[:, k, :], flags[:, 2, :], ALU.mult))
            for k in range(2):
                ins = dve.tensor_scalar(flags[:, 2 + k, :], flags[:, k, :], -1.0, BIG, ALU.add, ALU.mult)
            ins.then_inc(flags_ready, 1)
            dve.wait_ge(flags_ready, 1)

            carries = [0]

            def carry(values, forward, maximum):
                step(dve.tensor_copy(car_l, values))
                init = -BIG if maximum else 0.0
                flag = flags[:, (2 if maximum else 0) + (0 if forward else 1), :]
                ops = (ALU.add, ALU.max) if maximum else (ALU.mult, ALU.add)
                end = slice(0, 1) if forward else slice(P - 1, P)
                dve.memset(car_t[:, end], init).then_inc(ends_in, 1)
                carries[0] += 1
                dve.wait_ge(ends_turned, carries[0])
                if forward:
                    ins = dve.tensor_tensor_scan(car_t[:, 1:P], flag[:, 0:P - 1], hp[0:HEADS, 0:P - 1], init, *ops)
                else:
                    ins = dve.tensor_tensor_scan(car_t[:, P - 2::-1], flag[:, P - 1:0:-1], hp[0:HEADS, P - 1:0:-1], init, *ops)
                ins.then_inc(ends_back, 1)
                dve.wait_ge(ends_done, carries[0])
                step(dve.tensor_copy(car_l, hp[:, P:P + HEADS]))

            def scan_heads(to, mask, of, forward, maximum, initial):
                ops = (ALU.add, ALU.max) if maximum else (ALU.mult, ALU.add)
                d = slice(None) if forward else slice(None, None, -1)
                for h in range(HEADS):
                    ins = dve.tensor_tensor_scan(to[:, d, h], mask[:, d], of[:, d, h],
                                                 initial if initial is not None else car_l[:, h:h + 1], *ops)
                step(ins)

            dve.wait_ge(starts1, 16)
            dve.wait_ge(carry1, 16)
            for h in range(2 * HEADS):
                ins = dve.tensor_tensor_scan(d16[:, :, h], same_prev[:], d16[:, :, h], carry_in[:, h:h + 1], ALU.mult, ALU.add)
            step(ins)
            leaky = lambda v: dve.scalar_tensor_tensor(out=v, in0=v, scalar=0.2, in1=v, op0=ALU.mult, op1=ALU.max)
            step(dve.tensor_copy(self1, d16[:, :, 8:16]))
            step(leaky(self1))
            for q in range(RING):
                dve.wait_ge(src1_kept[q], 16 * LOOPS + 16)
            step(dve.tensor_tensor(alpha, asrc_e, d16[:, :, 0:8], ALU.add))
            step(leaky(alpha))
            step(dve.tensor_tensor(seg, alpha, self1, ALU.max))
            step(dve.tensor_scalar(pen[:], same_prev[:], -1.0, BIG, ALU.add, ALU.mult))
            scan_heads(tmp8, pen[:], seg, True, True, -BIG)
            carry(tmp8[:, J - 1, :], True, True)
            scan_heads(seg, pen[:], seg, True, True, None)
            step(dve.tensor_scalar(pen[:], same_next[:], -1.0, BIG, ALU.add, ALU.mult))
            scan_heads(tmp8, pen[:], seg, False, True, -BIG)
            carry(tmp8[:, 0, :], False, True)
            scan_heads(seg, pen[:], seg, False, True, None)
            step(dve.tensor_tensor(alpha, alpha, seg, ALU.subtract))
            dve.tensor_tensor(self1, self1, seg, ALU.subtract).then_inc(exp_in, 1)
            dve.wait_ge(exp_out, 1)
            scan_heads(tmp8, same_prev[:], alpha, True, False, 0.0)
            carry(tmp8[:, J - 1, :], True, False)
            scan_heads(seg, same_prev[:], alpha, True, False, None)
            step(dve.tensor_scalar(pen[:], same_next[:], -1.0, 1.0, ALU.mult, ALU.add))
            step(dve.tensor_tensor(seg, seg, pen[:].unsqueeze(2).to_broadcast([P, J, HEADS]), ALU.mult))
            scan_heads(tmp8, same_next[:], seg, False, False, 0.0)
            carry(tmp8[:, 0, :], False, False)
            scan_heads(seg, same_next[:], seg, False, False, None)
            dve.wait_ge(exp_out, 2)
            step(dve.scalar_tensor_tensor(out=seg, in0=seg, scalar=1e-16, in1=self1, op0=ALU.add, op1=ALU.add))
            step(dve.reciprocal(seg, seg))
            step(dve.tensor_tensor(alpha, alpha, seg, ALU.mult))
            step(dve.tensor_tensor(self1, self1, seg, ALU.mult))
            split([apart[:, :, 8 * k:8 * k + 8] for k in range(3)], alpha, alpha).then_inc(attn_ready, 1)
            dve.wait_ge(attn_ready, 1)

            dve.wait_ge(attn_out, 32)
            step(dve.memset(ww1_, 0.0))
            for q in range(RING):
                ins = dve.tensor_copy(wst_wide[:, q, :, C * q:C * q + C], wst_s[:])
            ins.then_inc(wide_ready, 1)

            with dve.Fori(0, LOOPS) as i:
                for q in range(RING):
                    c = RING * i + q
                    dve.wait_ge(xrep1_out, c + 2)
                    dve.wait_ge(tiles1_done, c + 1)
                    dve.wait_ge(arep1, c + 1)
                    dve.tensor_tensor(prod1[:, q % 2, :, :], rep[:, q % 2, :, :],
                                      xrep[:, q % 2, :].unsqueeze(1).to_broadcast([P, 2, CE]), ALU.mult).then_inc(prod1_done, 1)
            dve.wait_ge(tiles1_out, LOOPS + 1)
            sum_edges(sums1_ready, last1)

            for g in range(-(-A // 2)):
                n = min(2, A - 2 * g)
                dve.wait_ge(own_done, g + 1)
                of = rep[:, g % 4 // 2, g % 2, 0:256 * n].rearrange("p (a h c) -> p a h c", h=HEADS, c=C)
                if g == 0:
                    dve.wait_ge(ended1, 16 * A)
                for k in range(n):
                    ins = dve.tensor_tensor(xself[:, 2 * g + k, :, :], of[:, k],
                                            agg[:, 2 * g + k, C:C + HEADS].unsqueeze(2).to_broadcast([P, HEADS, C]), ALU.mult)
                ins.then_inc(own_used, 1)
            dve.wait_ge(own_used, -(-A // 2))
            hist_row = lambda v: v[:].rearrange("p a c -> p (a c)")
            dve.wait_ge(carried, 2)
            step(dve.reduce_sum(nt[:], xself.rearrange("p a h c -> p a c h"), AX.X))
            step(dve.scalar_tensor_tensor(out=hist_row(nt), in0=hist_row(nt), scalar=1.0 / HEADS, in1=hist_row(hn), op0=ALU.mult, op1=ALU.add))
            step(dve.tensor_tensor(nt[:], nt[:], agg[:, :, 0:C], ALU.add))
            step(dve.tensor_tensor(nt[:], nt[:], row(bias_g), ALU.add))
            add_carried(nt[:], 2)
            layer_norm(hn[:], nt[:], agg[:, :, 0:C])
            step(dve.tensor_tensor(hn[:], hn[:], row(g1_r), ALU.mult))
            dve.tensor_tensor(hn[:], hn[:], row(be1_r), ALU.add).then_inc(nodes_in, 1)
            dve.wait_ge(nodes_in, 2)
            dve.wait_ge(nodes_turned, 3 * GROUPS)
            step(dve.tensor_tensor(hn[:], hn[:], row(b2_r), ALU.add))
            dve.wait_ge(ffn2_done, 1)
            step(dve.tensor_tensor(hist_row(nt), hist_row(hn), rep[:, 0, :, :].rearrange("p g e -> p (g e)")[:, 0:A * C], ALU.add))
            layer_norm(hn[:], nt[:], agg[:, :, 0:C])
            step(dve.tensor_tensor(hn[:], hn[:], row(g2_r), ALU.mult))
            step(dve.tensor_tensor(hn[:], hn[:], row(be2_r), ALU.add))
            dve.tensor_tensor(hn[:], hn[:], xn[:], ALU.add).then_inc(result, 1)

        @block.scalar
        def _(act):
            roots = [0]

            def root_of(to, of, scale, bias):
                roots[0] += 1
                act.wait_ge(var_ready, roots[0])
                act.activation(to, of, ACT.Sqrt, scale=scale, bias=bias).then_inc(root_ready, 1)

            variance_root = lambda: root_of(st[:, 2, :], st[:, 1, :], 1.0 / C, eps_s[:])

            def nodes_to_sbuf(first):
                for g in range(GROUPS):
                    n = min(CE, NP - CE * g)
                    act.wait_ge(nodes_turned, first + g + 1)
                    act.activation(node_t[:, CE * g:CE * g + n], tp[0:C, g % 2, 0:n], ACT.Copy).then_inc(nodes_out, 1)

            act.sem_inc(turned_out, 1)
            act.sem_inc(hidden_ready, 1)
            act.sem_inc(tiles_out, 3)
            act.sem_inc(features_out, 2)
            act.sem_inc(turned1_out, 1)
            act.sem_inc(xrep1_out, 1)
            act.sem_inc(tiles1_out, 1)
            act.sem_inc(features1_out, 1)
            act.sem_inc(post_read, 2)
            act.sem_inc(prod_done, 8)
            act.sem_inc(prod1_done, 2)
            variance_root()
            roots[0] += 1
            act.wait_ge(var_ready, roots[0])
            act.activation(r_, r_, ACT.Sqrt).then_inc(root_ready, 1)
            quarter = lambda v, q: v[:, q * JQ:(q + 1) * JQ, :]
            act.wait_ge(spread_ready, 1)
            for q in range(QUARTERS + 1):
                if q < QUARTERS:
                    act.activation(quarter(b_parts, q)[:, :, 0:C], quarter(a3, q), ACT.Copy).then_inc(hi_cast, 1)
                if q > 0:
                    act.wait_ge(r1_done, q)
                    act.activation(quarter(b_parts, q - 1)[:, :, C:2 * C], quarter(a3, q - 1), ACT.Copy).then_inc(mid_cast, 1)
            act.wait_ge(parts_out, 16 * QUARTERS)

            def open_chunk(c, s):
                hold(act, turned, c + 1 + RING)
                act.activation(x_t[0:S3, s, :, :], tpb[0:S3, 0, :, :], ACT.Copy).then_inc(turned_out, 1)
                hold(act, prod_done, 4 * c + 4)
                hold(act, hidden_done, c + 1 + RING)
                act.activation(hid[:, s, :], hp[:], ACT.Relu, scale=(2.0 / 10.0 / K) ** 0.5).then_inc(hidden_ready, 1)

            def tiles_to_sbuf(c, q, pair_read):
                if pair_read is not None:
                    hold(act, post_read, pair_read)
                hold(act, tiles_back, c + 1)
                act.activation(tp_out[:, TC * q:TC * q + TC, :], hp[:].rearrange("p (t c) -> p t c", c=P), ACT.Copy).then_inc(tiles_out, 1)

            def gates(g):
                hold(act, gates_in, g + 1)
                act.activation(sg, acc[:, :, 0:16], ACT.Tanh, scale=PW_S).then_inc(gates_out, 1)

            def group(i, first, final):
                for q in range(RING):
                    c = RING * i + q
                    if not (final and q == RING - 1):
                        open_chunk(c + 1, (q + 1) % 2)
                    if not (first and q == 0):
                        tiles_to_sbuf(c - 1, (q - 1) % RING, {1: 2 * i + 1, 3: 2 * i + 2}.get(q))
                    if q == 3 or (q == 1 and not first):
                        gates(2 * i - 1 if q == 1 else 2 * i)
                    hold(act, tiles_done, c + 3)
                    act.activation(by_feature[:, q % 2, :], po2[q % 2], ACT.Copy).then_inc(features_out, 1)

            open_chunk(0, 0)
            group(0, True, False)
            with act.Fori(1, LOOPS - 1) as i:
                group(i, False, False)
            group(LOOPS - 1, False, True)
            tiles_to_sbuf(NCH - 1, RING - 1, None)
            gates(2 * LOOPS - 1)

            variance_root()
            nodes_to_sbuf(0)
            act.wait_ge(exp_in, 1)
            act.activation(alpha, alpha, ACT.Exp).then_inc(exp_out, 1)
            act.activation(self1, self1, ACT.Exp).then_inc(exp_out, 1)
            act.wait_ge(attn_out, 32)

            def open_chunk1(c, s):
                hold(act, turned1, c + 1 + RING)
                act.activation(xt1_s[:, s, :], tp[:].bitcast(BF16)[0:S3, 0, 0:CE + P], ACT.Copy).then_inc(turned1_out, 1)
                hold(act, prod1_done, c + 1)
                hold(act, xrep1, c + 1)
                act.activation(xrep[:, s, :], hp[:], ACT.Copy).then_inc(xrep1_out, 1)

            open_chunk1(0, 0)

            def tiles1_to_sbuf(i):
                hold(act, tiles1_back, i + 1)
                act.activation(a3[:, bass.ds(16 * i, 16), :].rearrange("p (q t) c -> p t q c", q=RING),
                               tp[:, 1, :].rearrange("p (t q c) -> p t q c", t=TC, q=RING), ACT.Copy).then_inc(tiles1_out, 1)

            def group1(i, first, final):
                for q in range(RING):
                    if not (final and q == RING - 1):
                        open_chunk1(RING * i + q + 1, (q + 1) % 2)
                    if q == 1 and not first:
                        tiles1_to_sbuf(i - 1)
                hold(act, tiles1_done, RING * i + RING + 2)
                act.activation(fm1_, po[:], ACT.Copy).then_inc(features1_out, 1)

            group1(0, True, False)
            with act.Fori(1, LOOPS - 1) as i:
                group1(i, False, False)
            group1(LOOPS - 1, False, True)
            tiles1_to_sbuf(LOOPS - 1)
            nodes_to_sbuf(GROUPS)
            variance_root()
            nodes_to_sbuf(2 * GROUPS)
            for g in range(GROUPS):
                n = min(CE, NP - CE * g)
                act.wait_ge(ffn_done, g + 1)
                act.activation(hid1_[:, CE * g:CE * g + n], tp[:, g % 2, 0:n], ACT.Relu, bias=b1_s[:]).then_inc(ffn_out, 1)
            variance_root()

        @block.tensor
        def _(pe):
            pe.sem_inc(onehot_used, 2)
            pe.sem_inc(turned, RING)
            pe.sem_inc(hidden_done, RING)
            pe.sem_inc(tiles_done, 2)
            pe.sem_inc(turned1, RING)
            pe.sem_inc(tiles1_done, 2)
            pe.wait_ge(consts, CONSTS)
            pe.wait_ge(agg_set, 1)
            pe.matmul(po[:, 0:A], zerob[:], zerob[:, 0:A], start=True, stop=False, skip_group_check=True)
            with pe.Fori(0, LOOPS // 2) as i:
                for half in range(2):
                    pe.wait_ge(onehot_ready, 2 * i + half + 1)
                    for t in range(16):
                        ins = pe.matmul(po[:, 0:A], oh_lo[:, half, :, t], oh_hi[:, :, bass.ds(32 * i + 16 * half + t, 1)].squeeze(2),
                                        start=False, stop=False, skip_group_check=True)
                    ins.then_inc(onehot_used, 1)
            pe.matmul(po[:, 0:A], zerob[:], zerob[:, 0:A], start=False, stop=True, skip_group_check=True).then_inc(hist_done, 1)
            pe.wait_ge(hist_copied, 1)
            pe.matmul(hp[:, 0:A], tri_s, hist[:], start=True, stop=True)
            pe.matmul(hp[:, 32:32 + A], ones_s[:], hist[:], start=True, stop=True).then_inc(cum_done, 1)
            pe.wait_ge(parts_ready, QUARTERS)

            def turn(c, i, q):
                s = q % 2
                pe.wait_ge(turned_out, c + 1)
                pe.wait_ge(src_landed[q], 16 * TC * (i + 1))
                for t in range(TC):
                    pe.transpose(tpb[0:S3, 0, 0, P * t:P * t + P], xs_ring[:, q, t, 0:S3], identb_s[:])
                pe.wait_ge(dst_landed[q], 16 * (i + 1))
                for t in range(TC):
                    ins = pe.transpose(tpb[0:S3, 0, 1, P * t:P * t + P], xd_ring[:, q, t, :], identb_s[:])
                ins.then_inc(turned, 1)
                pe.wait_ge(tiles_out, c + 1)
                pe.wait_ge(emb_landed[q], 16 * (i + 1))
                pe.matmul(hp[:], w1_s[:], emb_ring[0:10, q, :], start=True, stop=True).then_inc(hidden_done, 1)

            def repeat(c, q, u):
                if u == 0:
                    pe.wait_ge(turned_out, c + 2)
                pe.wait_ge(prod_done, 4 * c + u + 7)
                for d in range(2):
                    ins = pe.matmul(rep[:, u % 2, d, :], sel_s[:, u, :], x_t[0:S3, q % 2, d, :], start=True, stop=True)
                ins.then_inc(rep_ready, 1)

            def contract(c, q, u):
                pe.wait_ge(prod_done, 4 * c + u + 9)
                if u == 0:
                    pe.wait_ge(features_out, c + 1)
                for d in range(2):
                    ins = pe.matmul(po2[q % 2], w2_wide[:, u, d, :], prod[:, q % 2, u, d, :],
                                    start=(u == 0 and d == 0), stop=(u == 3 and d == 1))
                if u == 3:
                    ins.then_inc(tiles_done, 1)

            def turn_back(c, q, hidden):
                pe.wait_ge(features_out, c + 3)
                pe.wait_ge(hidden_ready, hidden + 2)
                for t in range(TC):
                    ins = pe.transpose(hp[:, P * t:P * t + P], by_feature[:, q % 2, P * t:P * t + P], ident_s[:])
                ins.then_inc(tiles_back, 1)

            def chunk0(c, i, q, first=False, final=False):
                contract(c, q, 0)
                repeat(c, q, 2)
                if not final:
                    turn(c + 1, i if q + 1 < RING else i + 1, (q + 1) % RING)
                contract(c, q, 1)
                repeat(c, q, 3)
                if not first:
                    turn_back(c - 1, (q - 1) % 2, c if final else c + 1)
                contract(c, q, 2)
                if not final:
                    repeat(c + 1, q + 1, 0)
                contract(c, q, 3)
                if not final:
                    repeat(c + 1, q + 1, 1)

            pe.wait_ge(wide_ready, 1)
            turn(0, 0, 0)
            repeat(0, 0, 0)
            repeat(0, 0, 1)
            for q in range(RING):
                chunk0(q, 0, q, first=q == 0)
            with pe.Fori(1, LOOPS - 1) as i:
                for q in range(RING):
                    chunk0(RING * i + q, i, q)
            for q in range(RING):
                chunk0(RING * (LOOPS - 1) + q, LOOPS - 1, q, final=q == RING - 1)
            turn_back(NCH - 1, (NCH - 1) % 2, NCH - 1)

            def carry_over(ready):
                pe.wait_ge(ready, 1)
                flat = nt[:].rearrange("p a c -> p (a c)")
                for k in range(2):
                    ins = pe.matmul((po, hp)[k][:, 0:A * C // 2], e_lo[:], flat[:, 400 * k:400 * k + 400], start=True, stop=True)
                ins.then_inc(carried, 1)

            def turn_nodes(first):
                for g in range(GROUPS):
                    pe.wait_ge(nodes_out, first + g - 1) if first + g > 1 else None
                    for a in range(4 * g, min(4 * g + 4, A)):
                        ins = pe.transpose(tp[0:C, g % 2, P * (a - 4 * g):P * (a - 4 * g) + P], hn[:, a, :], ident_s[:])
                    ins.then_inc(nodes_turned, 1)
                pe.wait_ge(nodes_out, first + GROUPS)

            carry_over(last0)
            pe.wait_ge(nodes_in, 1)
            turn_nodes(0)
            pe.wait_ge(vatt_ready, 1)
            for a in range(A):
                ins = pe.matmul(po[:, 16 * a:16 * a + 16], node_t[:, P * a:P * a + P], vatt[:], start=True, stop=True)
            ins.then_inc(att_done, 1)
            for k in range(4):
                pe.wait_ge(ends_in, k + 1)
                pe.transpose(hp[0:HEADS, 0:P], car_l, ident_s[:]).then_inc(ends_turned, 1)
                pe.wait_ge(ends_back, k + 1)
                pe.transpose(hp[:, P:P + HEADS], car_t, ident_s[0:HEADS, 0:HEADS]).then_inc(ends_done, 1)

            pe.wait_ge(attn_out, 32)

            def open1(c, i, q):
                s = q % 2
                pe.wait_ge(turned1_out, c + 1)
                pe.wait_ge(x1_landed[q], 16 * (i + 1))
                for t in range(TC):
                    pe.transpose(tpb[0:S3, 0, 0, P * t:P * t + P], xs_ring[:, q, t, 0:S3], identb_s[:])
                pe.wait_ge(at_landed[q], 16 * (i + 1))
                pe.transpose(tpb[0:S3, 0, 1, 0:P], xd_ring[:, q, 0, :], identb_s[:]).then_inc(turned1, 1)
                pe.wait_ge(turned1_out, c + 2)
                pe.wait_ge(xrep1_out, c + 1)
                pe.matmul(hp[:], selx_s[:], xt1_s[:, s, 0:CE], start=True, stop=True).then_inc(xrep1, 1)
                pe.wait_ge(prod1_done, c + 1)
                for g in range(2):
                    for t in range(TC):
                        ins = pe.matmul(rep[:, s, g, P * t:P * t + P], sela_s[:, t, g, :], xt1_s[:, s, CE:CE + P], start=True, stop=True)
                ins.then_inc(arep1, 1)

            def close1(c, i, q):
                pe.wait_ge(prod1_done, c + 3)
                if q == 0:
                    pe.wait_ge(features1_out, i + 1)
                for g in range(2):
                    ins = pe.matmul(po[:], wst_wide[:, q, g, :], prod1[:, q % 2, g, :],
                                    start=(q == 0 and g == 0), stop=(q == RING - 1 and g == 1))
                ins.then_inc(tiles1_done, 1)

            def turn_back1(i):
                pe.wait_ge(features1_out, i + 2)
                pe.wait_ge(tiles1_out, i + 1)
                for t in range(TC):
                    ins = pe.transpose(tp[:, 1, P * t:P * t + P], fm1_[:, P * t:P * t + P], ident_s[:])
                ins.then_inc(tiles1_back, 1)

            def chunk1(c, i, q, first=False, final=False):
                if not final:
                    open1(c + 1, i if q + 1 < RING else i + 1, (q + 1) % RING)
                close1(c, i, q)
                if q == 0 and not first:
                    turn_back1(i - 1)

            pe.wait_ge(wide_ready, 2)
            open1(0, 0, 0)
            for q in range(RING):
                chunk1(q, 0, q, first=q == 0)
            with pe.Fori(1, LOOPS - 1) as i:
                for q in range(RING):
                    chunk1(RING * i + q, i, q)
            for q in range(RING):
                chunk1(RING * (LOOPS - 1) + q, LOOPS - 1, q, final=q == RING - 1)
            turn_back1(LOOPS - 1)

            carry_over(last1)
            turn_nodes(GROUPS)
            for g in range(-(-A // 2)):
                if g >= 4:
                    pe.wait_ge(own_used, g - 3)
                for k in range(min(2, A - 2 * g)):
                    a = 2 * g + k
                    ins = pe.matmul(rep[:, g % 4 // 2, g % 2, 256 * k:256 * k + 256], node_t[:, P * a:P * a + P], wgat_s[:],
                                    start=True, stop=True)
                ins.then_inc(own_done, 1)
            pe.wait_ge(own_used, -(-A // 2))
            pe.wait_ge(nodes_in, 2)
            turn_nodes(2 * GROUPS)
            for g in range(GROUPS):
                n = min(CE, NP - CE * g)
                if g >= 2:
                    pe.wait_ge(ffn_out, g - 1)
                pe.matmul(tp[:, g % 2, 0:n], f1_s[:], node_t[:, CE * g:CE * g + n], start=True, stop=True).then_inc(ffn_done, 1)
            pe.wait_ge(ffn_out, GROUPS)
            ff = rep[:, 0, :, :].rearrange("p g e -> p (g e)")
            for a in range(A):
                ins = pe.matmul(ff[:, C * a:C * a + C], hid1_[:, P * a:P * a + P], f2_s[:], start=True, stop=True)
            ins.then_inc(ffn2_done, 1)


def kernel(x, src, dst, edge_attr_10, edge_attr_3, edge_weight, L0_gnn_W1, L0_gnn_W2, L1_gnn_W_gat, L1_gnn_att_src,
           L1_gnn_att_dst, L1_gnn_bias_gat, L1_gnn_w1, L1_gnn_b1, L1_gnn_w2, L1_gnn_b2, L1_gnn_g1, L1_gnn_be1,
           L1_gnn_g2, L1_gnn_be2):
    import ml_dtypes
    import concourse.bacc as bacc
    from concourse.bass_utils import run_bass_kernel_spmd

    arr = np.asarray
    bf = ml_dtypes.bfloat16
    pads = EP - E

    def edge_rows(v, fill, n=pads):
        return np.concatenate([arr(v), np.full((n,) + arr(v).shape[1:], fill, arr(v).dtype)])

    d = np.concatenate([np.array([4000], np.int32), edge_rows(dst, NP - 1), np.array([5000], np.int32)]).astype(np.int32, copy=False)
    dst_ext = np.stack([d[p * J:p * J + J + 2] for p in range(P)])
    emb = edge_rows(edge_attr_10, 0).reshape(P, J, 10)
    w2 = arr(L0_gnn_W2).reshape(K, 7, 2 * U, U)[:, [0, 2, 4, 1, 3, 6, 5]]
    eye = np.eye(P, dtype=np.float32)
    rep_sel = np.zeros((3, C, 4, U, K), bf)
    sel_x = np.zeros((3, C, C, 4), bf)
    sel_attn = np.zeros((TC, 3, HEADS, TC, 2, C, 4), bf)
    for part in range(3):
        for u in range(U):
            rep_sel[part, u, 0, u] = 1
            for k in range(3):
                rep_sel[part, U + 3 * u + k, k + 1, u] = 1
        for c in range(C):
            sel_x[part, c, c] = 1
        for t in range(TC):
            for h in range(HEADS):
                sel_attn[t, part, h, t, h // 4, :, h % 4] = 1
    wg = arr(L1_gnn_W_gat)
    feeds = {
        "x": np.concatenate([arr(x), np.zeros((NP - N, C), np.float32)]),
        "src": edge_rows(src, 0).reshape(P, J),
        "dst_ext": dst_ext,
        "dst_ends": np.ascontiguousarray(dst_ext[:, [1, J, 0, J + 1]].T),
        "emb": np.ascontiguousarray(emb.transpose(2, 1, 0)).reshape(10, EP),
        "vec": np.ascontiguousarray(edge_rows(edge_attr_3, 1).reshape(P, J, 3).transpose(0, 2, 1)),
        "weight": edge_rows(edge_weight, 0).reshape(P, J),
        "w1rep": np.tile(arr(L0_gnn_W1), (1, U)),
        "w2r": np.ascontiguousarray(w2.transpose(2, 0, 1, 3).reshape(2, P, 56).transpose(1, 0, 2)),
        "rep_sel": rep_sel.reshape(S3, 4, P),
        "ident": eye, "identb": eye.astype(bf), "tri": np.triu(np.ones((P, P), np.float32)),
        "iota_b": np.tile(np.arange(P), (P, 1)).astype(bf),
        "w_gat": wg,
        "w_stack": np.ascontiguousarray(wg.reshape(C, 2, 4, C).transpose(0, 2, 1, 3)).reshape(P, 2, C),
        "att": np.stack([arr(L1_gnn_att_src).reshape(-1), arr(L1_gnn_att_dst).reshape(-1)]),
        "sel_x": sel_x.reshape(S3, P), "sel_attn": sel_attn.reshape(S3, TC, 2, P),
        "ffn1": arr(L1_gnn_w1), "ffn2": arr(L1_gnn_w2),
        "rows": np.stack([arr(v) for v in (L1_gnn_bias_gat, L1_gnn_b2, L1_gnn_g1, L1_gnn_be1, L1_gnn_g2, L1_gnn_be2)]),
        "b1": arr(L1_gnn_b1).reshape(P, 1),
    }
    feeds = {k: np.ascontiguousarray(v) for k, v in feeds.items()}
    nc = bacc.Bacc("TRN2", target_bir_lowering=False, num_devices=1)
    args = [nc.dram_tensor(k, v.shape, mybir.dt.from_np(v.dtype), kind="ExternalInput").ap() for k, v in feeds.items()]
    out = nc.dram_tensor("out", (N, C), F32, kind="ExternalOutput").ap()
    tensor_network(nc, *args, out)
    return run_bass_kernel_spmd(nc, [feeds], core_ids=[0]).results[0]["out"]
```

```python
from contextlib import ExitStack

import numpy as np
import concourse.bass as bass
from concourse import mybir

F32 = mybir.dt.float32
I32 = mybir.dt.int32
BF16 = mybir.dt.bfloat16
ALU = mybir.AluOpType
ACT = mybir.ActivationFunctionType
AX = mybir.AxisListType

N, E, C = 3125, 53125, 32
P = 128
A = -(-N // P)
NP = A * P
B64 = 64
J = 416
EP = P * J
S3 = 3 * C
HEADS = 8
EMB = 10
K = 16
U = 8
TC = 4
CE = TC * P
NCH = J // TC
RING = 4
PT = 2 * TC
ROW1 = S3 + 2 * HEADS
LN_EPS = 1e-5
TANH_GAIN = 1.593
PW_S = 0.17677669529663687
PW_V = 0.25
BIG = 1e30
NOWHERE = 1e6


def tensor_network(nc, x, src, dst_ext, dst_ends, emb, vec, weight, w1rep, w2r, rep_sel, ident, identb, tri,
                   iota_b, which, w_gat, meets, att, ffn1, ffn2, rows, b1, out):
    dram = lambda name, shape, dt: nc.dram_tensor(name, shape, dt, kind="Internal").ap()
    src_table0 = dram("src_table0", (NP, S3), BF16)
    node_table0 = dram("node_table0", (NP, C), F32)
    at_starts0 = dram("at_starts0", (EP, C), F32)
    emb_parts = dram("emb_parts", (6 * EMB, EP), BF16)
    sums0 = dram("sums0", (EP, C), F32)
    src_table1 = dram("src_table1", (NP, ROW1 // 2), F32)
    node_table1 = dram("node_table1", (NP, 2 * HEADS), F32)
    at_starts1 = dram("at_starts1", (EP, 2 * HEADS), F32)
    sums1 = dram("sums1", (EP, C + HEADS), F32)

    nodes_of = lambda t: t.rearrange("(a b) c -> b a c", b=P)
    edges_of = lambda t: t.rearrange("(p j) c -> p j c", p=P)

    with ExitStack() as ctx:
        sb = lambda name, shape, dt=F32: ctx.enter_context(nc.sbuf_tensor(name, shape, dt))
        psum = lambda name, shape, dt=F32: ctx.enter_context(nc.psum_tensor(name, shape, dt))
        sem = lambda name: ctx.enter_context(nc.semaphore(name))

        area_a = sb("area_a", [P, J * C])
        area_b = sb("area_b", [P, J * ROW1 // 2])
        area_e = sb("area_e", [P, 2 * J * HEADS])
        zeros = area_a[:].rearrange("p (j c) -> p j c", c=C)

        def views(area, sizes, start=0):
            got, at = [], start
            for s in sizes:
                got.append(area[:, at:at + s])
                at += s
            return got

        msg_, msgmask_, sums_ = views(area_a, [17 * C, 17 * C, 16 * C])
        msg, msgmask = (v.rearrange("p (c j) -> p c j", c=C) for v in (msg_, msgmask_))
        sums_by_edge = sums_.rearrange("p (j c) -> p j c", c=C)
        pr_, xt_, hid_, emb_, g_, tmp_, acc_, v_, sg_, sgn_, fm_, w2w_, starts_, runs_, runmask_, rest_, w1b_ = views(
            area_b, [2 * 8 * CE, 2 * CE, 2 * CE, RING * CE // 2, 16 * P, PT * 72, PT * 24, PT * 24, PT * 16, PT * 8, 2 * CE, 8 * P,
                     16 * C, 17 * C, 17 * C, 16 * C, P // 2])
        starts_in = starts_.rearrange("p (j c) -> p j c", c=C)
        runs = runs_.rearrange("p (c j) -> p c j", c=C)
        runmask = runmask_.rearrange("p (c j) -> p c j", c=C)
        prod = pr_.rearrange("p (s u d e) -> p s u d e", s=2, u=4, d=2)
        x_t = xt_.bitcast(BF16).rearrange("p (s d e) -> p s d e", s=2, d=2)
        hid = hid_.rearrange("p (s e) -> p s e", s=2)
        emb_ring = emb_.bitcast(BF16)[0:6 * EMB, :].rearrange("p (s e) -> p s e", s=RING)
        w1b_s = w1b_[0:6 * EMB, :].bitcast(BF16)
        tp_out = g_.rearrange("p (t c) -> p t c", c=P)
        tmp = tmp_.rearrange("p (t i w) -> p t i w", t=PT, i=3)
        acc = acc_.rearrange("p (t w) -> p t w", t=PT)
        vbuf = v_.rearrange("p (t k w) -> p t k w", t=PT, k=3)
        sg = sg_.rearrange("p (t w) -> p t w", t=PT)
        sgn = sgn_.rearrange("p (t w) -> p t w", t=PT)
        by_feature = fm_.rearrange("p (s e) -> p s e", s=2)
        w2_wide = w2w_.rearrange("p (u d n) -> p u d n", u=4, d=2)
        oh_hi_, oh_lo_, iota_x_, es_, ep_ = views(
            area_b, [4 * 2 * A * 4, 4 * B64 * 4, B64 * 4, EMB * J, 3 * EMB * J // 2])
        wr_, wp_, hist_rows = views(area_a, [P, 3 * P // 2, 2 * P])
        hist_rows = hist_rows[0:2 * A, :].rearrange("p (k n) -> p k n", k=2)
        emb_s = es_
        emb_parts_s = ep_.bitcast(BF16).rearrange("p (k n) -> p k n", k=3)
        w1_rest, w1_parts = wr_[0:6 * EMB, :], wp_[0:6 * EMB, :].bitcast(BF16).rearrange("p (k n) -> p k n", k=3)
        onehot_hi = oh_hi_.bitcast(BF16).rearrange("p (s a t) -> p s a t", s=4, a=2 * A)
        onehot_lo = oh_lo_.bitcast(BF16).rearrange("p (s b t) -> p s b t", s=4, b=B64)
        iota_x = iota_x_.bitcast(BF16).rearrange("p (b t) -> p b t", b=B64)
        hid1_, xself_ = views(area_b, [NP, A * 256])
        node_t = area_b[0:C, 9600:9600 + NP]
        xself = xself_.rearrange("p (a h c) -> p a h c", a=A, h=HEADS)
        vec_, wt_, r_, dlo_, dhi_, dbf_ = views(area_e, [3 * J, J, J, J, J, J])
        nvec = vec_.rearrange("p (i j) -> p i j", i=3)
        lo_i, hi_i = dlo_.bitcast(I32), dhi_.bitcast(I32)
        lo_bf, hi_bf = views(dbf_.bitcast(BF16), [J, J])
        gath1 = area_b[:].rearrange("p (j c) -> p j c", c=ROW1 // 2)
        h8 = lambda v: v.rearrange("p (j h) -> p j h", h=HEADS)
        alpha, self1 = map(h8, views(area_e, [J * HEADS] * 2))
        d16_, seg_, tmp8_ = views(area_a, [2 * J * HEADS, J * HEADS, J * HEADS])
        d16 = d16_.rearrange("p (j c) -> p j c", c=2 * HEADS)
        seg, tmp8 = h8(seg_), h8(tmp8_)
        gath1_bf = area_b[:].bitcast(BF16).rearrange("p (j c) -> p j c", c=ROW1)
        _, msg_odd_, xt1_, pr1_ = views(area_a, [34 * C, 17 * C, CE, RING * 2 * CE])
        own_sums_, mask_odd_ = views(area_a, [16 * (C + HEADS), 17 * C], 3 * J * HEADS)
        mask_odd = mask_odd_.rearrange("p (c j) -> p c j", c=C)
        msg_odd = msg_odd_.rearrange("p (c j) -> p c j", c=C)
        sums1_by_edge = own_sums_.rearrange("p (j c) -> p j c", c=C + HEADS)
        prod1 = pr1_.rearrange("p (s t h c) -> p s t h c", s=RING, t=TC, h=HEADS)
        xt1_s = xt1_.bitcast(BF16).rearrange("p (s e) -> p s e", s=2)
        wrest_s = tmp8_[:, 0:2 * P]

        asrc_e = area_b[:].rearrange("p (j c) -> p j c", c=ROW1 // 2)[:, :, S3 // 2:ROW1 // 2]
        split_, att_, dnode_, tri_s, iota_, sel_, ends_ = views(
            area_b, [A * ROW1 // 2, 4 * P, A * 2 * HEADS, P, P // 2, 2 * P, 4 * P], J * S3 // 2)
        hsplit = split_.bitcast(BF16).rearrange("p (a c) -> p a c", a=A)
        att_s = att_[0:C, :].rearrange("p (k n) -> p k n", k=2)
        dnode = dnode_.rearrange("p (a c) -> p a c", a=A)
        iota_s = iota_.bitcast(BF16)
        sel_s = sel_[0:S3, :].bitcast(BF16).rearrange("p (u n) -> p u n", u=4)
        ends_s = ends_[0:HEADS, :].bitcast(I32).rearrange("p (k n) -> p k n", k=4)
        ident_s, identb_s = sb("ident_s", [P, P]), sb("identb_s", [P, P], BF16)
        ones_s = sb("ones_s", [P, P])
        w1_s, w2_s = sb("w1_s", [6 * EMB, P]), sb("w2_s", [P, 2, 56])
        wgat_s, wval_s = sb("wgat_s", [P, 2 * P]), sb("wval_s", [P, 3, 2 * P], BF16)
        meets_s = sb("meets_s", [P, 3])
        f1_s, f2_s, b1_s, rows_s = sb("f1_s", [C, P]), sb("f2_s", [P, C]), sb("b1_s", [P, 1]), sb("rows_s", [P, 6, C])
        bias_g, b2_r, g1_r, be1_r, g2_r, be2_r = (rows_s[:, i, :] for i in range(6))
        src_s, dst_s = sb("src_s", [P, J], I32), sb("dst_s", [P, J + 2], I32)
        eps_s, which_s = sb("eps_s", [P, 1]), sb("which_s", [6 * EMB, 3])
        same_prev, same_next = sb("same_prev", [P, J]), sb("same_next", [P, J])
        pen = sb("pen", [P, J])
        idx_ring = sb("idx_ring", [P, 2, 16], I32)
        xs_words = sb("xs_words", [P, RING, TC, ROW1 // 2])
        xs_ring = xs_words[:].bitcast(BF16)
        xd_area = sb("xd_area", [P, RING * TC * S3 // 2])
        xd_ring = xd_area[:].bitcast(BF16).rearrange("p (q t c) -> p q t c", q=RING, t=TC)
        flags_, car_t_, car_l = views(xd_area[:], [4 * P, P, HEADS])
        flags = flags_[0:HEADS, :].rearrange("p (k n) -> p k n", k=4)
        car_t = car_t_[0:HEADS, :]
        node = lambda name: sb(name, [P, A, C])
        xn, hn, nt, agg = node("xn"), node("hn"), node("nt"), sb("agg", [P, A, C + HEADS])
        hsp = hsplit[:, :, 0:S3]
        asrc_n = hsplit[:, :, S3:ROW1].bitcast(F32)
        st = sb("st", [P, 4, A])
        hist, start_i, end_i = sb("hist", [P, A]), sb("start_i", [P, A], I32), sb("end_i", [P, A], I32)
        e_lo, e_hi = sb("e_lo", [P, P]), sb("e_hi", [P, A])
        carry_in, last = sb("carry_in", [P, C]), sb("last", [P, C])
        endf = sb("endf", [P, 4])
        zerob = sb("zerob", [P, P], BF16)
        vatt = sb("vatt", [C, 16])

        rep = psum("rep", [P, 2, 2, CE])
        tp = psum("tp", [P, 2, CE])
        hp = psum("hp", [P, CE])
        po = psum("po", [P, CE])
        tpb = tp[:].bitcast(BF16).rearrange("p s (d e) -> p s d e", d=2)
        po2 = (po[:], tp[:, 1, :])

        consts, x_in, dst_in = sem("consts"), sem("x_in"), sem("dst_in")
        zero_set, zeroed = sem("zero_set"), sem("zeroed")
        dve_step, pool_step = sem("dve_step"), sem("pool_step")
        var_ready, root_ready = sem("var_ready"), sem("root_ready")
        table0_ready, tables0, wide_ready = sem("table0_ready"), sem("tables0"), sem("wide_ready")
        onehot_ready, onehot_used, hist_done = sem("onehot_ready"), sem("onehot_used"), sem("hist_done")
        hist_out, hist_turned = sem("hist_out"), sem("hist_turned")
        emb_in, emb_hi, emb_rest, emb_mid, emb_lo, embs_out = (
            sem("emb_in"), sem("emb_hi"), sem("emb_rest"), sem("emb_mid"), sem("emb_lo"), sem("embs_out"))
        hist_copied, cum_done, bounds_ready = sem("hist_copied"), sem("cum_done"), sem("bounds_ready")
        carry0, scattered0, starts_landed, starts_used, dst_ready = (
            sem("carry0"), sem("scattered0"), sem("starts_landed"), sem("starts_used"), sem("dst_ready"))
        idx_copied = [sem(f"idx_copied{i}") for i in range(2)]
        idx_used = [sem(f"idx_used{i}") for i in range(2)]
        src_landed = [sem(f"src_landed{q}") for q in range(RING)]
        emb_landed = [sem(f"emb_landed{q}") for q in range(RING)]
        turned, hidden_done = sem("turned"), sem("hidden_done")
        turned_out, hidden_ready = sem("turned_out"), sem("hidden_ready")
        rep_ready, prod_done, tiles_done, tiles_out, post_read = (
            sem("rep_ready"), sem("prod_done"), sem("tiles_done"), sem("tiles_out"), sem("post_read"))
        features_out, tiles_back = sem("features_out"), sem("tiles_back")
        msg1_used, inverse_ready, self_ready = sem("msg1_used"), sem("inverse_ready"), sem("self_ready")
        masks1, scanned1, mask_columns = sem("masks1"), sem("scanned1"), sem("mask_columns")
        gates_in, gates_out = sem("gates_in"), sem("gates_out")
        sums0_ready, sums0_out, ended0, last0 = sem("sums0_ready"), sem("sums0_out"), sem("ended0"), sem("last0")
        carried, flags_ready = sem("carried"), sem("flags_ready")
        nodes_in, nodes_turned, nodes_out = sem("nodes_in"), sem("nodes_turned"), sem("nodes_out")
        vatt_ready, att_done, table1_ready, tables1 = (
            sem("vatt_ready"), sem("att_done"), sem("table1_ready"), sem("tables1"))
        carry1, scattered1, starts1 = sem("carry1"), sem("scattered1"), sem("starts1")
        src1_landed = [sem(f"src1_landed{q}") for q in range(RING)]
        src1_kept = [sem(f"src1_kept{q}") for q in range(RING)]
        ends_in, ends_turned, ends_back, ends_done = (
            sem("ends_in"), sem("ends_turned"), sem("ends_back"), sem("ends_done"))
        exp_in, exp_out = sem("exp_in"), sem("exp_out")
        attn_ready = sem("attn_ready")
        turned1, turned1_out, values1, prod1_done, halved1, first_halved1, heads1_summed = (
            sem("turned1"), sem("turned1_out"), sem("values1"), sem("prod1_done"), sem("halved1"), sem("first_halved1"),
            sem("heads1_summed"))
        sums1_ready, sums1_out, ended1_first, ended1, last1, agg_set = (
            sem("sums1_ready"), sem("sums1_out"), sem("ended1_first"), sem("ended1"), sem("last1"), sem("agg_set"))
        own_done, own_out, own_summed, ffn_done, ffn_out, ffn2_done = (
            sem("own_done"), sem("own_out"), sem("own_summed"), sem("ffn_done"), sem("ffn_out"), sem("ffn2_done"))
        result, written = sem("result"), sem("written")

        constants = [(ident_s, ident), (identb_s, identb), (tri_s, tri), (iota_s, iota_b), (sel_s, rep_sel),
                     (w1_s, w1rep), (which_s, which), (w2_s, w2r), (wgat_s, w_gat), (meets_s, meets), (f1_s, ffn1), (f2_s, ffn2), (b1_s, b1),
                     (rows_s, rows.partition_broadcast(P)), (att_s, att.partition_broadcast(C)),
                     (ends_s, dst_ends.partition_broadcast(HEADS)), (src_s, src), (nvec, vec), (wt_, weight)]
        CONSTS = 16 * len(constants)
        GROUPS = -(-NP // CE)
        GROUP_STEPS = 21
        LOOPS = J // 16

        def hold(eng, semaphore, value):
            eng.wait_ge(semaphore, value)
            eng.wait_ge(consts, CONSTS)

        def hold_pool(pool, semaphore, value):
            pool.wait_ge(semaphore, value)
            pool.sem_inc(pool_step, 1)

        class Steps:

            def __init__(self, eng, semaphore):
                self.eng, self.sem, self.count, self.offset = eng, semaphore, 0, 0

            def __call__(self, instruction):
                instruction.then_inc(self.sem, 1)
                self.count += 1
                self.eng.wait_ge(self.sem, self.offset + self.count)

        HALVED = 2
        OWN = 19

        def own_messages(eng, cols):
            return eng.tensor_tensor(xself[:, cols], xself[:, cols],
                                     agg[:, cols, C:C + HEADS].unsqueeze(3).to_broadcast([P, cols.stop - cols.start, HEADS, C]), ALU.mult)

        block = ctx.enter_context(nc.Block())

        @block.sync
        def _(sp):
            for q in range(RING):
                sp.sem_inc(src1_kept[q], 16)
            sp.dma_start(dst_s[:], dst_ext).then_inc(dst_in, 16)
            sp.dma_start(xn[:], nodes_of(x)).then_inc(x_in, 16)
            sp.dma_start(emb_s, emb).then_inc(emb_in, 16)
            for to, of in constants:
                sp.dma_start(to[:] if not isinstance(to, bass.AP) else to, of).then_inc(consts, 16)
            sp.wait_ge(zero_set, 1)
            sp.dma_start(edges_of(at_starts0), zeros).then_inc(zeroed, 16)
            sp.dma_start(edges_of(at_starts1), area_a[:, 0:J * 16].rearrange("p (j c) -> p j c", c=16)).then_inc(zeroed, 16)
            sp.wait_ge(table0_ready, 1)
            sp.dma_start(nodes_of(node_table0), hn[:]).then_inc(tables0, 16)
            sp.dma_start(nodes_of(src_table0), hsp).then_inc(tables0, 16)
            of_block = lambda k: emb_parts[EMB * k:EMB * (k + 1), :].rearrange("r e -> (r e)").rearrange("(p n) -> p n", p=P)
            for part, (ready, blocks) in enumerate(((emb_hi, (0, 3, 5)), (emb_mid, (1, 4)), (emb_lo, (2,)))):
                sp.wait_ge(ready, 1)
                for k in blocks:
                    sp.dma_start(of_block(k), emb_parts_s[:, part, :]).then_inc(embs_out, 16)
            sp.wait_ge(embs_out, 96)
            sp.wait_ge(scattered0, 16 * A)
            def load_group(i):
                hold(sp, starts_used, i + 1)
                sp.dma_start(starts_in, edges_of(at_starts0)[:, bass.ds(16 * i, 16), :]).then_inc(starts_landed, 16)
                for q in range(RING):
                    hold(sp, hidden_done, RING * i + q + 1)
                    sp.dma_start(emb_ring[:, q, :], emb_parts[:, bass.ds((RING * i + q) * CE, CE)]).then_inc(emb_landed[q], 16)

            def store_sums(i, sums, by_edge, ready, out):
                hold(sp, ready, i + 1)
                sp.dma_start(edges_of(sums)[:, bass.ds(16 * i, 16), :], by_edge).then_inc(out, 16)

            AHEAD = 3
            with sp.Fori(0, AHEAD) as i:
                load_group(i)
            with sp.Fori(AHEAD, LOOPS) as i:
                load_group(i)
                store_sums(i - AHEAD, sums0, sums_by_edge, sums0_ready, sums0_out)
            with sp.Fori(LOOPS - AHEAD, LOOPS) as i:
                store_sums(i, sums0, sums_by_edge, sums0_ready, sums0_out)
            sp.wait_ge(table1_ready, 1)
            sp.dma_start(nodes_of(node_table1), dnode).then_inc(tables1, 16)
            sp.dma_start(nodes_of(src_table1), split_.rearrange("p (a c) -> p a c", a=A)).then_inc(tables1, 16)
            sp.wait_ge(scattered1, 16 * A)
            sp.wait_ge(sums0_out, 16 * LOOPS + 16)
            sp.dma_start(d16, edges_of(at_starts1)).then_inc(starts1, 16)
            sp.wait_ge(flags_ready, 1)
            with sp.Fori(0, LOOPS) as i:
                for q in range(RING):
                    hold(sp, src1_landed[q], 16 * TC * (i + 1))
                    sp.dma_start(gath1[:, bass.ds(16 * i + TC * q, TC), :], xs_words[:, q, :, :]).then_inc(src1_kept[q], 16)
            with sp.Fori(0, LOOPS) as i:
                store_sums(i, sums1, sums1_by_edge, sums1_ready, sums1_out)
            sp.wait_ge(result, 1)
            full = N // P
            sp.dma_start(out[0:full * P, :].rearrange("(a b) c -> b a c", b=P), hn[:, 0:full, :]).then_inc(written, 16)
            sp.dma_start(out[full * P:N, :], hn[0:N - full * P, full, :]).then_inc(written, 16)
            sp.wait_ge(written, 32)

        @block.gpsimd
        def _(pool):
            pool.memset(area_a[:], 0.0).then_inc(zero_set, 1)

            def gather_row(to, table, index, last_row, semaphore):
                pool.indirect_dma_start(to, None, table, bass.IndirectOffsetOnAxis(ap=index, axis=0),
                                        bounds_check=last_row, oob_is_err=False).then_inc(semaphore, 16)

            def gather_sources(table, ring, landed, first):
                with pool.Fori(0, LOOPS // 2) as i:
                    for half in range(2):
                        if first:
                            hold_pool(pool, turned, 2 * RING * i + RING * half + 1)
                        else:
                            hold_pool(pool, src1_kept[0], 16 * (2 * i + half) + 16)
                        pool.tensor_copy(idx_ring[:, half, :], src_s[:, bass.ds(32 * i + 16 * half, 16)]).then_inc(idx_copied[half], 1)
                        hold_pool(pool, idx_copied[half], i + 1 + (0 if first else LOOPS // 2))
                        for q in range(RING):
                            c = 2 * RING * i + RING * half + q
                            if first:
                                hold_pool(pool, turned, c + 1)
                            else:
                                hold_pool(pool, src1_kept[q], 16 * (2 * i + half) + 16)
                            for t in range(TC):
                                gather_row(ring[:, q, t, :], table, idx_ring[:, half, TC * q + t:TC * q + t + 1],
                                           NP - 1, landed[q])

            pool.wait_ge(emb_hi, 1)
            pool.tensor_tensor(emb_s, emb_s, emb_parts_s[:, 0, :], ALU.subtract).then_inc(emb_rest, 1)
            pool.wait_ge(emb_mid, 1)
            pool.tensor_tensor(emb_parts_s[:, 2, :], emb_s, emb_parts_s[:, 1, :], ALU.subtract).then_inc(emb_lo, 1)
            pool.wait_ge(tables0, 32)
            gather_row(carry_in[:], node_table0, dst_s[:, 0:1], NP - 1, carry0)
            pool.wait_ge(bounds_ready, 1)
            pool.wait_ge(zeroed, 32)
            for a in range(A):
                pool.indirect_dma_start(at_starts0, bass.IndirectOffsetOnAxis(ap=start_i[:, a:a + 1], axis=0), hn[:, a, :],
                                        None, bounds_check=EP - 1, oob_is_err=False).then_inc(scattered0, 16)
            pool.wait_ge(consts, CONSTS)
            gather_sources(src_table0, xs_ring[:, :, :, 0:S3], src_landed, True)
            pool.wait_ge(sums0_out, 16 * LOOPS + 16)
            pool.wait_ge(agg_set, 1)
            for a in range(A):
                gather_row(agg[:, a, 0:C], sums0, end_i[:, a:a + 1], EP - 1, ended0)
            pool.wait_ge(tables1, 32)
            gather_row(carry_in[:, 0:16], node_table1, dst_s[:, 0:1], NP - 1, carry1)
            for a in range(A):
                pool.indirect_dma_start(at_starts1, bass.IndirectOffsetOnAxis(ap=start_i[:, a:a + 1], axis=0), dnode[:, a, :],
                                        None, bounds_check=EP - 1, oob_is_err=False).then_inc(scattered1, 16)
            gather_sources(src_table1, xs_words, src1_landed, False)
            pool.wait_ge(inverse_ready, 1)
            pool.tensor_tensor(self1, self1, seg, ALU.mult).then_inc(self_ready, 1)
            with pool.Fori(0, LOOPS // 2) as i:
                for half, q in [(half, q) for half in range(2) for q in range(RING)]:
                    c = 2 * RING * i + RING * half + q
                    heads, to = prod1[:, q], (msg, msg_odd)[half]
                    hold_pool(pool, prod1_done, c + 3)
                    pool.tensor_tensor(heads[:, HALVED:TC, 0:4, :], heads[:, HALVED:TC, 0:4, :], heads[:, HALVED:TC, 4:8, :], ALU.add).then_inc(halved1, 1)
                    hold_pool(pool, halved1, 2 * c + 1)
                    hold_pool(pool, first_halved1, c + 1)
                    pool.tensor_tensor(heads[:, :, 0:2, :], heads[:, :, 0:2, :], heads[:, :, 2:4, :], ALU.add).then_inc(halved1, 1)
                    hold_pool(pool, halved1, 2 * c + 2)
                    if q == 0:
                        hold_pool(pool, msg1_used, 2 * i + half + 1)
                    pool.tensor_tensor(to[:, :, 1 + TC * q:1 + TC * q + TC].rearrange("p c t -> p t c"),
                                       heads[:, :, 0, :], heads[:, :, 1, :], ALU.add).then_inc(heads1_summed, 1)
            pool.wait_ge(agg_set, 2)
            pool.wait_ge(sums1_out, 16 * LOOPS + 16)
            for a in range(A):
                gather_row(agg[:, a, :], sums1, end_i[:, a:a + 1], EP - 1, ended1_first if a < OWN else ended1)
            pool.wait_ge(own_out, -(-A // 2))
            pool.wait_ge(ended1, 16 * (A - OWN))
            own_messages(pool, slice(OWN, A)).then_inc(own_summed, 1)
            for k, h in enumerate((4, 2, 1)):
                pool.wait_ge(own_summed, k + 1)
                pool.tensor_tensor(xself[:, OWN:A, 0:h, :], xself[:, OWN:A, 0:h, :], xself[:, OWN:A, h:2 * h, :], ALU.add).then_inc(own_summed, 1)

        @block.vector
        def _(dve):
            step = Steps(dve, dve_step)
            roots = [0]
            across = lambda v, n=C: v.unsqueeze(2).to_broadcast([P, A, n])
            row = lambda v: v.unsqueeze(1).to_broadcast([P, A, C])

            def root():
                roots[0] += 1
                dve.wait_ge(root_ready, roots[0])

            def layer_norm(to, of, scratch):
                step(dve.reduce_sum(st[:, 0, :], of, AX.X))
                step(dve.tensor_scalar(st[:, 0, :], st[:, 0, :], -1.0 / C, None, ALU.mult))
                step(dve.tensor_tensor(scratch, of, across(st[:, 0, :]), ALU.add))
                step(dve.tensor_tensor(to, scratch, scratch, ALU.mult))
                dve.reduce_sum(st[:, 1, :], to, AX.X).then_inc(var_ready, 1)
                root()
                step(dve.reciprocal(st[:, 3, :], st[:, 2, :]))
                step(dve.tensor_tensor(to, scratch, across(st[:, 3, :]), ALU.mult))

            def split(parts, of, scratch):
                step(dve.tensor_copy(parts[0], of))
                step(dve.tensor_tensor(scratch, of, parts[0], ALU.subtract))
                step(dve.tensor_copy(parts[1], scratch))
                step(dve.tensor_tensor(scratch, scratch, parts[1], ALU.subtract))
                return dve.tensor_copy(parts[2], scratch)

            three = lambda v: [v[:, :, C * k:C * (k + 1)] for k in range(3)]

            step(dve.memset(eps_s[:], LN_EPS))
            step(dve.memset(ones_s[:], 1.0))
            step(dve.memset(zerob[:], 0.0))
            step(dve.memset(carry_in[:], 0.0))
            dve.memset(agg[:], 0.0).then_inc(agg_set, 1)

            dve.wait_ge(x_in, 16)
            layer_norm(hn[:], xn[:], nt[:])
            step(dve.tensor_scalar(hn[:], hn[:], 0.0, None, ALU.max))
            split(three(hsp), hn[:], nt[:]).then_inc(table0_ready, 1)

            dve.wait_ge(dst_in, 16)
            target = dst_s[:, 1:J + 1]
            dve.wait_ge(consts, CONSTS)
            step(dve.tensor_tensor(same_prev[:], target, dst_s[:, 0:J], ALU.is_equal))
            step(dve.tensor_tensor(same_next[:], target, dst_s[:, 2:J + 2], ALU.is_equal))
            step(dve.tensor_scalar(lo_i, target, B64 - 1, None, ALU.bitwise_and))
            step(dve.tensor_scalar(hi_i, target, B64.bit_length() - 1, None, ALU.logical_shift_right))
            step(dve.tensor_copy(lo_bf, lo_i))
            step(dve.tensor_copy(hi_bf, hi_i))
            step(dve.tensor_copy(iota_x, iota_s[:, 0:B64].unsqueeze(2).to_broadcast([P, B64, 8])))
            with dve.Fori(0, J // 32) as i:
                for slot in range(4):
                    dve.wait_ge(onehot_used, 4 * i + slot + 1)
                    dve.tensor_tensor(onehot_hi[:, slot, :, :], iota_x[:, 0:2 * A, :],
                                      hi_bf[:, bass.ds(32 * i + 8 * slot, 8)].unsqueeze(1).to_broadcast([P, 2 * A, 8]),
                                      ALU.is_equal).then_inc(onehot_ready, 1)
                    dve.tensor_tensor(onehot_lo[:, slot, :, :], iota_x,
                                      lo_bf[:, bass.ds(32 * i + 8 * slot, 8)].unsqueeze(1).to_broadcast([P, B64, 8]),
                                      ALU.is_equal).then_inc(onehot_ready, 1)
            step(dve.tensor_scalar(lo_i[:, 0:1], target[:, J - 1:J], P - 1, None, ALU.bitwise_and))
            step(dve.tensor_scalar(hi_i[:, 0:1], target[:, J - 1:J], P.bit_length() - 1, None, ALU.logical_shift_right))
            step(dve.tensor_copy(endf[:, 0:1], lo_i[:, 0:1]))
            step(dve.tensor_copy(endf[:, 1:2], hi_i[:, 0:1]))
            step(dve.tensor_scalar(e_lo[:], iota_s, endf[:, 0:1], same_next[:, J - 1:J], ALU.is_equal, ALU.mult))
            step(dve.tensor_scalar(e_hi[:], iota_s[:, 0:A], endf[:, 1:2], None, ALU.is_equal))

            dve.wait_ge(hist_done, 1)
            dve.wait_ge(zeroed, 32)
            step(dve.memset(hist_rows, 0.0))
            for k in range(2):
                ins = dve.tensor_copy(hist_rows[:, k, B64 * k:B64 * k + B64], po[0:2 * A, 0:B64])
            ins.then_inc(hist_out, 1)
            dve.wait_ge(hist_turned, 1)
            dve.tensor_copy(hist[:], hp[:, 64:64 + A]).then_inc(hist_copied, 1)
            dve.wait_ge(hist_copied, 1)
            dve.wait_ge(cum_done, 1)
            step(dve.tensor_tensor_scan(st[:, 0, :], ones_s[:, 0:A], hp[:, 32:32 + A], 0.0, ALU.mult, ALU.add))
            step(dve.tensor_tensor(st[:, 0, :], st[:, 0, :], hp[:, 32:32 + A], ALU.subtract))
            step(dve.tensor_tensor(st[:, 0, :], st[:, 0, :], hp[:, 0:A], ALU.add))
            step(dve.tensor_scalar(st[:, 1, :], hist[:], 0.0, NOWHERE, ALU.is_equal, ALU.mult))
            step(dve.tensor_tensor(st[:, 2, :], st[:, 0, :], hist[:], ALU.subtract))
            step(dve.tensor_tensor(start_i[:], st[:, 2, :], st[:, 1, :], ALU.add))
            dve.scalar_tensor_tensor(out=end_i[:], in0=st[:, 0, :], scalar=-1.0, in1=st[:, 1, :],
                                     op0=ALU.add, op1=ALU.add).then_inc(bounds_ready, 1)
            dve.wait_ge(bounds_ready, 1)

            step(dve.tensor_tensor(r_, nvec[:, 0, :], nvec[:, 0, :], ALU.mult))
            for k in (1, 2):
                step(dve.tensor_tensor(dlo_, nvec[:, k, :], nvec[:, k, :], ALU.mult))
                ins = dve.tensor_tensor(r_, r_, dlo_, ALU.add)
                if k == 1:
                    step(ins)
            ins.then_inc(var_ready, 1)
            root()
            step(dve.reciprocal(dlo_, r_))
            step(dve.tensor_tensor(nvec, nvec, dlo_.unsqueeze(1).to_broadcast([P, 3, J]), ALU.mult))
            step(dve.tensor_scalar(wt_, wt_, TANH_GAIN, None, ALU.mult))
            step(dve.tensor_scalar(w2_s[:, :, 48:56], w2_s[:, :, 48:56], PW_V / 3 ** 0.5, None, ALU.mult))
            step(dve.scalar_tensor_tensor(out=w2_s[:, :, 48:56], in0=w2_s[:, :, 40:48], scalar=-PW_V / 6 ** 0.5,
                                          in1=w2_s[:, :, 48:56], op0=ALU.mult, op1=ALU.add))
            step(dve.tensor_scalar(w2_s[:, :, 40:48], w2_s[:, :, 40:48], PW_V * 1.5 ** 0.5, None, ALU.mult))
            step(dve.tensor_scalar(w2_s[:, :, 16:24], w2_s[:, :, 16:24], PW_V, None, ALU.mult))

            step(dve.tensor_copy(w1_parts[:, 0, :], w1_s[:]))
            step(dve.tensor_tensor(w1_rest, w1_s[:], w1_parts[:, 0, :], ALU.subtract))
            step(dve.tensor_copy(w1_parts[:, 1, :], w1_rest))
            step(dve.tensor_tensor(w1_parts[:, 2, :], w1_rest, w1_parts[:, 1, :], ALU.subtract))
            dve.wait_ge(embs_out, 96)
            step(dve.tensor_scalar(w1_s[:], w1_parts[:, 0, :], which_s[:, 0:1], None, ALU.mult))
            for k in (1, 2):
                step(dve.scalar_tensor_tensor(out=w1_s[:], in0=w1_parts[:, k, :], scalar=which_s[:, k:k + 1], in1=w1_s[:],
                                              op0=ALU.mult, op1=ALU.add))
            step(dve.tensor_copy(w1b_s, w1_s[:]))
            step(dve.memset(w2_wide, 0.0))
            for u in range(4):
                lo, hi = (0, 24) if u == 0 else (24, 56)
                ins = dve.tensor_copy(w2_wide[:, u, :, 32 * u:32 * u + hi - lo], w2_s[:, :, lo:hi])
            ins.then_inc(wide_ready, 1)
            step(dve.memset(runmask[:, :, 0:1], 0.0))
            dve.wait_ge(carry0, 16)
            step(dve.tensor_copy(runs[:, :, 16:17], carry_in[:].unsqueeze(2)))

            x_dst, x_dst_rest = runs[:, :, 1:17].rearrange("p c j -> p j c"), rest_.rearrange("p (j c) -> p j c", c=C)
            dst_parts = xd_ring.rearrange("p q t c -> p (q t) c")

            def load_starts(i):
                dve.wait_ge(starts_landed, 16 * i + 16)
                step(dve.tensor_copy(runs[:, :, 0:1], runs[:, :, 16:17]))
                dve.tensor_copy(x_dst, starts_in).then_inc(starts_used, 1)

            def mask_starts(i):
                step(dve.tensor_copy(runmask[:, :, 1:17], same_prev[:, bass.ds(16 * i, 16)].unsqueeze(1).to_broadcast([P, C, 16])))

            def spread_starts(i):
                dve.wait_ge(starts_used, i + 2)
                step(dve.tensor_tensor_scan(runs_, runmask_, runs_, 0.0, ALU.mult, ALU.add))

            def first_dst_part(i):
                dve.wait_ge(turned, RING * i + RING)
                step(dve.tensor_copy(dst_parts[:, :, 0:C], x_dst))

            def other_dst_parts():
                step(dve.tensor_tensor(x_dst_rest, x_dst, dst_parts[:, :, 0:C], ALU.subtract))
                step(dve.tensor_copy(dst_parts[:, :, C:2 * C], x_dst_rest))
                dve.tensor_tensor(dst_parts[:, :, 2 * C:S3], x_dst_rest, dst_parts[:, :, C:2 * C], ALU.subtract).then_inc(dst_ready, 1)

            def product(c, q, u):
                if u == 0:
                    dve.wait_ge(hidden_ready, c + 2)
                    dve.wait_ge(tiles_done, c + 1)
                dve.wait_ge(rep_ready, 4 * c + u + 1)
                dve.tensor_tensor(prod[:, q % 2, u, :, :], rep[:, u % 2, :, :],
                                  hid[:, q % 2, :].unsqueeze(1).to_broadcast([P, 2, CE]), ALU.mult).then_inc(prod_done, 1)

            tiles = lambda g: bass.ds(PT * g, PT)
            n_of = lambda g: nvec[:, :, tiles(g)].rearrange("p i t -> p t i").unsqueeze(3)
            weight_of = lambda g: wt_[:, tiles(g)].unsqueeze(2)
            scalars = lambda half: tp_out[:, PT * half:PT * half + PT, 0:24]
            vectors = lambda half: tp_out[:, PT * half:PT * half + PT, 32:128].rearrange("p t (i w) -> p t i w", i=3)

            def along_n(g, half):
                dve.wait_ge(tiles_out, 2 * g + 5)
                step(dve.tensor_tensor(tmp, vectors(half)[:, :, :, 0:24], n_of(g).to_broadcast([P, PT, 3, 24]), ALU.mult))

            def scalar_sums(half):
                step(dve.tensor_tensor(acc, scalars(half), tmp[:, :, 0, :], ALU.add))
                step(dve.tensor_tensor(acc, acc, tmp[:, :, 1, :], ALU.add))
                dve.tensor_tensor(acc, acc, tmp[:, :, 2, :], ALU.add).then_inc(gates_in, 1)

            def vector_sums(g, half):
                dve.wait_ge(gates_in, g + 1)
                step(dve.tensor_tensor(vbuf, n_of(g).to_broadcast([P, PT, 3, 8]),
                                       acc[:, :, 16:24].unsqueeze(2).to_broadcast([P, PT, 3, 8]), ALU.mult))
                dve.tensor_tensor(vbuf, vbuf, vectors(half)[:, :, :, 24:32], ALU.add).then_inc(post_read, 1)

            def messages(g, half):
                dve.wait_ge(gates_out, g + 1)
                step(dve.tensor_tensor(sgn, sg[:, :, 8:16], weight_of(g).to_broadcast([P, PT, 8]), ALU.mult))
                dve.wait_ge(post_read, g + 3)
                to = msg[:, :, 1 + PT * half:1 + PT * half + PT].rearrange("p c t -> p t c")
                dve.tensor_tensor(to[:, :, 0:8], sg[:, :, 0:8], weight_of(g).to_broadcast([P, PT, 8]), ALU.mult)
                step(dve.tensor_tensor(to[:, :, 8:32].rearrange("p t (w k) -> p t k w", k=3), vbuf,
                                       sgn.unsqueeze(2).to_broadcast([P, PT, 3, 8]), ALU.mult))

            def start_sums():
                step(dve.memset(msg[:, :, 0:1], 0.0))
                step(dve.memset(msgmask[:, :, 0:1], 0.0))

            def running_sums0(i):
                step(dve.tensor_copy(msgmask[:, :, 1:17], same_prev[:, bass.ds(16 * i, 16)].unsqueeze(1).to_broadcast([P, C, 16])))
                step(dve.tensor_tensor_scan(msg_, msgmask_, msg_, 0.0, ALU.mult, ALU.add))

            def store_sums0(i):
                dve.wait_ge(sums0_out, 16 * i + 16)
                step(dve.tensor_copy(msg[:, :, 0:1], msg[:, :, 16:17]))
                dve.tensor_copy(sums_by_edge, msg[:, :, 1:17].rearrange("p c j -> p j c")).then_inc(sums0_ready, 1)

            def running_sums1(g, half):
                of, of_, following = ((msg, msg_, msg_odd), (msg_odd, msg_odd_, msg))[half]
                dve.wait_ge(heads1_summed, RING * g + 2 * RING)
                dve.wait_ge(masks1, g + 1)
                dve.wait_ge(scanned1, g + 1)
                step(dve.tensor_tensor_scan(of_, (msgmask_, mask_odd_)[half], of_, 0.0, ALU.mult, ALU.add))
                dve.tensor_copy(following[:, :, 0:1], of[:, :, 16:17]).then_inc(scanned1, 1)

            def group(i, first=False, final=False):
                c = RING * i
                product(c, 0, 0)
                if not final:
                    load_starts(i + 1)
                product(c, 0, 1)
                if not first:
                    messages(2 * i - 2, 0)
                product(c, 0, 2)
                if not final:
                    mask_starts(i + 1)
                product(c, 0, 3)
                if not final:
                    spread_starts(i + 1)

                product(c + 1, 1, 0)
                if not first:
                    along_n(2 * i - 1, 1)
                product(c + 1, 1, 1)
                if not first:
                    scalar_sums(1)
                product(c + 1, 1, 2)
                if not first:
                    vector_sums(2 * i - 1, 1)
                product(c + 1, 1, 3)

                product(c + 2, 2, 0)
                product(c + 2, 2, 1)
                if not first:
                    messages(2 * i - 1, 1)
                product(c + 2, 2, 2)
                if not final:
                    first_dst_part(i + 1)
                product(c + 2, 2, 3)
                if not final:
                    other_dst_parts()

                product(c + 3, 3, 0)
                if not first:
                    running_sums0(i - 1)
                along_n(2 * i, 0)
                product(c + 3, 3, 1)
                scalar_sums(0)
                product(c + 3, 3, 2)
                vector_sums(2 * i, 0)
                product(c + 3, 3, 3)
                if not first:
                    store_sums0(i - 1)

            start_sums()
            load_starts(0)
            mask_starts(0)
            spread_starts(0)
            first_dst_part(0)
            other_dst_parts()
            group(0, first=True)
            base = step.count
            with dve.Fori(1, LOOPS - 1) as i:
                step.offset, step.count = (i - 1) * GROUP_STEPS, base
                group(i)
                assert step.count - base == GROUP_STEPS
            step.offset, step.count = 0, base + GROUP_STEPS * (LOOPS - 2)
            group(LOOPS - 1, final=True)
            messages(2 * LOOPS - 2, 0)
            along_n(2 * LOOPS - 1, 1)
            scalar_sums(1)
            vector_sums(2 * LOOPS - 1, 1)
            messages(2 * LOOPS - 1, 1)
            running_sums0(LOOPS - 1)
            store_sums0(LOOPS - 1)

            def last_edges(last_ready):
                step(dve.tensor_copy(last[:].unsqueeze(2), msg[:, :, 0:1]))
                dve.tensor_tensor(nt[:], last[:].unsqueeze(1).to_broadcast([P, A, C]), across(e_hi[:]), ALU.mult).then_inc(last_ready, 1)

            def add_carried(to, n):
                dve.wait_ge(carried, n)
                for k in range(2):
                    half = to.rearrange("p a c -> p (a c)")[:, A * C // 2 * k:A * C // 2 * (k + 1)]
                    ins = dve.tensor_tensor(half, half, (po, hp)[k][:, 0:A * C // 2], ALU.add)
                step(ins)

            dve.wait_ge(sums0_ready, LOOPS)
            last_edges(last0)
            add_carried(xn[:], 1)
            dve.wait_ge(ended0, 16 * A)
            step(dve.tensor_tensor(xn[:], xn[:], agg[:, :, 0:C], ALU.add))

            layer_norm(hn[:], xn[:], nt[:])
            dve.tensor_scalar(hn[:], hn[:], 0.0, None, ALU.max).then_inc(nodes_in, 1)
            dve.wait_ge(nodes_in, 1)
            for k in range(2):
                step(dve.tensor_tensor(att_s[:, k, :], att_s[:, k, :], wgat_s[0:C, :], ALU.mult))
                ins = dve.reduce_sum(vatt[:, 8 * k:8 * k + 8], att_s[:, k, :].rearrange("p (h c) -> p h c", c=C), AX.X)
            ins.then_inc(vatt_ready, 1)
            step(split(three(hsp), hn[:], nt[:]))
            dve.memset(agg[:, :, 0:C], 0.0)
            dve.memset(agg[:, :, C:C + HEADS], 1.0).then_inc(agg_set, 1)
            dve.wait_ge(att_done, 1)
            att_ps = po[:, 0:A * 16].rearrange("p (a h) -> p a h", h=16)
            step(dve.tensor_copy(asrc_n, att_ps[:, :, 0:8]))
            step(dve.tensor_copy(dnode[:, :, 0:8], att_ps[:, :, 8:16]))
            dve.tensor_tensor(dnode[:, :, 8:16], asrc_n, att_ps[:, :, 8:16], ALU.add).then_inc(table1_ready, 1)

            first_t, last_t, prev_t, next_t = (ends_s[:, k, :] for k in range(4))
            step(dve.tensor_tensor(flags[:, 2, :], first_t, last_t, ALU.is_equal))
            for k, (own, other) in enumerate(((first_t, prev_t), (last_t, next_t))):
                step(dve.tensor_tensor(flags[:, k, :], own, other, ALU.is_equal))
                step(dve.tensor_tensor(flags[:, k, :], flags[:, k, :], flags[:, 2, :], ALU.mult))
            for k in range(2):
                ins = dve.tensor_scalar(flags[:, 2 + k, :], flags[:, k, :], -1.0, BIG, ALU.add, ALU.mult)
            ins.then_inc(flags_ready, 1)
            dve.wait_ge(flags_ready, 1)

            carries = [0]

            MAXIMUM = (ALU.add, ALU.max, -BIG)
            SUM = (ALU.mult, ALU.add, 0.0)
            TOTAL = (ALU.mult, ALU.max, 0.0)

            def carry(values, forward, kind):
                step(dve.tensor_copy(car_l, values))
                *ops, init = kind
                flag = flags[:, (2 if kind == MAXIMUM else 0) + (0 if forward else 1), :]
                end = slice(0, 1) if forward else slice(P - 1, P)
                dve.memset(car_t[:, end], init).then_inc(ends_in, 1)
                carries[0] += 1
                dve.wait_ge(ends_turned, carries[0])
                if forward:
                    ins = dve.tensor_tensor_scan(car_t[:, 1:P], flag[:, 0:P - 1], hp[0:HEADS, 0:P - 1], init, *ops)
                else:
                    ins = dve.tensor_tensor_scan(car_t[:, P - 2::-1], flag[:, P - 1:0:-1], hp[0:HEADS, P - 1:0:-1], init, *ops)
                ins.then_inc(ends_back, 1)
                dve.wait_ge(ends_done, carries[0])
                step(dve.tensor_copy(car_l, hp[:, P:P + HEADS]))

            def scan_heads(to, mask, of, forward, kind, initial=None, columns=slice(None)):
                *ops, start = kind
                d = columns if forward else slice(None, None, -1)
                for h in range(HEADS):
                    ins = dve.tensor_tensor_scan(to[:, d, h], mask[:, d], of[:, d, h],
                                                 start if initial is None else initial[:, h:h + 1], *ops)
                step(ins)

            step(dve.tensor_scalar(wrest_s, wgat_s[:], 1.0 / HEADS, None, ALU.mult))
            for k in range(3):
                step(dve.tensor_copy(wval_s[:, k, :], wrest_s))
                if k < 2:
                    step(dve.tensor_tensor(wrest_s, wrest_s, wval_s[:, k, :], ALU.subtract))
            for k in range(2):
                step(dve.tensor_scalar(wval_s[:, k, :], wval_s[:, k, :], meets_s[:, k:k + 1], None, ALU.mult))
            step(dve.scalar_tensor_tensor(out=wval_s[:, 0, :], in0=wval_s[:, 2, :], scalar=meets_s[:, 2:3], in1=wval_s[:, 0, :],
                                          op0=ALU.mult, op1=ALU.add))
            dve.wait_ge(starts1, 16)
            dve.wait_ge(carry1, 16)
            for h in range(2 * HEADS):
                ins = dve.tensor_tensor_scan(d16[:, :, h], same_prev[:], d16[:, :, h], carry_in[:, h:h + 1], ALU.mult, ALU.add)
            step(ins)
            leaky = lambda v: dve.scalar_tensor_tensor(out=v, in0=v, scalar=0.2, in1=v, op0=ALU.mult, op1=ALU.max)
            step(dve.tensor_copy(self1, d16[:, :, 8:16]))
            step(leaky(self1))
            step(dve.tensor_scalar(pen[:], same_prev[:], -1.0, BIG, ALU.add, ALU.mult))
            for first, end in ((0, J - 16), (J - 16, J)):
                for q in range(RING):
                    dve.wait_ge(src1_kept[q], end + 16)
                part = slice(first, end)
                step(dve.tensor_tensor(alpha[:, part, :], asrc_e[:, part, :], d16[:, part, 0:8], ALU.add))
                step(leaky(alpha[:, part, :]))
                step(dve.tensor_tensor(seg[:, part, :], alpha[:, part, :], self1[:, part, :], ALU.max))
                scan_heads(tmp8, pen, seg, True, MAXIMUM, tmp8[:, first - 1, :] if first else None, part)
            carry(tmp8[:, J - 1, :], True, MAXIMUM)
            scan_heads(seg, pen, seg, True, MAXIMUM, car_l)
            step(dve.tensor_scalar(pen[:], same_next[:], -1.0, BIG, ALU.add, ALU.mult))
            scan_heads(tmp8, pen, seg, False, MAXIMUM)
            carry(tmp8[:, 0, :], False, MAXIMUM)
            scan_heads(seg, pen, seg, False, MAXIMUM, car_l)
            dve.tensor_tensor(alpha, alpha, seg, ALU.subtract).then_inc(exp_in, 1)
            dve.tensor_tensor(self1, self1, seg, ALU.subtract).then_inc(exp_in, 1)
            dve.wait_ge(exp_out, 1)
            scan_heads(tmp8, same_prev, alpha, True, SUM)
            carry(tmp8[:, J - 1, :], True, SUM)
            dve.wait_ge(exp_in, 2)
            scan_heads(seg, same_prev, alpha, True, SUM, car_l)
            scan_heads(tmp8, same_next, seg, False, TOTAL)
            carry(tmp8[:, 0, :], False, TOTAL)
            scan_heads(seg, same_next, seg, False, TOTAL, car_l)
            dve.wait_ge(exp_out, 2)
            step(dve.scalar_tensor_tensor(out=seg, in0=seg, scalar=1e-16, in1=self1, op0=ALU.add, op1=ALU.add))
            dve.reciprocal(seg, seg).then_inc(inverse_ready, 1)
            dve.wait_ge(inverse_ready, 1)
            dve.tensor_tensor(alpha, alpha, seg, ALU.mult).then_inc(attn_ready, 1)
            dve.wait_ge(attn_ready, 1)

            start_sums()
            dve.memset(mask_odd[:, :, 0:1], 0.0).then_inc(mask_columns, 1)

            def group1(g, half, first=False):
                for q in range(RING):
                    c = RING * g + q
                    heads = prod1[:, q]
                    dve.wait_ge(heads1_summed, c + 1)
                    dve.wait_ge(values1, c + 3)
                    dve.tensor_tensor(heads, rep[:, q % 2].rearrange("p g (t h c) -> p (g t) h c", h=HEADS, c=C),
                                      alpha[:, bass.ds(16 * g + TC * q, TC), :].unsqueeze(3).to_broadcast([P, TC, HEADS, C]),
                                      ALU.mult).then_inc(prod1_done, 1)
                    dve.wait_ge(prod1_done, c + 3)
                    dve.tensor_tensor(heads[:, 0:HALVED, 0:4, :], heads[:, 0:HALVED, 0:4, :], heads[:, 0:HALVED, 4:8, :], ALU.add).then_inc(first_halved1, 1)
                    if q == 1 and not first:
                        running_sums1(g - 1, 1 - half)

            group1(0, 0, first=True)
            group1(1, 1)
            base = step.count
            with dve.Fori(1, LOOPS // 2) as i:
                step.offset, step.count = (i - 1) * 2, base
                group1(2 * i, 0)
                group1(2 * i + 1, 1)
                assert step.count - base == 2
            step.offset, step.count = 0, base + 2 * (LOOPS // 2 - 1)
            running_sums1(LOOPS - 1, 1)
            dve.wait_ge(scanned1, LOOPS + 1)
            last_edges(last1)

            flat_nodes = lambda v: v[:].rearrange("p a c -> p (a c)")
            dve.wait_ge(nodes_turned, 2 * GROUPS)
            step(dve.tensor_tensor(hn[:], hn[:], row(bias_g), ALU.add))
            add_carried(hn[:], 2)
            dve.wait_ge(own_out, -(-A // 2))
            dve.wait_ge(ended1_first, 16 * OWN)
            step(own_messages(dve, slice(0, OWN)))
            step(dve.reduce_sum(nt[:, 0:OWN, :], xself[:, 0:OWN].rearrange("p a h c -> p a c h"), AX.X))
            dve.wait_ge(own_summed, 4)
            dve.wait_ge(ended1, 16 * (A - OWN))
            step(dve.tensor_copy(nt[:, OWN:A, :], xself[:, OWN:A, 0, :]))
            step(dve.scalar_tensor_tensor(out=flat_nodes(nt), in0=flat_nodes(nt), scalar=1.0 / HEADS, in1=flat_nodes(hn), op0=ALU.mult, op1=ALU.add))
            step(dve.tensor_tensor(nt[:], nt[:], agg[:, :, 0:C], ALU.add))
            layer_norm(hn[:], nt[:], agg[:, :, 0:C])
            step(dve.tensor_tensor(hn[:], hn[:], row(g1_r), ALU.mult))
            dve.tensor_tensor(hn[:], hn[:], row(be1_r), ALU.add).then_inc(nodes_in, 1)
            dve.wait_ge(nodes_in, 2)
            dve.wait_ge(nodes_turned, 3 * GROUPS)
            step(dve.tensor_tensor(hn[:], hn[:], row(b2_r), ALU.add))
            dve.wait_ge(ffn2_done, 1)
            step(dve.tensor_tensor(flat_nodes(nt), flat_nodes(hn), rep[:, 0, :, :].rearrange("p g e -> p (g e)")[:, 0:A * C], ALU.add))
            layer_norm(hn[:], nt[:], agg[:, :, 0:C])
            step(dve.tensor_tensor(hn[:], hn[:], row(g2_r), ALU.mult))
            step(dve.tensor_tensor(hn[:], hn[:], row(be2_r), ALU.add))
            dve.tensor_tensor(hn[:], hn[:], xn[:], ALU.add).then_inc(result, 1)

        @block.scalar
        def _(act):
            roots = [0]

            def root_of(to, of, scale, bias):
                roots[0] += 1
                act.wait_ge(var_ready, roots[0])
                act.activation(to, of, ACT.Sqrt, scale=scale, bias=bias).then_inc(root_ready, 1)

            variance_root = lambda: root_of(st[:, 2, :], st[:, 1, :], 1.0 / C, eps_s[:])

            def nodes_to_sbuf(first):
                for g in range(GROUPS):
                    n = min(CE, NP - CE * g)
                    act.wait_ge(nodes_turned, first + g + 1)
                    act.activation(node_t[:, CE * g:CE * g + n], tp[0:C, g % 2, 0:n], ACT.Copy).then_inc(nodes_out, 1)

            act.sem_inc(turned_out, 1)
            act.sem_inc(hidden_ready, 1)
            act.sem_inc(tiles_out, 3)
            act.sem_inc(features_out, 2)
            act.sem_inc(turned1_out, 2)
            act.sem_inc(values1, 2)
            act.sem_inc(heads1_summed, RING)
            act.sem_inc(post_read, 2)
            act.sem_inc(starts_used, 1)
            act.sem_inc(sums0_out, 16)
            act.sem_inc(sums1_out, 16)
            act.sem_inc(msg1_used, 2)
            act.sem_inc(scanned1, 1)
            act.sem_inc(prod_done, 8)
            act.sem_inc(prod1_done, 2)
            variance_root()
            act.wait_ge(emb_in, 16)
            act.activation(emb_parts_s[:, 0, :], emb_s, ACT.Copy).then_inc(emb_hi, 1)
            act.wait_ge(emb_rest, 1)
            act.activation(emb_parts_s[:, 1, :], emb_s, ACT.Copy).then_inc(emb_mid, 1)
            roots[0] += 1
            act.wait_ge(var_ready, roots[0])
            act.activation(r_, r_, ACT.Sqrt).then_inc(root_ready, 1)
            def open_chunk(c, s):
                hold(act, turned, c + 1 + RING)
                act.activation(x_t[0:S3, s, :, :], tpb[0:S3, 0, :, :], ACT.Copy).then_inc(turned_out, 1)
                hold(act, prod_done, 4 * c + 4)
                hold(act, hidden_done, c + 1 + RING)
                act.activation(hid[:, s, :], hp[:], ACT.Relu, scale=(2.0 / 10.0 / K) ** 0.5).then_inc(hidden_ready, 1)

            def tiles_to_sbuf(c, q, pair_read):
                if pair_read is not None:
                    hold(act, post_read, pair_read)
                hold(act, tiles_back, c + 1)
                act.activation(tp_out[:, TC * q:TC * q + TC, :], hp[:].rearrange("p (t c) -> p t c", c=P), ACT.Copy).then_inc(tiles_out, 1)

            def gates(g):
                hold(act, gates_in, g + 1)
                act.activation(sg, acc[:, :, 0:16], ACT.Tanh, scale=PW_S).then_inc(gates_out, 1)

            def group(i, first, final):
                for q in range(RING):
                    c = RING * i + q
                    if not (final and q == RING - 1):
                        open_chunk(c + 1, (q + 1) % 2)
                    if not (first and q == 0):
                        tiles_to_sbuf(c - 1, (q - 1) % RING, {1: 2 * i + 1, 3: 2 * i + 2}.get(q))
                    if q == 3 or (q == 1 and not first):
                        gates(2 * i - 1 if q == 1 else 2 * i)
                    hold(act, tiles_done, c + 3)
                    act.activation(by_feature[:, q % 2, :], po2[q % 2], ACT.Copy).then_inc(features_out, 1)

            open_chunk(0, 0)
            group(0, True, False)
            with act.Fori(1, LOOPS - 1) as i:
                group(i, False, False)
            group(LOOPS - 1, False, True)
            tiles_to_sbuf(NCH - 1, RING - 1, None)
            gates(2 * LOOPS - 1)

            variance_root()
            nodes_to_sbuf(0)
            act.wait_ge(exp_in, 1)
            act.activation(alpha, alpha, ACT.Exp).then_inc(exp_out, 1)
            act.wait_ge(exp_in, 2)
            act.activation(self1, self1, ACT.Exp).then_inc(exp_out, 1)
            act.wait_ge(attn_ready, 1)
            act.wait_ge(mask_columns, 1)

            def mask1(g, half):
                act.activation((msgmask, mask_odd)[half][:, :, 1:17],
                               same_prev[:, bass.ds(16 * g, 16)].unsqueeze(1).to_broadcast([P, C, 16]), ACT.Copy).then_inc(masks1, 1)

            def take_sums1(g, half):
                hold(act, scanned1, g + 2)
                hold(act, sums1_out, 16 * g + 16)
                act.activation(sums1_by_edge[:, :, 0:C], (msg, msg_odd)[half][:, :, 1:17].rearrange("p c j -> p j c"),
                               ACT.Copy).then_inc(msg1_used, 1)
                hold(act, msg1_used, g + 3)
                act.activation(sums1_by_edge[:, :, C:C + HEADS], self1[:, bass.ds(16 * g, 16), :], ACT.Copy).then_inc(sums1_ready, 1)

            def two_groups1(i, first=False):
                for half, q in [(half, q) for half in range(2) for q in range(RING)]:
                    g = 2 * i + half
                    c = RING * g + q
                    if q == 0 and not first:
                        take_sums1(g - 2, half)
                    if q == 0:
                        mask1(g, half)
                    hold(act, values1, c + 1)
                    hold(act, turned1, c + 1)
                    act.activation(xt1_s[S3:P, q % 2, :], tpb[0:C, q % 2, 0, :], ACT.Copy)
                    act.activation(xt1_s[0:S3, q % 2, :], tpb[0:S3, q % 2, 0, :], ACT.Copy).then_inc(turned1_out, 1)

            two_groups1(0, first=True)
            act.wait_ge(self_ready, 1)
            with act.Fori(1, LOOPS // 2) as i:
                two_groups1(i)
            take_sums1(LOOPS - 2, 0)
            take_sums1(LOOPS - 1, 1)
            nodes_to_sbuf(GROUPS)
            for g in range(-(-A // 2)):
                n = min(2, A - 2 * g)
                act.wait_ge(own_done, g + 1)
                act.activation(xself_[:, 512 * g:512 * g + 256 * n], rep[:, g % 4 // 2, g % 2, 0:256 * n], ACT.Copy).then_inc(own_out, 1)
            variance_root()
            nodes_to_sbuf(2 * GROUPS)
            for g in range(GROUPS):
                n = min(CE, NP - CE * g)
                act.wait_ge(ffn_done, g + 1)
                act.activation(hid1_[:, CE * g:CE * g + n], tp[:, g % 2, 0:n], ACT.Relu, bias=b1_s[:]).then_inc(ffn_out, 1)
            variance_root()

        @block.tensor
        def _(pe):
            pe.sem_inc(onehot_used, 4)
            pe.sem_inc(turned, RING)
            pe.sem_inc(hidden_done, RING)
            pe.sem_inc(tiles_done, 2)
            pe.wait_ge(consts, CONSTS)
            pe.wait_ge(agg_set, 1)
            pe.matmul(po[0:2 * A, 0:B64], zerob[:, 0:2 * A], zerob[:, 0:B64], start=True, stop=False, skip_group_check=True)
            with pe.Fori(0, J // 32) as i:
                for slot in range(4):
                    pe.wait_ge(onehot_ready, 8 * i + 2 * slot + 2)
                    for t in range(8):
                        ins = pe.matmul(po[0:2 * A, 0:B64], onehot_hi[:, slot, :, t], onehot_lo[:, slot, :, t],
                                        start=False, stop=False, skip_group_check=True)
                    ins.then_inc(onehot_used, 1)
            pe.matmul(po[0:2 * A, 0:B64], zerob[:, 0:2 * A], zerob[:, 0:B64], start=False, stop=True, skip_group_check=True).then_inc(hist_done, 1)
            pe.wait_ge(hist_out, 1)
            for k in range(2):
                ins = pe.matmul(hp[:, 64:64 + A], hist_rows[:, k, :], ident_s[0:2 * A, k:2 * A:2], start=(k == 0), stop=(k == 1))
            ins.then_inc(hist_turned, 1)
            pe.wait_ge(hist_copied, 1)
            pe.matmul(hp[:, 0:A], tri_s, hist[:], start=True, stop=True)
            pe.matmul(hp[:, 32:32 + A], ones_s[:], hist[:], start=True, stop=True).then_inc(cum_done, 1)
            def turn(c, i, q):
                s = q % 2
                pe.wait_ge(turned_out, c + 1)
                pe.wait_ge(src_landed[q], 16 * TC * (i + 1))
                for t in range(TC):
                    pe.transpose(tpb[0:S3, 0, 0, P * t:P * t + P], xs_ring[:, q, t, 0:S3], identb_s[:])
                if q == 0:
                    pe.wait_ge(dst_ready, i + 1)
                for t in range(TC):
                    ins = pe.transpose(tpb[0:S3, 0, 1, P * t:P * t + P], xd_ring[:, q, t, :], identb_s[:])
                ins.then_inc(turned, 1)
                pe.wait_ge(tiles_out, c + 1)
                pe.wait_ge(emb_landed[q], 16 * (i + 1))
                pe.matmul(hp[:], w1b_s, emb_ring[:, q, :], start=True, stop=True).then_inc(hidden_done, 1)

            def repeat(c, q, u):
                if u == 0:
                    pe.wait_ge(turned_out, c + 2)
                pe.wait_ge(prod_done, 4 * c + u + 7)
                for d in range(2):
                    ins = pe.matmul(rep[:, u % 2, d, :], sel_s[:, u, :], x_t[0:S3, q % 2, d, :], start=True, stop=True)
                ins.then_inc(rep_ready, 1)

            def contract(c, q, u):
                pe.wait_ge(prod_done, 4 * c + u + 9)
                if u == 0:
                    pe.wait_ge(features_out, c + 1)
                for d in range(2):
                    ins = pe.matmul(po2[q % 2], w2_wide[:, u, d, :], prod[:, q % 2, u, d, :],
                                    start=(u == 0 and d == 0), stop=(u == 3 and d == 1))
                if u == 3:
                    ins.then_inc(tiles_done, 1)

            def turn_back(c, q, hidden):
                pe.wait_ge(features_out, c + 3)
                pe.wait_ge(hidden_ready, hidden + 2)
                for t in range(TC):
                    ins = pe.transpose(hp[:, P * t:P * t + P], by_feature[:, q % 2, P * t:P * t + P], ident_s[:])
                ins.then_inc(tiles_back, 1)

            def chunk0(c, i, q, first=False, final=False):
                contract(c, q, 0)
                repeat(c, q, 2)
                if not final:
                    turn(c + 1, i if q + 1 < RING else i + 1, (q + 1) % RING)
                contract(c, q, 1)
                repeat(c, q, 3)
                if not first:
                    turn_back(c - 1, (q - 1) % 2, c if final else c + 1)
                contract(c, q, 2)
                if not final:
                    repeat(c + 1, q + 1, 0)
                contract(c, q, 3)
                if not final:
                    repeat(c + 1, q + 1, 1)

            pe.wait_ge(wide_ready, 1)
            turn(0, 0, 0)
            repeat(0, 0, 0)
            repeat(0, 0, 1)
            for q in range(RING):
                chunk0(q, 0, q, first=q == 0)
            with pe.Fori(1, LOOPS - 1) as i:
                for q in range(RING):
                    chunk0(RING * i + q, i, q)
            for q in range(RING):
                chunk0(RING * (LOOPS - 1) + q, LOOPS - 1, q, final=q == RING - 1)
            turn_back(NCH - 1, (NCH - 1) % 2, NCH - 1)

            def carry_over(ready):
                pe.wait_ge(ready, 1)
                flat = nt[:].rearrange("p a c -> p (a c)")
                for k in range(2):
                    ins = pe.matmul((po, hp)[k][:, 0:A * C // 2], e_lo[:], flat[:, 400 * k:400 * k + 400], start=True, stop=True)
                ins.then_inc(carried, 1)

            def turn_nodes(first):
                for g in range(GROUPS):
                    pe.wait_ge(nodes_out, first + g - 1) if first + g > 1 else None
                    for a in range(4 * g, min(4 * g + 4, A)):
                        ins = pe.transpose(tp[0:C, g % 2, P * (a - 4 * g):P * (a - 4 * g) + P], hn[:, a, :], ident_s[:])
                    ins.then_inc(nodes_turned, 1)
                pe.wait_ge(nodes_out, first + GROUPS)

            carry_over(last0)
            pe.wait_ge(nodes_in, 1)
            turn_nodes(0)
            pe.wait_ge(vatt_ready, 1)
            for a in range(A):
                ins = pe.matmul(po[:, 16 * a:16 * a + 16], node_t[:, P * a:P * a + P], vatt[:], start=True, stop=True)
            ins.then_inc(att_done, 1)
            for k in range(4):
                pe.wait_ge(ends_in, k + 1)
                pe.transpose(hp[0:HEADS, 0:P], car_l, ident_s[:]).then_inc(ends_turned, 1)
                pe.wait_ge(ends_back, k + 1)
                pe.transpose(hp[:, P:P + HEADS], car_t, ident_s[0:HEADS, 0:HEADS]).then_inc(ends_done, 1)

            pe.wait_ge(attn_ready, 1)

            def turn1(c, i, q):
                pe.wait_ge(turned1_out, c + 1)
                for t in range(TC):
                    ins = pe.transpose(tpb[0:S3, q % 2, 0, P * t:P * t + P],
                                       gath1_bf[:, bass.ds(16 * i + TC * q + t, 1), 0:S3].squeeze(1), identb_s[:])
                ins.then_inc(turned1, 1)

            def values(c, q):
                pe.wait_ge(turned1_out, c + 3)
                pe.wait_ge(prod1_done, c + 1)
                for t in range(TC):
                    for k in range(2):
                        ins = pe.matmul(rep[:, q % 2, t // 2, 256 * (t % 2):256 * (t % 2) + 256],
                                        xt1_s[:, q % 2, P * t:P * t + P], wval_s[:, k, :], start=(k == 0), stop=(k == 1))
                ins.then_inc(values1, 1)

            turn1(0, 0, 0)
            with pe.Fori(0, LOOPS - 1) as i:
                for q in range(RING):
                    turn1(RING * i + q + 1, i + (q + 1) // RING, (q + 1) % RING)
                    values(RING * i + q, q)
            for q in range(RING):
                if q + 1 < RING:
                    turn1(RING * (LOOPS - 1) + q + 1, LOOPS - 1, q + 1)
                values(RING * (LOOPS - 1) + q, q)

            carry_over(last1)
            turn_nodes(GROUPS)
            for g in range(-(-A // 2)):
                if g >= 4:
                    pe.wait_ge(own_out, g - 3)
                for k in range(min(2, A - 2 * g)):
                    a = 2 * g + k
                    ins = pe.matmul(rep[:, g % 4 // 2, g % 2, 256 * k:256 * k + 256], node_t[:, P * a:P * a + P], wgat_s[0:C, :],
                                    start=True, stop=True)
                ins.then_inc(own_done, 1)
            pe.wait_ge(own_out, -(-A // 2))
            pe.wait_ge(nodes_in, 2)
            turn_nodes(2 * GROUPS)
            ff = rep[:, 0, :, :].rearrange("p g e -> p (g e)")
            for g in range(GROUPS + 1):
                if g < GROUPS:
                    n = min(CE, NP - CE * g)
                    if g >= 2:
                        pe.wait_ge(ffn_out, g - 1)
                    pe.matmul(tp[:, g % 2, 0:n], f1_s[:], node_t[:, CE * g:CE * g + n], start=True, stop=True).then_inc(ffn_done, 1)
                if g > 0:
                    pe.wait_ge(ffn_out, g)
                    for a in range(4 * g - 4, min(4 * g, A)):
                        ins = pe.matmul(ff[:, C * a:C * a + C], hid1_[:, P * a:P * a + P], f2_s[:], start=True, stop=True)
            ins.then_inc(ffn2_done, 1)


def kernel(x, src, dst, edge_attr_10, edge_attr_3, edge_weight, L0_gnn_W1, L0_gnn_W2, L1_gnn_W_gat, L1_gnn_att_src,
           L1_gnn_att_dst, L1_gnn_bias_gat, L1_gnn_w1, L1_gnn_b1, L1_gnn_w2, L1_gnn_b2, L1_gnn_g1, L1_gnn_be1,
           L1_gnn_g2, L1_gnn_be2):
    import ml_dtypes
    import concourse.bacc as bacc
    from concourse.bass_utils import run_bass_kernel_spmd

    arr = np.asarray
    bf = ml_dtypes.bfloat16
    pads = EP - E

    def edge_rows(v, fill, n=pads):
        return np.concatenate([arr(v), np.full((n,) + arr(v).shape[1:], fill, arr(v).dtype)])

    d = np.concatenate([np.array([4000], np.int32), edge_rows(dst, NP - 1), np.array([5000], np.int32)]).astype(np.int32, copy=False)
    dst_ext = np.stack([d[p * J:p * J + J + 2] for p in range(P)])
    emb = edge_rows(edge_attr_10, 0).reshape(P, J, 10)
    w2 = arr(L0_gnn_W2).reshape(K, 7, 2 * U, U)[:, [0, 2, 4, 1, 3, 6, 5]]
    eye = np.eye(P, dtype=np.float32)
    rep_sel = np.zeros((3, C, 4, U, K), bf)
    for part in range(3):
        for u in range(U):
            rep_sel[part, u, 0, u] = 1
            for k in range(3):
                rep_sel[part, U + 3 * u + k, k + 1, u] = 1
    feeds = {
        "x": np.concatenate([arr(x), np.zeros((NP - N, C), np.float32)]),
        "src": edge_rows(src, 0).reshape(P, J),
        "dst_ext": dst_ext,
        "dst_ends": np.ascontiguousarray(dst_ext[:, [1, J, 0, J + 1]].T),
        "emb": np.ascontiguousarray(emb.transpose(2, 1, 0)).reshape(P, EMB * J),
        "vec": np.ascontiguousarray(edge_rows(edge_attr_3, 1).reshape(P, J, 3).transpose(0, 2, 1)),
        "weight": edge_rows(edge_weight, 0).reshape(P, J),
        "w1rep": np.tile(arr(L0_gnn_W1), (6, U)),
        "w2r": np.ascontiguousarray(w2.transpose(2, 0, 1, 3).reshape(2, P, 56).transpose(1, 0, 2)),
        "rep_sel": rep_sel.reshape(S3, 4, P),
        "ident": eye, "identb": eye.astype(bf), "tri": np.triu(np.ones((P, P), np.float32)),
        "iota_b": np.tile(np.arange(P), (P, 1)).astype(bf),
        "which": np.repeat(np.eye(3, dtype=np.float32)[[0, 0, 0, 1, 1, 2]], EMB, axis=0),
        "w_gat": np.tile(arr(L1_gnn_W_gat), (4, 1)),
        "meets": np.repeat(np.array([[1, 1, 0], [1, 1, 0], [1, 0, 0], [0, 0, 1]], np.float32), C, axis=0),
        "att": np.stack([arr(L1_gnn_att_src).reshape(-1), arr(L1_gnn_att_dst).reshape(-1)]),
        "ffn1": arr(L1_gnn_w1), "ffn2": arr(L1_gnn_w2),
        "rows": np.stack([arr(v) for v in (L1_gnn_bias_gat, L1_gnn_b2, L1_gnn_g1, L1_gnn_be1, L1_gnn_g2, L1_gnn_be2)]),
        "b1": arr(L1_gnn_b1).reshape(P, 1),
    }
    feeds = {k: np.ascontiguousarray(v) for k, v in feeds.items()}
    nc = bacc.Bacc("TRN2", target_bir_lowering=False, num_devices=1)
    args = [nc.dram_tensor(k, v.shape, mybir.dt.from_np(v.dtype), kind="ExternalInput").ap() for k, v in feeds.items()]
    out = nc.dram_tensor("out", (N, C), F32, kind="ExternalOutput").ap()
    tensor_network(nc, *args, out)
    return run_bass_kernel_spmd(nc, [feeds], core_ids=[0]).results[0]["out"]
```
